# Optimizing a Trainium2 kernel written in Bass

```python
import numpy as np
import jax
import jax.numpy as jnp

def _softmax(x, axis=-1):
    return jax.nn.softmax(x, axis=axis)

def _gelu(x):
    return jax.nn.gelu(x, approximate=True)

def _silu(x):
    return jax.nn.silu(x)

def _sigmoid(x):
    return jax.nn.sigmoid(x)

def _layernorm(x, axis=-1, eps=1e-05):
    m = jnp.mean(x, axis=axis, keepdims=True)
    v = jnp.var(x, axis=axis, keepdims=True)
    return (x - m) / jnp.sqrt(v + eps)

def _scatter_add(tgt, idx, src, axis=0):
    return tgt.at[idx].add(src)

def _segment_sum(src, seg, n):
    return jax.ops.segment_sum(src, seg, n)
kernel_name = 'mk_cond_seq_d2_seqx_r2_ce791e'

def setup_inputs(seed: int=0):
    np.random.seed(seed)
    _w = jnp.asarray

    def _rec_inputs():
        import jax
        import jax.numpy as jnp
        _rk = jax.random.key(seed)
        x = -0.0002928 + 1 * jax.random.normal(jax.random.fold_in(_rk, 1), (32, 128, 512), jnp.float32)
        _lenS = 128 - jax.random.randint(jax.random.fold_in(_rk, 7), (32,), 0, max(1, 128 // 4) + 1, jnp.int32)
        _lenS2 = 128 - jax.random.randint(jax.random.fold_in(_rk, 8), (32,), 0, max(1, 128 // 4) + 1, jnp.int32)
        cond_1024 = 0.0061147 + 1.02565 * jax.random.normal(jax.random.fold_in(_rk, 11), (32, 512), jnp.float32)
        return (x, cond_1024)
    x, cond_1024 = _rec_inputs()

    def _L0_cond_setup():
        import jax, jax.numpy as jnp
        import numpy as np
        EPS = 1e-05

        def _sln(h, w, ln_g, ln_b, Wg, bg, Wb, bb):
            mu = jnp.mean(h, axis=-1, keepdims=True)
            var = jnp.mean((h - mu) ** 2, axis=-1, keepdims=True)
            ln = (h - mu) / jnp.sqrt(var + EPS) * ln_g + ln_b
            gamma = (w @ Wg.T + bg)[:, None, :]
            beta = (w @ Wb.T + bb)[:, None, :]
            return gamma * ln + beta
        key = jax.random.key(seed)
        ks = jax.random.split(key, 20)
        B, N, D = (4, 512, 512)
        F = 4 * D
        s = lambda fan: 1.0 / np.sqrt(fan)
        inp = {'hidden': jax.random.normal(ks[0], (B, N, D), jnp.float32), 'w': jax.random.normal(ks[1], (B, D), jnp.float32), 'ln_g': jnp.ones((D,), jnp.float32), 'ln_b': jnp.zeros((D,), jnp.float32), 'Wg': jax.random.normal(ks[2], (D, D), jnp.float32) * s(D), 'bg': jnp.zeros((D,), jnp.float32), 'Wb': jax.random.normal(ks[3], (D, D), jnp.float32) * s(D), 'bb': jnp.zeros((D,), jnp.float32), 'Wqkv': jax.random.normal(ks[4], (3 * D, D), jnp.float32) * s(D), 'bqkv': jnp.zeros((3 * D,), jnp.float32), 'Wp': jax.random.normal(ks[5], (D, D), jnp.float32) * s(D), 'bp': jnp.zeros((D,), jnp.float32), 'W1': jax.random.normal(ks[6], (F, D), jnp.float32) * s(D), 'b1': jnp.zeros((F,), jnp.float32), 'W2': jax.random.normal(ks[7], (D, F), jnp.float32) * s(F), 'b2': jnp.zeros((D,), jnp.float32), 'num_heads': 16}
        return inp
    _L0_cond_all = _L0_cond_setup()
    _L0_cond_in = {k: v for k, v in _L0_cond_all.items() if k in ('ln_g', 'ln_b', 'Wg', 'bg', 'Wb', 'bb', 'Wqkv', 'bqkv', 'Wp', 'bp', 'W1', 'b1', 'W2', 'b2')}
    del _L0_cond_all

    def _L1_cond_setup():
        import jax, jax.numpy as jnp
        import numpy as np
        DIM = 512
        MLP_RATIO = 4
        EPS = 1e-06

        def rmsnorm(x, w):
            return x * jax.lax.rsqrt(jnp.mean(x * x, axis=-1, keepdims=True) + EPS) * w

        def film(x, cond, w, b):
            ss = cond @ w + b
            scale, shift = jnp.split(ss, 2, axis=-1)
            return x * (1.0 + scale[:, None, :]) + shift[:, None, :]
        key = jax.random.key(seed)
        ks = jax.random.split(key, 16)
        B, N, D = (4, 1024, DIM)
        H = D * MLP_RATIO
        s = lambda fan_in: 1.0 / np.sqrt(fan_in)
        return {'x': jax.random.normal(ks[0], (B, N, D), jnp.float32), 'cond': jax.random.normal(ks[1], (B, D), jnp.float32), 'norm1_w': jnp.ones((D,), jnp.float32), 'film1_w': jax.random.normal(ks[2], (D, 2 * D), jnp.float32) * s(D), 'film1_b': jnp.zeros((2 * D,), jnp.float32), 'q_w': jax.random.normal(ks[3], (D, D), jnp.float32) * s(D), 'q_b': jnp.zeros((D,), jnp.float32), 'k_w': jax.random.normal(ks[4], (D, D), jnp.float32) * s(D), 'k_b': jnp.zeros((D,), jnp.float32), 'v_w': jax.random.normal(ks[5], (D, D), jnp.float32) * s(D), 'v_b': jnp.zeros((D,), jnp.float32), 'proj_w': jax.random.normal(ks[6], (D, D), jnp.float32) * s(D), 'proj_b': jnp.zeros((D,), jnp.float32), 'norm2_w': jnp.ones((D,), jnp.float32), 'film2_w': jax.random.normal(ks[7], (D, 2 * D), jnp.float32) * s(D), 'film2_b': jnp.zeros((2 * D,), jnp.float32), 'mlp_w1': jax.random.normal(ks[8], (D, H), jnp.float32) * s(D), 'mlp_b1': jnp.zeros((H,), jnp.float32), 'mlp_w2': jax.random.normal(ks[9], (H, D), jnp.float32) * s(H), 'mlp_b2': jnp.zeros((D,), jnp.float32)}
    _L1_cond_all = _L1_cond_setup()
    _L1_cond_in = {k: v for k, v in _L1_cond_all.items() if k in ('norm1_w', 'film1_w', 'film1_b', 'q_w', 'q_b', 'k_w', 'k_b', 'v_w', 'v_b', 'proj_w', 'proj_b', 'norm2_w', 'film2_w', 'film2_b', 'mlp_w1', 'mlp_b1', 'mlp_w2', 'mlp_b2')}
    del _L1_cond_all
    return {'x': x, 'cond_1024': cond_1024, 'L0_cond_ln_g': _L0_cond_in['ln_g'], 'L0_cond_ln_b': _L0_cond_in['ln_b'], 'L0_cond_Wg': _L0_cond_in['Wg'], 'L0_cond_bg': _L0_cond_in['bg'], 'L0_cond_Wb': _L0_cond_in['Wb'], 'L0_cond_bb': _L0_cond_in['bb'], 'L0_cond_Wqkv': _L0_cond_in['Wqkv'], 'L0_cond_bqkv': _L0_cond_in['bqkv'], 'L0_cond_Wp': _L0_cond_in['Wp'], 'L0_cond_bp': _L0_cond_in['bp'], 'L0_cond_W1': _L0_cond_in['W1'], 'L0_cond_b1': _L0_cond_in['b1'], 'L0_cond_W2': _L0_cond_in['W2'], 'L0_cond_b2': _L0_cond_in['b2'], 'L1_cond_norm1_w': _L1_cond_in['norm1_w'], 'L1_cond_film1_w': _L1_cond_in['film1_w'], 'L1_cond_film1_b': _L1_cond_in['film1_b'], 'L1_cond_q_w': _L1_cond_in['q_w'], 'L1_cond_q_b': _L1_cond_in['q_b'], 'L1_cond_k_w': _L1_cond_in['k_w'], 'L1_cond_k_b': _L1_cond_in['k_b'], 'L1_cond_v_w': _L1_cond_in['v_w'], 'L1_cond_v_b': _L1_cond_in['v_b'], 'L1_cond_proj_w': _L1_cond_in['proj_w'], 'L1_cond_proj_b': _L1_cond_in['proj_b'], 'L1_cond_norm2_w': _L1_cond_in['norm2_w'], 'L1_cond_film2_w': _L1_cond_in['film2_w'], 'L1_cond_film2_b': _L1_cond_in['film2_b'], 'L1_cond_mlp_w1': _L1_cond_in['mlp_w1'], 'L1_cond_mlp_b1': _L1_cond_in['mlp_b1'], 'L1_cond_mlp_w2': _L1_cond_in['mlp_w2'], 'L1_cond_mlp_b2': _L1_cond_in['mlp_b2']}

def reference(x, cond_1024, L0_cond_ln_g, L0_cond_ln_b, L0_cond_Wg, L0_cond_bg, L0_cond_Wb, L0_cond_bb, L0_cond_Wqkv, L0_cond_bqkv, L0_cond_Wp, L0_cond_bp, L0_cond_W1, L0_cond_b1, L0_cond_W2, L0_cond_b2, L1_cond_norm1_w, L1_cond_film1_w, L1_cond_film1_b, L1_cond_q_w, L1_cond_q_b, L1_cond_k_w, L1_cond_k_b, L1_cond_v_w, L1_cond_v_b, L1_cond_proj_w, L1_cond_proj_b, L1_cond_norm2_w, L1_cond_film2_w, L1_cond_film2_b, L1_cond_mlp_w1, L1_cond_mlp_b1, L1_cond_mlp_w2, L1_cond_mlp_b2):
    import jax
    import jax.numpy as jnp

    def _L0_cond_ref(hidden, w, ln_g, ln_b, Wg, bg, Wb, bb, Wqkv, bqkv, Wp, bp, W1, b1, W2, b2, num_heads):
        import jax, jax.numpy as jnp
        import numpy as np
        EPS = 1e-05

        def _sln(h, w, ln_g, ln_b, Wg, bg, Wb, bb):
            mu = jnp.mean(h, axis=-1, keepdims=True)
            var = jnp.mean((h - mu) ** 2, axis=-1, keepdims=True)
            ln = (h - mu) / jnp.sqrt(var + EPS) * ln_g + ln_b
            gamma = (w @ Wg.T + bg)[:, None, :]
            beta = (w @ Wb.T + bb)[:, None, :]
            return gamma * ln + beta
        B, N, D = hidden.shape
        hd = D // num_heads
        h = _sln(hidden, w, ln_g, ln_b, Wg, bg, Wb, bb)
        qkv = (h @ Wqkv.T + bqkv).reshape(B, N, num_heads, hd, 3)
        q = jnp.moveaxis(qkv[..., 0], 2, 1)
        k = jnp.moveaxis(qkv[..., 1], 2, 1)
        v = jnp.moveaxis(qkv[..., 2], 2, 1)
        energy = jnp.einsum('bhqd,bhkd->bhqk', q, k)
        att = jax.nn.softmax(energy, axis=-1) / D ** 0.5
        out = jnp.einsum('bhqk,bhkd->bhqd', att, v)
        out = jnp.moveaxis(out, 1, 2).reshape(B, N, D)
        out = out @ Wp.T + bp
        h1 = out + hidden
        h2 = _sln(h1, w, ln_g, ln_b, Wg, bg, Wb, bb)
        return h2 + h1

    def _L1_cond_ref(x, cond, norm1_w, film1_w, film1_b, q_w, q_b, k_w, k_b, v_w, v_b, proj_w, proj_b, norm2_w, film2_w, film2_b, mlp_w1, mlp_b1, mlp_w2, mlp_b2):
        import jax, jax.numpy as jnp
        import numpy as np
        DIM = 512
        MLP_RATIO = 4
        EPS = 1e-06

        def rmsnorm(x, w):
            return x * jax.lax.rsqrt(jnp.mean(x * x, axis=-1, keepdims=True) + EPS) * w

        def film(x, cond, w, b):
            ss = cond @ w + b
            scale, shift = jnp.split(ss, 2, axis=-1)
            return x * (1.0 + scale[:, None, :]) + shift[:, None, :]
        B, N, D = x.shape
        x_in = x
        h = film(rmsnorm(x, norm1_w), cond, film1_w, film1_b)
        Q = h @ q_w + q_b
        K = h @ k_w + k_b
        V = h @ v_w + v_b
        scores = jnp.einsum('bnd,bmd->bnm', Q, K) * D ** (-0.5)
        attn = jax.nn.softmax(scores, axis=-1)
        out = jnp.einsum('bnm,bmd->bnd', attn, V)
        x = x_in + (out @ proj_w + proj_b)
        x_in = x
        h = film(rmsnorm(x, norm2_w), cond, film2_w, film2_b)
        h = jax.nn.gelu(h @ mlp_w1 + mlp_b1, approximate=False) @ mlp_w2 + mlp_b2
        return x_in + h
    x = _L0_cond_ref(x, cond_1024, L0_cond_ln_g, L0_cond_ln_b, L0_cond_Wg, L0_cond_bg, L0_cond_Wb, L0_cond_bb, L0_cond_Wqkv, L0_cond_bqkv, L0_cond_Wp, L0_cond_bp, L0_cond_W1, L0_cond_b1, L0_cond_W2, L0_cond_b2, 16)
    x = _L1_cond_ref(x, cond_1024, L1_cond_norm1_w, L1_cond_film1_w, L1_cond_film1_b, L1_cond_q_w, L1_cond_q_b, L1_cond_k_w, L1_cond_k_b, L1_cond_v_w, L1_cond_v_b, L1_cond_proj_w, L1_cond_proj_b, L1_cond_norm2_w, L1_cond_film2_w, L1_cond_film2_b, L1_cond_mlp_w1, L1_cond_mlp_b1, L1_cond_mlp_w2, L1_cond_mlp_b2)
    return x

_drawn_inputs = setup_inputs


def setup_inputs(seed=0):
    import zlib

    import numpy as np

    out = dict(_drawn_inputs(seed))
    spreads = {'L0_cond_ln_g': (1.0, 0.2),
     'L0_cond_ln_b': (0.0, 0.1),
     'L0_cond_bg': (0.0, 0.1),
     'L0_cond_bb': (0.0, 0.1),
     'L0_cond_bqkv': (0.0, 0.8),
     'L0_cond_bp': (0.0, 0.1),
     'L0_cond_b1': (0.0, 0.1),
     'L0_cond_b2': (0.0, 0.1),
     'L1_cond_norm1_w': (1.0, 0.2),
     'L1_cond_film1_b': (0.0, 0.1),
     'L1_cond_q_b': (0.0, 0.429),
     'L1_cond_k_b': (0.0, 0.8),
     'L1_cond_v_b': (0.0, 0.1),
     'L1_cond_proj_b': (0.0, 0.1),
     'L1_cond_norm2_w': (1.0, 0.2),
     'L1_cond_film2_b': (0.0, 0.1),
     'L1_cond_mlp_b1': (0.0, 0.288),
     'L1_cond_mlp_b2': (0.0, 0.1)}
    factors = {}
    for name, (base, spread) in spreads.items():
        noise = np.random.default_rng([zlib.crc32(name.encode()), seed]).standard_normal(out[name].shape)
        drawn = base * np.exp(spread * noise) if base else spread * noise
        out[name] = jnp.asarray(drawn.astype(out[name].dtype))
    for name, factor in factors.items():
        out[name] = (out[name] * factor).astype(out[name].dtype)
    return out
```

```python
import concourse.bass as bass
from concourse import mybir
from contextlib import ExitStack

F32 = mybir.dt.float32
F32R = mybir.dt.float32r
BF16 = mybir.dt.bfloat16
ALU = mybir.AluOpType
ACT = mybir.ActivationFunctionType
AX = mybir.AxisListType

P = 128
D = 512
C = D // P
NB = 32
GB = 4
GT = GB * P
NG = NB // GB
HEADS = 16
HD = D // HEADS
HM = P // HD
UNITS = GB * C
FF = 4 * D
FT = FF // P
LAG = 3
EPS_LN, EPS_RMS = 1e-5, 1e-6
INV_SQRT_D = float(D) ** -0.5

COLS = ["ln_g", "ln_b", "bg", "bb", "bq0", "bk0", "norm1", "f1scale", "f1shift", "bq1", "bk1", "bv1",
        "norm2", "f2scale", "f2shift"]
COL = {n: i * C for i, n in enumerate(COLS)}
B1_COL = len(COLS) * C
N_COLS = B1_COL + FT


def wait(engine, sem, value):
    if isinstance(value, int) and value <= 0:
        return
    engine.wait_ge(sem, value)


def wait_apart(engine, sem, value, passed):
    wait(engine, sem, value)
    if not isinstance(value, int):
        engine.sem_inc(passed, 1)


def bank_uses(g, pos):
    return 8 * g + 2 + pos // 2


def groups(engine, body):
    body(0, True, False)
    with engine.Fori(1, NG - 1) as g:
        body(g, False, False)
    body(NG - 1, False, True)


def block_pair_kernel(nc, xt, cond_t, cols_d, bp0_d, bv0_d, pb1_d, b2_d, wg_t, wb_t, wqkv, wp0,
                      film1, film2, wq1, wk1, wv1_t, wp1, w1, w2, out):
    with ExitStack() as ctx:
        base = 16512
        kib = 1024

        def at(name, shape, dt, offset):
            return nc.alloc_sbuf_tensor_at(name, shape, dt, offset=base + offset)

        class Run:

            def __init__(self, offset):
                self.offset = offset

            def __call__(self, name, shape, dt=F32):
                n = 1
                for s in shape[1:]:
                    n *= s
                t = at(name, shape, dt, self.offset)
                self.offset += -(-n * (2 if dt == BF16 else 4) // 32) * 32
                return t

        keep = Run(0)
        ident = keep("ident", [P, P])
        cols = keep("cols", [P, N_COLS])
        cond = keep("cond", [P, C, NB])
        st_at = keep.offset
        st_ln = keep("st_ln", [P, NB, 2 * C])
        st_f1 = keep("st_f1", [P, NB, 2 * C])
        st_f2 = keep("st_f2", [P, NB, 2 * C])
        st_flat = keep("st_flat", [P, 2 * C, NB])
        tmp_a = keep("tmp_a", [P, C, NB])
        tmp_b = keep("tmp_b", [P, C, NB])
        cur_st = keep("cur_st", [P, GB, 2 * C])
        neg_half = keep("neg_half", [P, GB])
        stats = keep("stats", [P, 6])
        mv1 = keep("mv1", [P, 2, 2])
        ve1 = keep("ve1", [P, 2])
        rstd1 = keep("rstd1", [P, 2])
        stats2 = keep("stats2", [P, GB, 6])
        mv2 = keep("mv2", [P, GB, 2])
        ve2 = keep("ve2", [P, GB])
        rstd2 = keep("rstd2", [P, GB])
        neg_max = keep("neg_max", [P, 2, HM])
        sums = keep("sums", [P, 2, HEADS])
        rec = keep("rec", [P, HEADS])
        ssq = keep("ssq", [P, 2])
        ssq_rec = keep("ssq_rec", [P, 2])
        junk = keep("junk", [P, D], BF16)
        rows_at = keep.offset
        bp0 = keep("bp0", [P, D])
        bv0 = keep("bv0", [P, D])
        cb1 = keep("cb1", [P, D])
        b2 = keep("b2", [P, D])
        R0 = -(-keep.offset // 64) * 64

        run = Run(R0)
        wa_hi = run("wa_hi", [P, C, 3 * D], F32R)
        wa_lo = run("wa_lo", [P, C, 3 * D], F32R)
        wp_hi = run("wp_hi", [P, C, D], F32R)
        wp_lo = run("wp_lo", [P, C, D], F32R)
        k_diag = run("k_diag", [P, C, GB, HM, P])
        h_hi = run("h_hi", [P, C, GT], F32R)
        h_lo = run("h_lo", [P, C, GT], F32R)
        work_at = run.offset
        xa = run("xa", [P, GB, D])
        hf = run("hf", [P, C, P])
        qa = run("qa", [P, C, GT])
        va = run("va", [P, GB, D])
        pa_at = run.offset
        pa = run("pa", [P, 2, HM, P])
        pta = run("pta", [P, 2, HM, P])
        recx = run("recx", [P, HEADS, HD])
        rs = run("rs", [P, D])
        of = run("of", [P, C, P])
        o_hi = run("o_hi", [P, 2, C, P], F32R)
        o_lo = run("o_lo", [P, 2, C, P], F32R)
        xra = run("xra", [P, 2, D])
        stage_at = run.offset
        h1 = run("h1", [P, GB, D])
        rows = run("rows", [P, 2, 2 * D])
        nb = run("nb", [P, 2, D])
        assert base + run.offset <= 229344
        stage_a = at("stage_a", [P, 2, C, D], F32, stage_at)
        wgb = at("wgb", [P, 2, C, D], F32, R0 + 96 * kib)
        fv0 = at("fv0", [2 * NB, D], F32, pa_at)
        st_rows = at("st_rows", [NB, 2 * D], F32, pa_at + 4 * kib)

        raw_b = at("raw_b", [P, 4, C, D], F32, R0)
        film_b = at("film_b", [P, 2, C, 2 * D], F32, R0 + 32 * kib)
        run = Run(R0 + 64 * kib)
        wqk_hi = run("wqk_hi", [P, 2, C, D], F32R)
        wqk_lo = run("wqk_lo", [P, 2, C, D], F32R)
        wvp_hi = run("wvp_hi", [P, C, D], F32R)
        wvp_lo = run("wvp_lo", [P, C, D], F32R)
        assert run.offset == work_at
        hb_hi = run("hb_hi", [P, C, GT], F32R)
        hb_lo = run("hb_lo", [P, C, GT], F32R)
        xb = run("xb", [P, 2, D])
        xnb = run("xnb", [P, 2, D])
        hfb = run("hfb", [P, C, P])
        qb = run("qb", [P, C, GT])
        kb = run("kb", [P, C, GT])
        vb = run("vb", [P, GB, D])
        pb = run("pb", [P, 2, P])
        ptb = run("ptb", [P, 2, P])
        xrb = run("xrb", [P, GB, D])
        stage_w1 = run("stage_w1", [P, 2, FF])
        fv1 = run("fv1", [P, D])
        assert base + run.offset <= 229344

        run = Run(R0)
        w1_hi = run("w1_hi", [P, C, FF], F32R)
        w1_lo = run("w1_lo", [P, C, FF], F32R)
        w2_hi = run("w2_hi", [P, FT, D], F32R)
        w2_lo = run("w2_lo", [P, FT, D], F32R)
        hc_hi = run("hc_hi", [P, C, GT], F32R)
        hc_lo = run("hc_lo", [P, C, GT], F32R)
        xc = run("xc", [P, 2, D])
        xnc = run("xnc", [P, GB, D])
        hfc_act = run("hfc_act", [P, C, P])
        g_hi = run("g_hi", [P, LAG + 1, GT], F32R)
        g_lo = run("g_lo", [P, LAG + 1, GT], F32R)
        xrc = run("xrc", [P, GB, D])
        stage_w2 = run("stage_w2", [P, 2, 2, D])
        assert base + run.offset <= 229344
        run = Run(rows_at)
        hfc_dve = run("hfc_dve", [P, C, P])
        gf1 = run("gf1", [P, GT])
        gf0 = at("gf0", [P, GT], F32, st_at)
        gf = [gf0, gf1]

        bank = [ctx.enter_context(nc.psum_tensor(f"bank{i}", [P, D], F32)) for i in range(8)]
        ps_g = bank[0:2]
        ps_s = bank[2:4]
        ps_t = bank[4:6]
        ps_o = bank[6]
        ps_r = bank[7]

        st_dram = nc.dram_tensor("st_dram", (NB, 2 * D), F32).ap()
        x1_dram = nc.dram_tensor("x1_dram", (NB * P, D), F32).ap()
        x2_dram = nc.dram_tensor("x2_dram", (NB * P, D), F32).ap()

        def sem(name):
            return ctx.enter_context(nc.semaphore(name))

        consts_in, rows_in, wgb_in = sem("consts_in"), sem("rows_in"), sem("wgb_in")
        consts_made, k_zeroed = sem("consts_made"), sem("k_zeroed")
        bn_done, bn2_done, rstd_ready, rstd2_ready = sem("bn_done"), sem("bn2_done"), sem("rstd_ready"), sem("rstd2_ready")
        ln2_normed, braw, brstd, crstd = sem("ln2_normed"), sem("braw"), sem("brstd"), sem("crstd")
        film0_done, film0_copied, film0_t = sem("film0_done"), sem("film0_copied"), sem("film0_t")
        st0_made, st0_t, st_rows_made = sem("st0_made"), sem("st0_t"), sem("st_rows_made")
        st_stored = sem("st_stored")
        stage_in = [sem("stage_in0"), sem("stage_in1")]
        wa_hi_made, wa_lo_made = sem("wa_hi_made"), sem("wa_lo_made")
        dve_step, dve_passed, pool_passed = sem("dve_step"), sem("dve_passed"), sem("pool_passed")
        x_in = [sem(f"x_in{b}") for b in range(GB)]
        xr_in = [sem("xr_in0"), sem("xr_in1")]
        rows_ld = [sem("rows_ld0"), sem("rows_ld1")]
        x1_out = [sem(f"x1_out{b}") for b in range(GB)]
        var_ready, xn_ready, cur_ready = sem("var_ready"), sem("xn_ready"), sem("cur_ready")
        hi_ready, lo_ready = sem("hi_ready"), sem("lo_ready")
        g_full = [sem("g_full0"), sem("g_full1")]
        g_free = [sem("g_free0"), sem("g_free1")]
        s_done, max_done, exp_done = sem("s_done"), sem("max_done"), sem("exp_done")
        tp_done, pt_copied, pv_done = sem("tp_done"), sem("pt_copied"), sem("pv_done")
        rec_made, rec_ready, r_done, r_copied = sem("rec_made"), sem("rec_ready"), sem("r_done"), sem("r_copied")
        o_scaled, o_hi_ready, o_lo_ready = sem("o_scaled"), sem("o_hi_ready"), sem("o_lo_ready")
        proj_done, xr_ready, h1_ready = sem("proj_done"), sem("xr_ready"), sem("h1_ready")
        var2_ready, ln2_scaled, x1_ready = sem("var2_ready"), sem("ln2_scaled"), sem("x1_ready")
        raw_in = [sem(f"raw_in{i}") for i in range(4)]
        film_in = [sem("film_in0"), sem("film_in1")]
        wqk_hi_made, wqk_lo_made = sem("wqk_hi_made"), sem("wqk_lo_made")
        wvp_done, wvp_hi_made, wvp_lo_made = sem("wvp_done"), sem("wvp_hi_made"), sem("wvp_lo_made")
        bvp_done, film1_done, film1_copied = sem("bvp_done"), sem("film1_done"), sem("film1_copied")
        film1_t, st1_made, cb_made = sem("film1_t"), sem("st1_made"), sem("cb_made")
        bx_in = [sem("bx_in0"), sem("bx_in1")]
        bxr_in = [sem(f"bxr_in{b}") for b in range(GB)]
        x2_out = [sem(f"x2_out{b}") for b in range(GB)]
        bssq, bvar, bxn, bcur = sem("bssq"), sem("bvar"), sem("bxn"), sem("bcur")
        bhi, blo = sem("bhi"), sem("blo")
        bg_full = [sem("bg_full0"), sem("bg_full1")]
        bg_free = [sem("bg_free0"), sem("bg_free1")]
        bs_done, bmax, bexp, btp, bpt = sem("bs_done"), sem("bmax"), sem("bexp"), sem("btp"), sem("bpt")
        bpv, brec, bxr, x2_ready = sem("bpv"), sem("brec"), sem("bxr"), sem("x2_ready")
        w1_in = [sem("w1_in0"), sem("w1_in1")]
        w1_hi_made, w1_lo_made = sem("w1_hi_made"), sem("w1_lo_made")
        w2_in = [sem("w2_in0"), sem("w2_in1")]
        w2_hi_made, w2_lo_made = sem("w2_hi_made"), sem("w2_lo_made")
        cx_in = [sem("cx_in0"), sem("cx_in1")]
        cxr_in = [sem(f"cxr_in{b}") for b in range(GB)]
        y_out = [sem(f"y_out{b}") for b in range(GB)]
        cssq, cvar, cxn, ccur = sem("cssq"), sem("cvar"), sem("cxn"), sem("ccur")
        ct_full, ct_free_act, ct_free_dve = sem("ct_full"), sem("ct_free_act"), sem("ct_free_dve")
        chi_act, chi_dve, clo = sem("chi_act"), sem("chi_dve"), sem("clo")
        up_done, gelu_done = sem("up_done"), sem("gelu_done")
        g_hi_ready, g_lo_ready, down_done = sem("g_hi_ready"), sem("g_lo_ready"), sem("down_done")
        acc_done, cxr, y_ready = sem("acc_done"), sem("cxr"), sem("y_ready")

        block = ctx.enter_context(nc.Block())

        def tokens(dram, t):
            return dram[bass.ts(t, P), :]

        def weight(dram):
            return dram.rearrange("(k p) n -> p k n", p=P)

        def col(name, c):
            return cols[:, COL[name] + c:COL[name] + c + 1]

        def col_wide(name):
            return cols[:, COL[name]:COL[name] + C].unsqueeze(2).broadcast_to([P, C, NB])

        def loaded(n):
            return 16 * n

        @block.sync
        def _(sp):
            sp.dma_start(cols[:], cols_d).then_inc(consts_in, 16)
            sp.dma_start(cond[:], cond_t.rearrange("(k p) b -> p k b", p=P)).then_inc(consts_in, 16)
            sp.dma_start(wgb[:, 0], weight(wg_t)).then_inc(wgb_in, 16)
            sp.dma_start(wgb[:, 1], weight(wb_t)).then_inc(wgb_in, 16)
            for t in range(GB):
                sp.dma_start(xa[:, t], tokens(xt, t)).then_inc(x_in[t], 16)
            units = [wqkv[:, D:2 * D], wqkv[:, 0:D], wqkv[:, 2 * D:3 * D], wp0]
            for i in range(2):
                sp.dma_start(stage_a[:, i], weight(units[i])).then_inc(stage_in[i], 16)
            for row, src in ((bp0, bp0_d), (bv0, bv0_d), (cb1, pb1_d), (b2, b2_d)):
                sp.dma_start(row[:], src.partition_broadcast(P)).then_inc(rows_in, 16)
            for i in range(2, 4):
                sp.wait_ge(wa_lo_made, i - 1)
                sp.dma_start(stage_a[:, i % 2], weight(units[i])).then_inc(stage_in[i % 2], 16)
            sp.wait_ge(st_rows_made, 2)
            sp.dma_start(st_dram[:], st_rows[:]).then_inc(st_stored, 16)
            sp.wait_ge(st_stored, 16)

            def load_x(g, b):
                wait(sp, hi_ready, GB * (g - 1) + b + 1)
                sp.dma_start(xa[:, b], tokens(xt, GB * g + b)).then_inc(x_in[b], 16)

            def load_xr(g, b):
                wait(sp, h1_ready, GB * g + b - 1)
                sp.dma_start(xra[:, b % 2], tokens(xt, GB * g + b)).then_inc(xr_in[b % 2], 16)

            def load_rows(g, b):
                wait(sp, ln2_scaled, GB * g + max(b - 1, 0))
                sp.dma_start(rows[:, b % 2], st_dram[bass.ds(GB * g + b, 1), :].partition_broadcast(P))\
                    .then_inc(rows_ld[b % 2], 16)

            def store_x1(g, b):
                sp.wait_ge(x1_ready, GB * g + b + 1)
                sp.dma_start(tokens(x1_dram, GB * g + b), h1[:, b]).then_inc(x1_out[b], 16)

            def finish(g):
                load_rows(g, 0)
                load_rows(g, 1)
                store_x1(g, 0)
                load_rows(g, 2)
                store_x1(g, 1)
                load_rows(g, 3)
                store_x1(g, 2)
                store_x1(g, 3)

            def body(g, first, last):
                if not last:
                    for b in range(GB):
                        load_x(g + 1, b)
                load_xr(g, 0)
                load_xr(g, 1)
                if not first:
                    finish(g - 1)
                load_xr(g, 2)
                load_xr(g, 3)

            groups(sp, body)

            sp.wait_ge(g_free[1], bank_uses(NG - 1, 13) + 1)
            for i, w in enumerate((wv1_t, wp1, wq1, wk1)):
                sp.dma_start(raw_b[:, i], weight(w)).then_inc(raw_in[i], 16)
            sp.dma_start(film_b[:, 0], weight(film1)).then_inc(film_in[0], 16)
            sp.wait_ge(h1_ready, NB)
            sp.dma_start(film_b[:, 1], weight(film2)).then_inc(film_in[1], 16)
            finish(NG - 1)

            for b in range(GB):
                sp.wait_ge(x1_out[b], 16 * NG)

            def load_bx(g, b):
                wait(sp, bxn, GB * g + b - 1)
                sp.dma_start(xb[:, b % 2], tokens(x1_dram, GB * g + b)).then_inc(bx_in[b % 2], 16)

            def load_bxr(g, b):
                wait(sp, x2_out[b], 16 * g)
                sp.dma_start(xrb[:, b], tokens(x1_dram, GB * g + b)).then_inc(bxr_in[b], 16)

            def store_x2(g, b):
                sp.wait_ge(x2_ready, GB * g + b + 1)
                sp.dma_start(tokens(x2_dram, GB * g + b), xrb[:, b]).then_inc(x2_out[b], 16)

            for b in range(GB):
                load_bx(0, b)

            def body_b(g, first, last):
                if not last:
                    load_bx(g + 1, 0)
                    load_bx(g + 1, 1)
                for b in range(GB):
                    load_bxr(g, b)
                if first:
                    for k in range(2):
                        sp.dma_start(stage_w1[:, k], w1[k * P:(k + 1) * P, :]).then_inc(w1_in[k], 16)
                if not last:
                    load_bx(g + 1, 2)
                store_x2(g, 0)
                if first:
                    sp.wait_ge(w1_lo_made, 1)
                    sp.dma_start(stage_w1[:, 0], w1[2 * P:3 * P, :]).then_inc(w1_in[0], 16)
                if not last:
                    load_bx(g + 1, 3)
                store_x2(g, 1)
                if first:
                    sp.wait_ge(w1_lo_made, 2)
                    sp.dma_start(stage_w1[:, 1], w1[3 * P:4 * P, :]).then_inc(w1_in[1], 16)
                store_x2(g, 2)
                store_x2(g, 3)

            groups(sp, body_b)

            for b in range(GB):
                sp.wait_ge(x2_out[b], 16 * NG)

            def load_cx(g, b):
                wait(sp, cxn, GB * g + b - 1)
                sp.dma_start(xc[:, b % 2], tokens(x2_dram, GB * g + b)).then_inc(cx_in[b % 2], 16)

            def load_cxr(g, b):
                wait(sp, y_out[b], 16 * g)
                sp.dma_start(xrc[:, b], tokens(x2_dram, GB * g + b)).then_inc(cxr_in[b], 16)

            def store_y(g, b):
                sp.wait_ge(y_ready, GB * g + b + 1)
                sp.dma_start(tokens(out, GB * g + b), xrc[:, b]).then_inc(y_out[b], 16)

            def load_w2(i):
                wait(sp, w2_lo_made, i - 1)
                sp.dma_start(stage_w2[:, i % 2], weight(w2[2 * i * P:2 * (i + 1) * P, :]))\
                    .then_inc(w2_in[i % 2], 16)

            for b in range(2):
                load_cx(0, b)
            for i in range(2):
                load_w2(i)
            for b in range(2, GB):
                load_cx(0, b)

            def body_c(g, first, last):
                if not first:
                    for b in range(GB):
                        store_y(g - 1, b)
                for b in range(GB):
                    load_cxr(g, b)
                if not last:
                    for b in range(2):
                        load_cx(g + 1, b)
                if first:
                    for i in range(2, FT // 2):
                        load_w2(i)
                if not last:
                    for b in range(2, GB):
                        load_cx(g + 1, b)

            groups(sp, body_c)
            for b in range(GB):
                store_y(NG - 1, b)
            for b in range(GB):
                sp.wait_ge(y_out[b], 16 * NG)

        @block.tensor
        def _(pe):
            def split_product(dst, w_hi, w_lo, a_hi, a_lo, start, stop):
                nc.tensor.matmul(dst, w_hi, a_hi, start=start, stop=False)
                nc.tensor.matmul(dst, w_hi, a_lo, start=False, stop=False)
                return nc.tensor.matmul(dst, w_lo, a_hi, start=False, stop=stop)

            pe.wait_ge(consts_in, 32)
            pe.wait_ge(wgb_in, 32)
            for k in range(C):
                for i in range(2):
                    last = nc.tensor.matmul(ps_s[0][NB * i:NB * (i + 1), :], cond[:, k, :], wgb[:, i, k, :],
                                            start=(k == 0), stop=(k == C - 1))
            last.then_inc(film0_done, 1)
            pe.wait_ge(consts_made, 3)
            pe.wait_ge(film0_copied, 1)
            for c in range(C):
                last = nc.tensor.transpose(ps_s[1][:, 2 * NB * c:2 * NB * (c + 1)], fv0[:, c * P:(c + 1) * P],
                                           ident[0:2 * NB, 0:2 * NB])
            last.then_inc(film0_t, 1)
            pe.wait_ge(st0_made, 1)
            for i in range(2):
                for c in range(C):
                    last = nc.tensor.transpose(ps_t[i][0:NB, c * P:(c + 1) * P], st_flat[:, i * C + c, :], ident[:])
            last.then_inc(st0_t, 1)

            def norm_t(g, b, pos, banks_full, banks_free, xn, slot, ready):
                i, n = pos % 2, bank_uses(g, pos)
                pe.wait_ge(ready, GB * (g + 1) + b + 1)
                wait(pe, banks_free[i], n)
                for c in range(C):
                    last = nc.tensor.transpose(ps_g[i][:, c * P:(c + 1) * P], xn[:, slot, c * P:(c + 1) * P], ident[:])
                last.then_inc(banks_full[i], 1)

            def norm_a(g, b, pos):
                norm_t(g, b, pos, g_full, g_free, xa, b, xn_ready)

            for b in range(GB):
                norm_a(-1, b, 12 + b)

            def qk(g, m, pos, offset):
                i = pos % 2
                pe.wait_ge(g_free[i], bank_uses(g, pos))
                for k in range(C):
                    n = slice(offset + m * P, offset + (m + 1) * P)
                    last = split_product(ps_g[i][:], wa_hi[:, k, n], wa_lo[:, k, n], h_hi[:, k, :], h_lo[:, k, :],
                                         k == 0, k == C - 1)
                last.then_inc(g_full[i], 1)

            def values(g, b, pos, ks):
                i = pos % 2
                if ks[0] == 0:
                    pe.wait_ge(g_free[i], bank_uses(g, pos))
                t = slice(b * P, (b + 1) * P)
                for k in ks:
                    last = split_product(ps_g[i][:], h_hi[:, k, t], h_lo[:, k, t], wa_hi[:, k, 2 * D:3 * D],
                                         wa_lo[:, k, 2 * D:3 * D], k == 0, k == C - 1)
                if ks[-1] == C - 1:
                    last.then_inc(g_full[i], 1)

            def v_pos(b):
                return 8 if b == 0 else 7 + 2 * b

            def scores(g, u):
                b, m = u // C, u % C
                if b == 0:
                    pe.wait_ge(g_free[0], bank_uses(g, 2 * m) + 1)
                    pe.wait_ge(g_free[1], bank_uses(g, 2 * m + 1) + 1)
                wait(pe, exp_done, UNITS * g + u - 1)
                nc.tensor.matmul(ps_s[u % 2][:], qa[:, m, b * P:(b + 1) * P], k_diag[:, m, b, :, :],
                                 start=True, stop=True).then_inc(s_done, 1)

            def transpose_p(g, u):
                pe.wait_ge(exp_done, UNITS * g + u + 1)
                wait(pe, pt_copied, UNITS * g + u - 1)
                for j in range(HM):
                    last = nc.tensor.transpose(ps_t[u % 2][:, j * P:(j + 1) * P], pa[:, u % 2, j, :], ident[:])
                last.then_inc(tp_done, 1)

            def attend(g, u):
                b, m = u // C, u % C
                pe.wait_ge(pt_copied, UNITS * g + u + 1)
                if m == 0:
                    pe.wait_ge(g_free[v_pos(b) % 2], bank_uses(g, v_pos(b)) + 1)
                    wait(pe, o_scaled, GB * g + b)
                for j in range(HM):
                    f = (m * HM + j) * HD
                    last = nc.tensor.matmul(ps_o[j * HD:(j + 1) * HD, m * P:(m + 1) * P], va[:, b, f:f + HD],
                                            pta[:, u % 2, j, :], start=True, stop=True)
                last.then_inc(pv_done, 1)

            def recip_t(g, b):
                pe.wait_ge(rec_ready, GB * g + b + 1)
                wait(pe, h1_ready, GB * g + b)
                flat = recx[:].rearrange("p h d -> p (h d)")
                for m in range(C):
                    last = nc.tensor.transpose(ps_r[:, m * P:(m + 1) * P], flat[:, m * P:(m + 1) * P], ident[:])
                last.then_inc(r_done, 1)

            def project(g, b, ks):
                if ks[0] == 0:
                    pe.wait_ge(o_hi_ready, GB * g + b + 1)
                    pe.wait_ge(o_lo_ready, GB * g + b + 1)
                    pe.wait_ge(r_copied, GB * g + b + 1)
                for k in ks:
                    last = split_product(ps_r[:], o_hi[:, b % 2, k, :], o_lo[:, b % 2, k, :], wp_hi[:, k, :],
                                         wp_lo[:, k, :], k == 0, k == C - 1)
                if ks[-1] == C - 1:
                    last.then_inc(proj_done, 1)

            def body(g, first, last):
                pe.wait_ge(hi_ready, GB * g + GB)
                pe.wait_ge(lo_ready, GB * g + GB)
                for m in range(C):
                    if first and m == 0:
                        pe.wait_ge(wa_hi_made, 2)
                        pe.wait_ge(wa_lo_made, 2)
                    qk(g, m, 2 * m, D)
                    if m == 0 and not first:
                        recip_t(g - 1, GB - 1)
                    qk(g, m, 2 * m + 1, 0)
                    if m == 1 and not first:
                        project(g - 1, GB - 1, range(C))
                scores(g, 0)
                scores(g, 1)
                if first:
                    pe.wait_ge(wa_hi_made, 3)
                    pe.wait_ge(wa_lo_made, 3)
                values(g, 0, v_pos(0), range(C))
                for u in range(UNITS):
                    b, m = u // C, u % C
                    transpose_p(g, u)
                    if u > 0:
                        attend(g, u - 1)
                    if m == 0 and b > 0:
                        recip_t(g, b - 1)
                    if b < GB - 1:
                        values(g, b + 1, v_pos(b + 1), [m])
                    if m == 1 and not last:
                        norm_a(g, b, [10, 12, 14, 15][b])
                    if b > 0 and m >= 2:
                        if first and b == 1 and m == 2:
                            pe.wait_ge(wa_hi_made, 4)
                            pe.wait_ge(wa_lo_made, 4)
                        project(g, b - 1, [0, 1] if m == 2 else [2, 3])
                    if u + 2 < UNITS:
                        scores(g, u + 2)
                attend(g, UNITS - 1)

            groups(pe, body)
            recip_t(NG - 1, GB - 1)
            project(NG - 1, GB - 1, range(C))

            pe.wait_ge(raw_in[0], 16)
            pe.wait_ge(raw_in[1], 16)
            for i in range(C):
                for k in range(C):
                    last = nc.tensor.matmul(bank[2 + i][:], raw_b[:, 0, k, i * P:(i + 1) * P], raw_b[:, 1, k, :],
                                            start=(k == 0), stop=(k == C - 1))
                last.then_inc(wvp_done, 1)
            pe.wait_ge(g_free[1], bank_uses(NG - 1, 13) + 1)
            for k in range(C):
                last = nc.tensor.matmul(ps_g[1][:], col("bv1", k).broadcast_to([P, P]), raw_b[:, 1, k, :],
                                        start=(k == 0), stop=(k == C - 1))
            last.then_inc(bvp_done, 1)
            pe.wait_ge(film_in[0], 16)
            pe.wait_ge(film_in[1], 16)
            for k in range(C):
                for i in range(4):
                    last = nc.tensor.matmul(ps_g[0][NB * i:NB * (i + 1), :], cond[:, k, :],
                                            film_b[:, i // 2, k, (i % 2) * D:(i % 2 + 1) * D],
                                            start=(k == 0), stop=(k == C - 1))
            last.then_inc(film1_done, 1)
            pe.wait_ge(film1_copied, 1)
            pe.wait_ge(h1_ready, NB)
            for c in range(C):
                last = nc.tensor.transpose(ps_r[:, c * P:(c + 1) * P], fv1[:, c * P:(c + 1) * P], ident[:])
            last.then_inc(film1_t, 1)

            pe.wait_ge(cb_made, 1)

            def norm_b(g, b, pos):
                norm_t(g, b, pos, bg_full, bg_free, xnb, b % 2, bxn)

            for b in range(GB):
                norm_b(-1, b, 12 + b)

            def qk_b(g, m, pos, which):
                i = pos % 2
                pe.wait_ge(bg_free[i], bank_uses(g, pos))
                for k in range(C):
                    n = slice(m * P, (m + 1) * P)
                    last = split_product(ps_g[i][:], wqk_hi[:, which, k, n], wqk_lo[:, which, k, n], hb_hi[:, k, :],
                                         hb_lo[:, k, :], k == 0, k == C - 1)
                last.then_inc(bg_full[i], 1)

            def attend_b(g, b):
                t = GB * g + b
                pe.wait_ge(bpt, t + 1)
                pe.wait_ge(bg_free[0], bank_uses(g, 8 + 2 * b) + 1)
                wait(pe, x2_ready, t - 1)
                nc.tensor.matmul(bank[6 + b % 2][:], ptb[:, b % 2, :], vb[:, b, :], start=True, stop=True)\
                    .then_inc(bpv, 1)

            def body_b(g, first, last):
                pe.wait_ge(bhi, GB * g + GB)
                pe.wait_ge(blo, GB * g + GB)
                if first:
                    pe.wait_ge(wqk_hi_made, 2)
                    pe.wait_ge(wqk_lo_made, 2)
                    pe.wait_ge(st1_made, 1)
                for m in range(C):
                    qk_b(g, m, 2 * m, 1)
                    qk_b(g, m, 2 * m + 1, 0)
                if first:
                    pe.wait_ge(wvp_hi_made, C)
                    pe.wait_ge(wvp_lo_made, C)
                for b in range(GB):
                    t = GB * g + b
                    if b == 0:
                        pe.wait_ge(bg_free[0], bank_uses(g, 6) + 1)
                        pe.wait_ge(bg_free[1], bank_uses(g, 7) + 1)
                    wait(pe, bexp, t - 1)
                    tok = slice(b * P, (b + 1) * P)
                    for k in range(C):
                        s = nc.tensor.matmul(ps_s[b % 2][:, 0:P], qb[:, k, tok], kb[:, k, tok], start=(k == 0),
                                             stop=(k == C - 1))
                    s.then_inc(bs_done, 1)
                    pe.wait_ge(bg_free[0], bank_uses(g, 8 + 2 * b))
                    for k in range(C):
                        v = split_product(ps_g[0][:], hb_hi[:, k, tok], hb_lo[:, k, tok], wvp_hi[:, k, :],
                                          wvp_lo[:, k, :], k == 0, k == C - 1)
                    v.then_inc(bg_full[0], 1)
                    pe.wait_ge(bexp, t + 1)
                    wait(pe, bpt, t - 1)
                    nc.tensor.transpose(ps_t[b % 2][:, 0:P], pb[:, b % 2, :], ident[:]).then_inc(btp, 1)
                    if not last:
                        norm_b(g, b, 9 + 2 * b)
                    if b > 0:
                        attend_b(g, b - 1)
                attend_b(g, GB - 1)

            groups(pe, body_b)

            def norm_c(g, b):
                t = GB * g + b
                pe.wait_ge(cxn, t + 1)
                wait(pe, ct_free_act if b % 2 else ct_free_dve, 2 * g + b // 2)
                for c in range(C):
                    last = nc.tensor.transpose(bank[6 + b % 2][:, c * P:(c + 1) * P], xnc[:, b, c * P:(c + 1) * P],
                                               ident[:])
                last.then_inc(ct_full, 1)

            pe.wait_ge(x2_ready, NB)
            for b in range(GB):
                norm_c(0, b)

            def up(g, f):
                n = FT * g + f
                wait(pe, gelu_done, n - 1)
                for k in range(C):
                    last = split_product(bank[f % 2][:], w1_hi[:, k, f * P:(f + 1) * P], w1_lo[:, k, f * P:(f + 1) * P],
                                         hc_hi[:, k, :], hc_lo[:, k, :], k == 0, k == C - 1)
                last.then_inc(up_done, 1)

            def down(g, f, first):
                n = FT * g + f
                if first and f % 2 == 0:
                    pe.wait_ge(w2_hi_made, f // 2 + 1)
                    pe.wait_ge(w2_lo_made, f // 2 + 1)
                pe.wait_ge(g_hi_ready, n + 1)
                pe.wait_ge(g_lo_ready, n + 1)
                if f == 0:
                    wait(pe, y_ready, GB * g)
                for b in range(GB):
                    tok = slice(b * P, (b + 1) * P)
                    last = split_product(bank[2 + b][:], g_hi[:, f % (LAG + 1), tok], g_lo[:, f % (LAG + 1), tok],
                                         w2_hi[:, f, :], w2_lo[:, f, :], f == 0, f == FT - 1)
                    if f == FT - 1:
                        last.then_inc(acc_done, 1)
                if f < FT - 1:
                    last.then_inc(down_done, 1)

            def body_c(g, first, last):
                pe.wait_ge(clo, GB * g + GB)
                if first:
                    pe.wait_ge(w1_hi_made, C)
                    pe.wait_ge(w1_lo_made, C)
                for f in range(FT):
                    up(g, f)
                    if f >= LAG:
                        down(g, f - LAG, first)
                if not last:
                    for b in range(GB):
                        norm_c(g + 1, b)
                for f in range(FT - LAG, FT):
                    down(g, f, first)

            groups(pe, body_c)

        @block.scalar
        def _(act):
            act.wait_ge(film0_done, 1)
            nc.scalar.activation(fv0[:], ps_s[0][0:2 * NB, :], ACT.Identity).then_inc(film0_copied, 1)
            wa_dst = [wa_hi[:, :, D:2 * D], wa_hi[:, :, 0:D], wa_hi[:, :, 2 * D:3 * D], wp_hi[:]]

            def split_wa(i):
                act.wait_ge(stage_in[i % 2], 16 * (i // 2 + 1))
                nc.scalar.activation(wa_dst[i], stage_a[:, i % 2], ACT.Identity).then_inc(wa_hi_made, 1)

            split_wa(0)
            split_wa(1)

            def affine(src, dst, b, free, st=cur_st):
                for c in range(C):
                    last = nc.scalar.activation(dst[:, c, :], src[:, c * P:(c + 1) * P], ACT.Identity,
                                                bias=st[:, b, C + c:C + c + 1], scale=st[:, b, c:c + 1])
                last.then_inc(free, 1)

            def norm_split(g, b, pos, full, free, cur, low, high, buf, dst):
                i, n = pos % 2, bank_uses(g, pos)
                act.wait_ge(cur, g + 2)
                act.wait_ge(full[i], n + 1)
                wait(act, low, GB * (g + 1) + b)
                affine(ps_g[i], buf, b, free[i])
                act.wait_ge(free[i], n + 1)
                nc.scalar.activation(dst[:, :, b * P:(b + 1) * P], buf[:], ACT.Identity).then_inc(high, 1)

            def norm_a(g, b, pos):
                norm_split(g, b, pos, g_full, g_free, cur_ready, lo_ready, hi_ready, hf, h_hi)

            for b in range(GB):
                norm_a(-1, b, 12 + b)
            split_wa(2)
            split_wa(3)

            def keys(g, m):
                if isinstance(g, int) and g == 0 and m == 0:
                    act.wait_ge(k_zeroed, 1)
                act.wait_ge(g_full[0], bank_uses(g, 2 * m) + 1)
                for j in range(HM):
                    q = slice(j * HD, (j + 1) * HD)
                    c = COL["bk0"] + m
                    last = nc.scalar.activation(k_diag[q, m, :, j, :], ps_g[0][q, :].rearrange("p (b t) -> p b t", b=GB),
                                                ACT.Identity, bias=cols[q, c:c + 1])
                last.then_inc(g_free[0], 1)

            def exps(g, u):
                b, m = u // C, u % C
                act.wait_ge(max_done, UNITS * g + u + 1)
                wait(act, tp_done, UNITS * g + u - 1)
                for j in range(HM):
                    h = m * HM + j
                    last = nc.scalar.activation(pa[:, u % 2, j, :], ps_s[u % 2][:, j * P:(j + 1) * P], ACT.Exp,
                                                bias=neg_max[:, u % 2, j:j + 1], accum_out=sums[:, b % 2, h:h + 1])
                last.then_inc(exp_done, 1)

            def copy_r(g, b):
                t = GB * g + b
                act.wait_ge(r_done, t + 1)
                wait(act, o_scaled, t)
                nc.scalar.activation(rs[:], ps_r[:], ACT.Copy, scale=INV_SQRT_D).then_inc(r_copied, 1)

            def round_o(g, b):
                t = GB * g + b
                act.wait_ge(o_scaled, t + 1)
                wait(act, proj_done, t - 1)
                nc.scalar.activation(o_hi[:, b % 2], of[:], ACT.Identity).then_inc(o_hi_ready, 1)

            def body(g, first, last):
                keys(g, 0)
                if not first:
                    copy_r(g - 1, GB - 1)
                    round_o(g - 1, GB - 1)
                for m in range(1, C):
                    keys(g, m)
                exps(g, 0)
                for u in range(UNITS):
                    b, m = u // C, u % C
                    if u + 1 < UNITS:
                        exps(g, u + 1)
                    if m == 0 and b > 0:
                        copy_r(g, b - 1)
                        round_o(g, b - 1)
                    if m == 2 and not last:
                        norm_a(g, b, [10, 12, 14, 15][b])

            groups(act, body)
            copy_r(NG - 1, GB - 1)
            round_o(NG - 1, GB - 1)

            act.wait_ge(s_done, UNITS * NG)
            for i in range(2):
                act.wait_ge(raw_in[2 + i], 16)
                nc.scalar.activation(wqk_hi[:, i], raw_b[:, 2 + i], ACT.Identity).then_inc(wqk_hi_made, 1)
            for i in range(C):
                act.wait_ge(wvp_done, i + 1)
                nc.scalar.activation(wvp_hi[:, i], bank[2 + i][:], ACT.Identity).then_inc(wvp_hi_made, 1)
            act.wait_ge(x1_ready, NB)
            for b in range(GB):
                act.wait_ge(x1_out[b], 16 * NG)
            act.wait_ge(film1_done, 1)
            nc.scalar.activation(fv1[:], ps_g[0][:], ACT.Identity).then_inc(film1_copied, 1)

            def squares(g, b, x, x_sem, sum_sem, var_sem):
                act.wait_ge(x_sem[b % 2], loaded(2 * g + b // 2 + 1))
                wait(act, var_sem, GB * g + b - 1)
                nc.scalar.activation(junk[:], x[:, b % 2], ACT.Square, accum_out=ssq[:, b % 2:b % 2 + 1])\
                    .then_inc(sum_sem, 1)

            def norm_b(g, b, pos):
                norm_split(g, b, pos, bg_full, bg_free, bcur, blo, bhi, hfb, hb_hi)

            def squares_b(g, b):
                wait(act, bssq, GB * g + b)
                squares(g, b, xb, bx_in, bssq, bvar)

            squares_b(0, 0)
            for b in range(GB):
                if b + 1 < GB:
                    squares_b(0, b + 1)
                norm_b(-1, b, 12 + b)

            def body_b(g, first, last):
                if not last:
                    squares_b(g + 1, 0)
                for m in range(C):
                    act.wait_ge(bg_full[0], bank_uses(g, 2 * m) + 1)
                    nc.scalar.activation(kb[:, m, :], ps_g[0][:], ACT.Identity, bias=col("bk1", m))\
                        .then_inc(bg_free[0], 1)
                for b in range(GB):
                    t = GB * g + b
                    act.wait_ge(bmax, t + 1)
                    wait(act, btp, t - 1)
                    nc.scalar.activation(pb[:, b % 2, :], ps_s[b % 2][:, 0:P], ACT.Exp, scale=INV_SQRT_D,
                                         bias=neg_max[:, b % 2, 1:2], accum_out=sums[:, b % 2, 0:1]).then_inc(bexp, 1)
                    act.wait_ge(bg_full[0], bank_uses(g, 8 + 2 * b) + 1)
                    nc.scalar.activation(vb[:, b, :], ps_g[0][:], ACT.Identity).then_inc(bg_free[0], 1)
                    if not last:
                        norm_b(g, b, 9 + 2 * b)
                        if b + 1 < GB:
                            squares_b(g + 1, b + 1)
                    if first:
                        if b == 0:
                            act.wait_ge(wqk_lo_made, 2)
                        act.wait_ge(w1_in[b % 2], 16 * (b // 2 + 1))
                        nc.scalar.activation(w1_hi[:, b, :], stage_w1[:, b % 2], ACT.Identity).then_inc(w1_hi_made, 1)

            groups(act, body_b)

            def squares_c(g, b):
                wait(act, cssq, GB * g + b)
                squares(g, b, xc, cx_in, cssq, cvar)

            def norm_c(g, b):
                t = GB * g + b
                act.wait_ge(ccur, g + 1)
                act.wait_ge(ct_full, t + 1)
                wait(act, clo, t - 1)
                affine(bank[7], hfc_act, b, ct_free_act)
                act.wait_ge(ct_free_act, 2 * g + b // 2 + 1)
                nc.scalar.activation(hc_hi[:, :, b * P:(b + 1) * P], hfc_act[:], ACT.Identity).then_inc(chi_act, 1)

            act.wait_ge(x2_ready, NB)
            squares_c(0, 0)
            squares_c(0, 1)
            squares_c(0, 2)
            squares_c(0, 3)
            norm_c(0, 1)
            norm_c(0, 3)

            def body_c(g, first, last):
                for f in range(FT):
                    n = FT * g + f
                    if first and f < FT // 2:
                        act.wait_ge(w2_in[f % 2], 16 * (f // 2 + 1))
                        nc.scalar.activation(w2_hi[:, 2 * f:2 * f + 2, :], stage_w2[:, f % 2], ACT.Identity)\
                            .then_inc(w2_hi_made, 1)
                    act.wait_ge(up_done, n + 1)
                    wait(act, g_lo_ready, n - 1)
                    nc.scalar.activation(gf[f % 2][:], bank[f % 2][:], ACT.Gelu, bias=cols[:, B1_COL + f:B1_COL + f + 1])\
                        .then_inc(gelu_done, 1)
                    if not last and f % 2 == 1 and 3 <= f < 3 + 2 * GB:
                        squares_c(g + 1, (f - 3) // 2)
                if not last:
                    norm_c(g + 1, 1)
                    norm_c(g + 1, 3)

            groups(act, body_c)

        @block.vector
        def _(dve):
            step = [0]

            def then(instruction):
                step[0] += 1
                instruction.then_inc(dve_step, 1)
                dve.wait_ge(dve_step, step[0])

            def low_half(dst, whole, high):
                return nc.vector.tensor_tensor(dst, whole, high.bitcast(F32), ALU.subtract)

            def table(st, c0):
                return st[:, :, c0:c0 + C].rearrange("p b c -> p c b")

            def mean_var(g, b):
                dve.wait_ge(x_in[b], loaded(g + 1))
                wait(dve, xn_ready, GB * g + b - 1)
                wait(dve, var_ready, 2 * (GB * g + b))
                nc.vector.bn_stats(stats[:], xa[:, b]).then_inc(bn_done, 1)
                wait_apart(dve, bn_done, GB * g + b + 1, dve_passed)
                nc.vector.bn_aggr(mv1[:, b % 2], stats[:]).then_inc(var_ready, 1)
                dve.wait_ge(var_ready, 2 * (GB * g + b) + 1)
                nc.vector.tensor_scalar(ve1[:, b % 2:b % 2 + 1], mv1[:, b % 2, 1:2], EPS_LN, None, ALU.add)\
                    .then_inc(var_ready, 1)

            mean_var(0, 0)
            mean_var(0, 1)
            dve.wait_ge(film0_t, 1)
            dve.wait_ge(consts_in, 32)
            ft = ps_s[1][:, 0:2 * NB * C].rearrange("p (c v b) -> p c v b", c=C, v=2)
            then(nc.vector.tensor_tensor(tmp_a[:], ft[:, :, 0, :], col_wide("bg"), ALU.add))
            then(nc.vector.tensor_tensor(tmp_b[:], ft[:, :, 1, :], col_wide("bb"), ALU.add))
            nc.vector.tensor_tensor(st_flat[:, 0:C, :], tmp_a[:], col_wide("ln_g"), ALU.mult)
            then(nc.vector.tensor_tensor(st_flat[:, C:2 * C, :], tmp_a[:], col_wide("ln_b"), ALU.mult))
            then(nc.vector.tensor_tensor(st_flat[:, C:2 * C, :], st_flat[:, C:2 * C, :], tmp_b[:], ALU.add))
            nc.vector.tensor_copy(st_ln[:], st_flat[:].rearrange("p v b -> p b v")).then_inc(st0_made, 1)

            wa_dst = [wa_lo[:, :, D:2 * D], wa_lo[:, :, 0:D], wa_lo[:, :, 2 * D:3 * D], wp_lo[:]]
            wa_src = [wa_hi[:, :, D:2 * D], wa_hi[:, :, 0:D], wa_hi[:, :, 2 * D:3 * D], wp_hi[:]]

            def split_wa(i):
                dve.wait_ge(wa_hi_made, i + 1)
                low_half(wa_dst[i], stage_a[:, i % 2], wa_src[i]).then_inc(wa_lo_made, 1)

            split_wa(0)
            split_wa(1)

            def norm_low(t, b, high, low, dst, buf, src):
                dve.wait_ge(high, t + 1)
                tok = slice(b * P, (b + 1) * P)
                low_half(dst[:, :, tok], buf[:], src[:, :, tok]).then_inc(low, 1)

            for b in range(GB):
                norm_low(b, b, hi_ready, lo_ready, h_lo, hf, h_hi)
                if b < 2:
                    mean_var(0, b + 2)
            dve.wait_ge(st0_t, 1)
            for i in range(2):
                nc.vector.tensor_copy(st_rows[:, i * D:(i + 1) * D], ps_t[i][0:NB, :]).then_inc(st_rows_made, 1)
            split_wa(2)
            split_wa(3)

            def row_max(g, u):
                dve.wait_ge(s_done, UNITS * g + u + 1)
                nc.vector.tensor_reduce(neg_max[:, u % 2, :], ps_s[u % 2][:].rearrange("p (h k) -> p h k", h=HM), AX.X,
                                        ALU.max, negate=True).then_inc(max_done, 1)

            def copy_v(g, b, pos):
                i = pos % 2
                dve.wait_ge(g_full[i], bank_uses(g, pos) + 1)
                nc.vector.tensor_tensor(va[:, b, :], ps_g[i][:], bv0[:], ALU.add).then_inc(g_free[i], 1)

            def copy_pt(g, u):
                dve.wait_ge(tp_done, UNITS * g + u + 1)
                wait(dve, pv_done, UNITS * g + u - 1)
                nc.vector.tensor_copy(pta[:, u % 2].rearrange("p h q -> p (h q)"), ps_t[u % 2][:]).then_inc(pt_copied, 1)

            def recip(g, b):
                t = GB * g + b
                wait(dve, r_copied, t)
                dve.wait_ge(exp_done, UNITS * g + C * b + C)
                nc.vector.reciprocal(rec[:], sums[:, b % 2, :]).then_inc(rec_made, 1)
                dve.wait_ge(rec_made, t + 1)
                nc.vector.tensor_copy(recx[:], rec[:].unsqueeze(2).broadcast_to([P, HEADS, HD]))\
                    .then_inc(rec_ready, 1)

            def scale_o(g, b):
                t = GB * g + b
                dve.wait_ge(r_copied, t + 1)
                wait(dve, o_lo_ready, t)
                dve.wait_ge(pv_done, UNITS * g + C * b + C)
                nc.vector.tensor_tensor(of[:].rearrange("p c t -> p (c t)"), ps_o[:], rs[:], ALU.mult)\
                    .then_inc(o_scaled, 1)

            def low_o(g, b):
                t = GB * g + b
                dve.wait_ge(o_hi_ready, t + 1)
                low_half(o_lo[:, b % 2], of[:], o_hi[:, b % 2]).then_inc(o_lo_ready, 1)

            def residual(g, b):
                t = GB * g + b
                dve.wait_ge(proj_done, t + 1)
                dve.wait_ge(xr_ready, t + 1)
                wait(dve, x1_out[b], 16 * g)
                nc.vector.tensor_tensor(h1[:, b], ps_r[:], xra[:, b % 2], ALU.add).then_inc(h1_ready, 1)

            def mean_var2(g):
                dve.wait_ge(h1_ready, GB * g + GB)
                wait(dve, ln2_scaled, GB * g)
                for b in range(GB):
                    nc.vector.bn_stats(stats2[:, b], h1[:, b]).then_inc(bn2_done, 1)
                for b in range(GB):
                    wait_apart(dve, bn2_done, 2 * GB * g + GB + b, dve_passed)
                    nc.vector.bn_aggr(mv2[:, b], stats2[:, b]).then_inc(bn2_done, 1)
                dve.wait_ge(bn2_done, 2 * GB * g + 2 * GB)
                nc.vector.tensor_scalar(ve2[:], mv2[:, :, 1], EPS_LN, None, ALU.add).then_inc(var2_ready, 1)

            def add_x1(g, b):
                dve.wait_ge(ln2_scaled, GB * g + b + 1)
                nc.vector.tensor_tensor(h1[:, b], h1[:, b], nb[:, b % 2], ALU.add).then_inc(x1_ready, 1)

            def body(g, first, last):
                for m in range(C):
                    if m == 0 and not first:
                        scale_o(g - 1, GB - 1)
                    dve.wait_ge(g_full[1], bank_uses(g, 2 * m + 1) + 1)
                    nc.vector.tensor_scalar(qa[:, m, :], ps_g[1][:], col("bq0", m), None, ALU.add).then_inc(g_free[1], 1)
                    if m == 0 and not first:
                        low_o(g - 1, GB - 1)
                    if not last:
                        mean_var(g + 1, m)
                    if m == 1 and not first:
                        residual(g - 1, GB - 1)
                        mean_var2(g - 1)
                if not first:
                    add_x1(g - 1, 0)
                row_max(g, 0)
                row_max(g, 1)
                for u in range(UNITS):
                    b, m = u // C, u % C
                    if m == 0:
                        copy_v(g, b, 8 if b == 0 else 7 + 2 * b)
                    copy_pt(g, u)
                    if m == 0 and b > 0:
                        scale_o(g, b - 1)
                    if m == 1 and b > 0:
                        low_o(g, b - 1)
                    if m == 3:
                        if not last:
                            norm_low(GB * (g + 1) + b, b, hi_ready, lo_ready, h_lo, hf, h_hi)
                        recip(g, b)
                        if b > 0:
                            residual(g, b - 1)
                    if u + 2 < UNITS:
                        row_max(g, u + 2)
                    if b == 0 and m > 0 and not first:
                        add_x1(g - 1, m)

            groups(dve, body)
            scale_o(NG - 1, GB - 1)
            low_o(NG - 1, GB - 1)
            residual(NG - 1, GB - 1)
            mean_var2(NG - 1)

            for i in range(2):
                dve.wait_ge(wqk_hi_made, i + 1)
                low_half(wqk_lo[:, i], raw_b[:, 2 + i], wqk_hi[:, i]).then_inc(wqk_lo_made, 1)
            for b in range(GB):
                add_x1(NG - 1, b)
            for i in range(C):
                dve.wait_ge(wvp_hi_made, i + 1)
                low_half(wvp_lo[:, i], bank[2 + i][:], wvp_hi[:, i]).then_inc(wvp_lo_made, 1)
            dve.wait_ge(rows_in, 64)
            dve.wait_ge(bvp_done, 1)
            nc.vector.tensor_tensor(cb1[:], ps_g[1][:], cb1[:], ALU.add).then_inc(cb_made, 1)
            dve.wait_ge(film1_t, 1)
            fl = ps_r[:].rearrange("p (c v b) -> p c v b", c=C, v=4)
            for i, (st, n) in enumerate(((st_f1, "1"), (st_f2, "2"))):
                then(nc.vector.tensor_tensor(tmp_a[:], fl[:, :, 2 * i, :], col_wide(f"f{n}scale"), ALU.add))
                then(nc.vector.tensor_scalar(tmp_a[:], tmp_a[:], 1.0, None, ALU.add))
                nc.vector.tensor_tensor(table(st, 0), tmp_a[:], col_wide(f"norm{n}"), ALU.mult)
                then(nc.vector.tensor_tensor(table(st, C), fl[:, :, 2 * i + 1, :], col_wide(f"f{n}shift"), ALU.add))
            nc.vector.memset(tmp_b[:, 0, 0:1], 0.0).then_inc(st1_made, 1)

            def mean_square(g, b, sum_sem, xn_sem, var_sem):
                dve.wait_ge(sum_sem, GB * g + b + 1)
                wait(dve, xn_sem, GB * g + b - 1)
                nc.vector.tensor_scalar(ve1[:, b % 2:b % 2 + 1], ssq[:, b % 2:b % 2 + 1], 1.0 / D, EPS_RMS, ALU.mult,
                                        ALU.add).then_inc(var_sem, 1)

            def norm_low_b(g, b):
                norm_low(GB * g + b, b, bhi, blo, hb_lo, hfb, hb_hi)

            mean_square(0, 0, bssq, bxn, bvar)
            for b in range(GB):
                if b + 1 < GB:
                    mean_square(0, b + 1, bssq, bxn, bvar)
                norm_low_b(0, b)

            def residual_b(g, b):
                t = GB * g + b
                dve.wait_ge(bpv, t + 1)
                dve.wait_ge(bxr, t + 1)
                nc.vector.scalar_tensor_tensor(xrb[:, b], bank[6 + b % 2][:], ssq_rec[:, b % 2:b % 2 + 1], xrb[:, b],
                                               ALU.mult, ALU.add).then_inc(x2_ready, 1)

            def body_b(g, first, last):
                if not last:
                    mean_square(g + 1, 0, bssq, bxn, bvar)
                for m in range(C):
                    dve.wait_ge(bg_full[1], bank_uses(g, 2 * m + 1) + 1)
                    nc.vector.tensor_scalar(qb[:, m, :], ps_g[1][:], col("bq1", m), None, ALU.add)\
                        .then_inc(bg_free[1], 1)
                for b in range(GB):
                    t = GB * g + b
                    dve.wait_ge(bs_done, t + 1)
                    nc.vector.tensor_reduce(neg_max[:, b % 2, 0:1], ps_s[b % 2][:, 0:P], AX.X, ALU.max, negate=True)\
                        .then_inc(braw, 1)
                    dve.wait_ge(braw, t + 1)
                    nc.vector.tensor_scalar(neg_max[:, b % 2, 1:2], neg_max[:, b % 2, 0:1], INV_SQRT_D, None, ALU.mult)\
                        .then_inc(bmax, 1)
                    dve.wait_ge(btp, t + 1)
                    wait(dve, bpv, t - 1)
                    nc.vector.tensor_copy(ptb[:, b % 2, :], ps_t[b % 2][:, 0:P]).then_inc(bpt, 1)
                    wait(dve, x2_ready, t - 1)
                    nc.vector.reciprocal(ssq_rec[:, b % 2:b % 2 + 1], sums[:, b % 2, 0:1]).then_inc(brec, 1)
                    if b > 0:
                        dve.wait_ge(brec, t)
                        residual_b(g, b - 1)
                    if not last:
                        norm_low_b(g + 1, b)
                        if b + 1 < GB:
                            mean_square(g + 1, b + 1, bssq, bxn, bvar)
                    if first:
                        dve.wait_ge(w1_hi_made, b + 1)
                        low_half(w1_lo[:, b, :], stage_w1[:, b % 2], w1_hi[:, b, :]).then_inc(w1_lo_made, 1)
                dve.wait_ge(brec, GB * g + GB)
                residual_b(g, GB - 1)

            groups(dve, body_b)

            def norm_c(g, b):
                t = GB * g + b
                tok = slice(b * P, (b + 1) * P)
                if b % 2 == 0:
                    dve.wait_ge(ccur, g + 1)
                    dve.wait_ge(ct_full, t + 1)
                    wait(dve, clo, t - 1)
                    for c in range(C):
                        last = nc.vector.tensor_scalar(hfc_dve[:, c, :], bank[6][:, c * P:(c + 1) * P],
                                                       cur_st[:, b, c:c + 1], cur_st[:, b, C + c:C + c + 1], ALU.mult,
                                                       ALU.add)
                    last.then_inc(ct_free_dve, 1)
                    dve.wait_ge(ct_free_dve, 2 * g + b // 2 + 1)
                    nc.vector.tensor_copy(hc_hi[:, :, tok], hfc_dve[:]).then_inc(chi_dve, 1)
                    dve.wait_ge(chi_dve, 2 * g + b // 2 + 1)
                    low_half(hc_lo[:, :, tok], hfc_dve[:], hc_hi[:, :, tok]).then_inc(clo, 1)
                else:
                    dve.wait_ge(chi_act, 2 * g + b // 2 + 1)
                    low_half(hc_lo[:, :, tok], hfc_act[:], hc_hi[:, :, tok]).then_inc(clo, 1)

            for b in range(GB):
                mean_square(0, b, cssq, cxn, cvar)
            for b in range(GB):
                norm_c(0, b)

            def body_c(g, first, last):
                for f in range(FT):
                    n = FT * g + f
                    if first and f < FT // 2:
                        dve.wait_ge(w2_hi_made, f + 1)
                        low_half(w2_lo[:, 2 * f:2 * f + 2, :], stage_w2[:, f % 2], w2_hi[:, 2 * f:2 * f + 2, :])\
                            .then_inc(w2_lo_made, 1)
                    r = f % (LAG + 1)
                    dve.wait_ge(gelu_done, n + 1)
                    if f >= LAG + 1:
                        dve.wait_ge(down_done, (FT - 1) * g + f - LAG)
                    elif f < LAG:
                        wait(dve, down_done, (FT - 1) * (g - 1) + FT - LAG + f)
                    else:
                        wait(dve, acc_done, GB * g)
                    nc.vector.tensor_copy(g_hi[:, r, :], gf[f % 2][:]).then_inc(g_hi_ready, 1)
                    dve.wait_ge(g_hi_ready, n + 1)
                    low_half(g_lo[:, r, :], gf[f % 2][:], g_hi[:, r, :]).then_inc(g_lo_ready, 1)
                    if not last and f % 2 == 0 and 4 <= f < 4 + 2 * GB:
                        mean_square(g + 1, (f - 4) // 2, cssq, cxn, cvar)
                if not last:
                    for b in range(GB):
                        norm_c(g + 1, b)
                for b in range(GB):
                    t = GB * g + b
                    dve.wait_ge(acc_done, t + 1)
                    dve.wait_ge(cxr, t + 1)
                    nc.vector.tensor_tensor(xrc[:, b], bank[2 + b][:], xrc[:, b], ALU.add).then_inc(y_ready, 1)

            groups(dve, body_c)

        @block.gpsimd
        def _(pool):
            nc.gpsimd.memset(ident[:], 0.0).then_inc(consts_made, 1)
            nc.gpsimd.memset(neg_half[:], -0.5).then_inc(consts_made, 1)
            pool.wait_ge(consts_made, 2)
            nc.gpsimd.affine_select(out=ident[:], in_=ident[:], compare_op=ALU.not_equal, fill=1.0, base=0,
                                    pattern=[[-1, P]], channel_multiplier=1).then_inc(consts_made, 1)

            def scales(g, table, cur, used):
                wait(pool, used, GB * g)
                nc.gpsimd.tensor_copy(cur_st[:], table[:, bass.ds(GB * g, GB), :]).then_inc(cur, 1)

            def norm_a(g, b):
                t = GB * g + b
                i = b % 2
                pool.wait_ge(var_ready, 2 * t + 2)
                nc.gpsimd.tensor_tensor(rstd1[:, i:i + 1], ve1[:, i:i + 1], neg_half[:, 0:1], ALU.pow)\
                    .then_inc(rstd_ready, 1)
                wait_apart(pool, rstd_ready, t + 1, pool_passed)
                nc.gpsimd.tensor_scalar(xa[:, b], xa[:, b], mv1[:, i, 0:1], rstd1[:, i:i + 1], ALU.subtract,
                                        ALU.mult).then_inc(xn_ready, 1)

            norm_a(0, 0)
            norm_a(0, 1)
            pool.wait_ge(st0_made, 1)
            scales(0, st_ln, cur_ready, hi_ready)
            nc.gpsimd.memset(k_diag[:], 0.0).then_inc(k_zeroed, 1)
            norm_a(0, 2)
            norm_a(0, 3)
            pool.wait_ge(rows_in, 64)

            def add_bias(t, i, x, row, x_sem, count, ready):
                pool.wait_ge(x_sem, count)
                nc.gpsimd.tensor_tensor(x[:, i], x[:, i], row[:], ALU.add).then_inc(ready, 1)

            def finish(g):
                pool.wait_ge(var2_ready, g + 1)
                nc.gpsimd.tensor_tensor(rstd2[:], ve2[:], neg_half[:], ALU.pow).then_inc(rstd2_ready, 1)
                wait_apart(pool, rstd2_ready, g + 1, pool_passed)
                for b in range(GB):
                    t = GB * g + b
                    i = b % 2
                    wait_apart(pool, x1_ready, GB * g + max(b - 1, 0), pool_passed)
                    nc.gpsimd.tensor_scalar(nb[:, i], h1[:, b], mv2[:, b, 0:1], rstd2[:, b:b + 1], ALU.subtract,
                                            ALU.mult).then_inc(ln2_normed, 1)
                    pool.wait_ge(rows_ld[i], loaded(2 * g + b // 2 + 1))
                    pool.wait_ge(ln2_normed, t + 1)
                    nc.gpsimd.tensor_tensor(nb[:, i], nb[:, i], rows[:, i, 0:D], ALU.mult)
                    nc.gpsimd.tensor_tensor(h1[:, b], h1[:, b], rows[:, i, D:2 * D], ALU.add).then_inc(ln2_scaled, 1)

            def body(g, first, last):
                if not last:
                    scales(g + 1, st_ln, cur_ready, hi_ready)
                    norm_a(g + 1, 0)
                    norm_a(g + 1, 1)
                if not first:
                    finish(g - 1)
                for b in range(GB):
                    if b >= 2 and not last:
                        norm_a(g + 1, b)
                    add_bias(GB * g + b, b % 2, xra, bp0, xr_in[b % 2], loaded(2 * g + b // 2 + 1), xr_ready)

            groups(pool, body)
            finish(NG - 1)

            def norm_rms(g, b, x, xn, slot, var, ready, freed, freed_at, rr):
                t = GB * g + b
                i = b % 2
                pool.wait_ge(var, t + 1)
                nc.gpsimd.tensor_tensor(rstd1[:, i:i + 1], ve1[:, i:i + 1], neg_half[:, 0:1], ALU.pow).then_inc(rr, 1)
                wait(pool, freed, freed_at)
                wait_apart(pool, rr, t + 1, pool_passed)
                nc.gpsimd.tensor_scalar(xn[:, slot], x[:, i], rstd1[:, i:i + 1], None, ALU.mult).then_inc(ready, 1)

            def norm_b(g, b):
                norm_rms(g, b, xb, xnb, b % 2, bvar, bxn, bhi, GB * g + b - 1, brstd)

            pool.wait_ge(st1_made, 1)
            pool.wait_ge(cb_made, 1)
            scales(0, st_f1, bcur, bhi)
            for b in range(GB):
                norm_b(0, b)

            def body_b(g, first, last):
                if not last:
                    scales(g + 1, st_f1, bcur, bhi)
                    norm_b(g + 1, 0)
                for b in range(GB):
                    add_bias(GB * g + b, b, xrb, cb1, bxr_in[b], loaded(g + 1), bxr)
                    if b + 1 < GB and not last:
                        norm_b(g + 1, b + 1)

            groups(pool, body_b)

            def norm_c(g, b):
                norm_rms(g, b, xc, xnc, b, cvar, cxn, clo, GB * g, crstd)

            pool.wait_ge(x2_ready, NB)
            scales(0, st_f2, ccur, clo)
            for b in range(GB):
                norm_c(0, b)

            def body_c(g, first, last):
                for b in range(GB):
                    add_bias(GB * g + b, b, xrc, b2, cxr_in[b], loaded(g + 1), cxr)
                if not last:
                    scales(g + 1, st_f2, ccur, clo)
                    for b in range(GB):
                        norm_c(g + 1, b)

            groups(pool, body_c)


def kernel(**inputs):
    import numpy as np
    import concourse.bacc as bacc
    from concourse.bass_utils import run_bass_kernel_spmd as run

    a = {k: np.asarray(v) for k, v in inputs.items()}
    l0, l1 = "L0_cond_", "L1_cond_"

    def chunks(v):
        return v.reshape(-1, P).T

    qkv_b = a[l0 + "bqkv"].reshape(D, 3)
    f1b, f2b = a[l1 + "film1_b"], a[l1 + "film2_b"]
    vectors = {
        "ln_g": a[l0 + "ln_g"], "ln_b": a[l0 + "ln_b"], "bg": a[l0 + "bg"], "bb": a[l0 + "bb"],
        "bq0": qkv_b[:, 0], "bk0": qkv_b[:, 1], "norm1": a[l1 + "norm1_w"], "f1scale": f1b[:D], "f1shift": f1b[D:],
        "bq1": a[l1 + "q_b"], "bk1": a[l1 + "k_b"], "bv1": a[l1 + "v_b"], "norm2": a[l1 + "norm2_w"],
        "f2scale": f2b[:D], "f2shift": f2b[D:],
    }
    arrays = {
        "xt": a["x"].reshape(NB * P, D),
        "cond_t": a["cond_1024"].T,
        "cols_d": np.concatenate([chunks(vectors[n]) for n in COLS] + [chunks(a[l1 + "mlp_b1"])], axis=1),
        "bp0_d": a[l0 + "bp"],
        "bv0_d": qkv_b[:, 2],
        "pb1_d": a[l1 + "proj_b"],
        "b2_d": a[l1 + "mlp_b2"],
        "wg_t": a[l0 + "Wg"].T,
        "wb_t": a[l0 + "Wb"].T,
        "wqkv": a[l0 + "Wqkv"].reshape(D, 3, D).transpose(2, 1, 0).reshape(D, 3 * D),
        "wp0": a[l0 + "Wp"].T,
        "film1": a[l1 + "film1_w"],
        "film2": a[l1 + "film2_w"],
        "wq1": a[l1 + "q_w"],
        "wk1": a[l1 + "k_w"],
        "wv1_t": a[l1 + "v_w"].T,
        "wp1": a[l1 + "proj_w"],
        "w1": a[l1 + "mlp_w1"],
        "w2": a[l1 + "mlp_w2"],
    }
    nc = bacc.Bacc("TRN2", target_bir_lowering=False, num_devices=1)
    sent, args = {}, {}
    for name, v in arrays.items():
        sent[name + "_in"] = v = np.ascontiguousarray(v)
        args[name] = nc.dram_tensor(name + "_in", v.shape, mybir.dt.from_np(v.dtype), kind="ExternalInput").ap()
    out = nc.dram_tensor("out", (NB * P, D), F32, kind="ExternalOutput").ap()
    block_pair_kernel(nc, **args, out=out)
    r = run(nc, [sent], core_ids=[0])
    return r.results[0]["out"].reshape(NB, P, D)
```

```python
import concourse.bass as bass
from concourse import mybir
from contextlib import ExitStack

F32 = mybir.dt.float32
F32R = mybir.dt.float32r
BF16 = mybir.dt.bfloat16
ALU = mybir.AluOpType
ACT = mybir.ActivationFunctionType
AX = mybir.AxisListType

P = 128
D = 512
C = D // P
NB = 32
GB = 4
GT = GB * P
NG = NB // GB
HEADS = 16
HD = D // HEADS
HM = P // HD
UNITS = GB * C
FF = 4 * D
FT = FF // P
LAG = 3
EPS_LN, EPS_RMS = 1e-5, 1e-6
INV_SQRT_D = float(D) ** -0.5

COLS = ["ln_g", "ln_b", "bg", "bb", "bq0", "bk0", "norm1", "f1scale", "f1shift", "bq1", "bk1", "bv1",
        "norm2", "f2scale", "f2shift"]
COL = {n: i * C for i, n in enumerate(COLS)}
B1_COL = len(COLS) * C
N_COLS = B1_COL + FT


def wait(engine, sem, value):
    if isinstance(value, int) and value <= 0:
        return
    engine.wait_ge(sem, value)


def wait_apart(engine, sem, value, passed):
    wait(engine, sem, value)
    if not isinstance(value, int):
        engine.sem_inc(passed, 1)


def bank_uses(g, pos):
    return 8 * g + 2 + pos // 2


def groups(engine, body):
    body(0, True, False)
    with engine.Fori(1, NG - 1) as g:
        body(g, False, False)
    body(NG - 1, False, True)


def block_pair_kernel(nc, xt, cond_t, cols_d, bp0_d, bv0_d, pb1_d, b2_d, wg_t, wb_t, wqkv, wp0,
                      film1, film2, wq1, wk1, wv1_t, wp1, w1, w2, out):
    with ExitStack() as ctx:
        base = 16512
        kib = 1024

        def at(name, shape, dt, offset):
            return nc.alloc_sbuf_tensor_at(name, shape, dt, offset=base + offset)

        class Run:

            def __init__(self, offset):
                self.offset = offset

            def __call__(self, name, shape, dt=F32):
                n = 1
                for s in shape[1:]:
                    n *= s
                t = at(name, shape, dt, self.offset)
                self.offset += -(-n * (2 if dt == BF16 else 4) // 32) * 32
                return t

        keep = Run(0)
        ident = keep("ident", [P, P])
        cols = keep("cols", [P, N_COLS])
        cond = keep("cond", [P, C, NB])
        st_at = keep.offset
        st_ln = keep("st_ln", [P, NB, 2 * C])
        st_f1 = keep("st_f1", [P, NB, 2 * C])
        st_f2 = keep("st_f2", [P, NB, 2 * C])
        st_flat_at = keep.offset
        st_flat = keep("st_flat", [P, 2 * C, NB])
        junk = at("junk", [P, D], BF16, st_flat_at)
        tmp_at = keep.offset
        tmp_a = keep("tmp_a", [P, C, NB])
        tmp_b = keep("tmp_b", [P, C, NB])
        cur_st = keep("cur_st", [P, GB, 2 * C])
        neg_half = keep("neg_half", [P, GB])
        stats = keep("stats", [P, 6])
        mv1 = keep("mv1", [P, 2, 2])
        ve1 = keep("ve1", [P, 2])
        rstd1 = keep("rstd1", [P, 2])
        stats2 = keep("stats2", [P, GB, 6])
        mv2 = keep("mv2", [P, GB, 2])
        ve2 = keep("ve2", [P, GB])
        rstd2 = keep("rstd2", [P, GB])
        neg_max = keep("neg_max", [P, 2, HM])
        sums = keep("sums", [P, 2, HEADS])
        rec = keep("rec", [P, HEADS])
        ssq = keep("ssq", [P, 2])
        ssq_rec = keep("ssq_rec", [P, 2])
        rows_at = keep.offset
        bp0 = keep("bp0", [P, D])
        bv0 = keep("bv0", [P, D])
        cb1 = keep("cb1", [P, D])
        b2 = keep("b2", [P, D])
        R0 = -(-keep.offset // 64) * 64

        run = Run(R0)
        wa_hi = run("wa_hi", [P, C, 3 * D], F32R)
        wa_lo = run("wa_lo", [P, C, 3 * D], F32R)
        wp_hi = run("wp_hi", [P, C, D], F32R)
        wp_lo = run("wp_lo", [P, C, D], F32R)
        k_diag = run("k_diag", [P, C, GB, HM, P])
        h_hi = run("h_hi", [P, C, GT], F32R)
        h_lo = run("h_lo", [P, C, GT], F32R)
        work_at = run.offset
        xa = run("xa", [P, GB, D])
        hf = run("hf", [P, 2, C, P])
        qa = run("qa", [P, C, GT])
        va = run("va", [P, GB, D])
        pa_at = run.offset
        pa = run("pa", [P, 2, HM, P])
        pta = run("pta", [P, 2, HM, P])
        recx = run("recx", [P, HEADS, HD])
        rs = run("rs", [P, D])
        of = run("of", [P, C, P])
        o_hi = run("o_hi", [P, 2, C, P], F32R)
        o_lo = run("o_lo", [P, 2, C, P], F32R)
        xra = run("xra", [P, 2, D])
        stage_at = run.offset
        h1 = run("h1", [P, GB, D])
        rows = run("rows", [P, 2, 2 * D])
        nb = run("nb", [P, GB, D])
        assert base + run.offset <= 229344
        stage_a = at("stage_a", [P, 2, C, D], F32, stage_at)
        wgb = at("wgb", [P, 2, C, D], F32, R0 + 96 * kib)
        fv0 = at("fv0", [2 * NB, D], F32, pa_at)
        st_rows = at("st_rows", [NB, 2 * D], F32, pa_at + 4 * kib)

        raw_b = at("raw_b", [P, 4, C, D], F32, R0)
        film_b = at("film_b", [P, 2, C, 2 * D], F32, R0 + 32 * kib)
        run = Run(R0 + 64 * kib)
        wqk_hi = run("wqk_hi", [P, 2, C, D], F32R)
        wqk_lo = run("wqk_lo", [P, 2, C, D], F32R)
        wvp_hi = run("wvp_hi", [P, C, D], F32R)
        wvp_lo = run("wvp_lo", [P, C, D], F32R)
        assert run.offset == work_at
        qb = run("qb", [P, C, GT])
        kb = run("kb", [P, C, GT])
        hb_at = run.offset
        hb_hi = run("hb_hi", [P, C, GT], F32R)
        hb_lo = run("hb_lo", [P, C, GT], F32R)
        xb = run("xb", [P, 2, D])
        xnb = run("xnb", [P, GB, D])
        vb_at = run.offset
        vb = run("vb", [P, GB, D])
        xrb_at = run.offset
        assert xrb_at <= stage_at
        xrb = run("xrb", [P, GB, D])
        stage_w1_at = run.offset
        stage_w1 = run("stage_w1", [P, 2, FF])
        assert base + run.offset <= 229344
        ptb = at("ptb", [P, 2, P], F32, st_at)
        pb = at("pb", [P, 2, P], F32, tmp_at)
        fv1 = at("fv1", [P, D], F32, vb_at)
        hfb = at("hfb", [P, 2, C, P], F32, rows_at)

        run = Run(R0)
        w1_hi = run("w1_hi", [P, C, FF], F32R)
        w1_lo = run("w1_lo", [P, C, FF], F32R)
        w2_hi = run("w2_hi", [P, FT, D], F32R)
        w2_lo = run("w2_lo", [P, FT, D], F32R)
        assert run.offset == hb_at
        hc_hi, hc_lo, xc, xnc = hb_hi, hb_lo, xb, xnb
        run = Run(vb_at)
        hfc_act = run("hfc_act", [P, C, P])
        stage_w2 = [None, run("stage_w2_1", [P, 2, D])]
        assert run.offset <= xrb_at
        xrc = at("xrc", [P, GB, D], F32, xrb_at)
        run = Run(stage_w1_at)
        g_hi = run("g_hi", [P, LAG + 1, GT], F32R)
        g_lo = run("g_lo", [P, LAG + 1, GT], F32R)
        stage_w2[0] = run("stage_w2_0", [P, 2, D])
        assert base + run.offset <= 229344
        run = Run(rows_at)
        hfc_dve = run("hfc_dve", [P, C, P])
        gf1 = run("gf1", [P, GT])
        gf0 = at("gf0", [P, GT], F32, st_at)
        gf = [gf0, gf1]

        bank = [ctx.enter_context(nc.psum_tensor(f"bank{i}", [P, D], F32)) for i in range(8)]
        ps_g = bank[0:2]
        ps_s = bank[2:4]
        ps_t = bank[4:6]
        ps_o = bank[6]
        ps_r = bank[7]

        st_dram = nc.dram_tensor("st_dram", (NB, 2 * D), F32).ap()
        x1_dram = nc.dram_tensor("x1_dram", (NB * P, D), F32).ap()
        x2_dram = nc.dram_tensor("x2_dram", (NB * P, D), F32).ap()

        def sem(name):
            return ctx.enter_context(nc.semaphore(name))

        consts_in, rows_in, wgb_in = sem("consts_in"), sem("rows_in"), sem("wgb_in")
        consts_made, k_zeroed = sem("consts_made"), sem("k_zeroed")
        bn_done, bn2_done, rstd_ready, rstd2_ready = sem("bn_done"), sem("bn2_done"), sem("rstd_ready"), sem("rstd2_ready")
        ln2_normed, braw, brstd, crstd = sem("ln2_normed"), sem("braw"), sem("brstd"), sem("crstd")
        film0_done, film0_copied, film0_t = sem("film0_done"), sem("film0_copied"), sem("film0_t")
        st0_made, st0_t, st_rows_made = sem("st0_made"), sem("st0_t"), sem("st_rows_made")
        st_stored = sem("st_stored")
        stage_in = [sem("stage_in0"), sem("stage_in1")]
        wa_hi_made, wa_lo_made = sem("wa_hi_made"), sem("wa_lo_made")
        dve_step, dve_passed, pool_passed = sem("dve_step"), sem("dve_passed"), sem("pool_passed")
        x_in = [sem(f"x_in{b}") for b in range(GB)]
        xr_in = [sem("xr_in0"), sem("xr_in1")]
        rows_ld = [sem("rows_ld0"), sem("rows_ld1")]
        x1_out = [sem(f"x1_out{b}") for b in range(GB)]
        var_ready, xn_ready, cur_ready = sem("var_ready"), sem("xn_ready"), sem("cur_ready")
        hi_ready, lo_ready = sem("hi_ready"), sem("lo_ready")
        g_full = [sem("g_full0"), sem("g_full1")]
        g_free = [sem("g_free0"), sem("g_free1")]
        s_done, max_done, exp_done = sem("s_done"), sem("max_done"), sem("exp_done")
        tp_done, pt_copied, pv_done = sem("tp_done"), sem("pt_copied"), sem("pv_done")
        rec_made, rec_ready, r_done, r_copied = sem("rec_made"), sem("rec_ready"), sem("r_done"), sem("r_copied")
        o_scaled, o_hi_ready, o_lo_ready = sem("o_scaled"), sem("o_hi_ready"), sem("o_lo_ready")
        proj_done, xr_ready, h1_ready = sem("proj_done"), sem("xr_ready"), sem("h1_ready")
        var2_ready, ln2_shifted, x1_ready = sem("var2_ready"), sem("ln2_shifted"), sem("x1_ready")
        raw_in = [sem(f"raw_in{i}") for i in range(4)]
        film_in = [sem("film_in0"), sem("film_in1")]
        wqk_hi_made, wqk_lo_made = sem("wqk_hi_made"), sem("wqk_lo_made")
        wvp_done, wvp_hi_made, wvp_lo_made = sem("wvp_done"), sem("wvp_hi_made"), sem("wvp_lo_made")
        bvp_done, film1_done, film1_copied = sem("bvp_done"), sem("film1_done"), sem("film1_copied")
        film1_t, st1_made, cb_made = sem("film1_t"), sem("st1_made"), sem("cb_made")
        bx_in = [sem("bx_in0"), sem("bx_in1")]
        bxr_in = [sem(f"bxr_in{b}") for b in range(GB)]
        x2_out = [sem(f"x2_out{b}") for b in range(GB)]
        bssq, bvar, bxn, bcur = sem("bssq"), sem("bvar"), sem("bxn"), sem("bcur")
        bhi, blo = sem("bhi"), sem("blo")
        bg_full = [sem("bg_full0"), sem("bg_full1")]
        bg_free = [sem("bg_free0"), sem("bg_free1")]
        bs_done, bmax, bexp, btp, bpt = sem("bs_done"), sem("bmax"), sem("bexp"), sem("btp"), sem("bpt")
        bpv, brec, bxr, x2_ready = sem("bpv"), sem("brec"), sem("bxr"), sem("x2_ready")
        w1_in = [sem("w1_in0"), sem("w1_in1")]
        w1_hi_made, w1_lo_made = sem("w1_hi_made"), sem("w1_lo_made")
        w2_in = [sem("w2_in0"), sem("w2_in1")]
        w2_hi_made, w2_lo_made = sem("w2_hi_made"), sem("w2_lo_made")
        cx_in = [sem("cx_in0"), sem("cx_in1")]
        cxr_in = [sem(f"cxr_in{b}") for b in range(GB)]
        y_out = [sem(f"y_out{b}") for b in range(GB)]
        cssq, cvar, cxn, ccur = sem("cssq"), sem("cvar"), sem("cxn"), sem("ccur")
        ct_full, ct_free_act, ct_free_dve = sem("ct_full"), sem("ct_free_act"), sem("ct_free_dve")
        chi_act, chi_dve, clo = sem("chi_act"), sem("chi_dve"), sem("clo")
        up_done, gelu_done = sem("up_done"), sem("gelu_done")
        g_hi_ready, g_lo_ready, down_done = sem("g_hi_ready"), sem("g_lo_ready"), sem("down_done")
        acc_done, cxr, y_ready = sem("acc_done"), sem("cxr"), sem("y_ready")

        block = ctx.enter_context(nc.Block())

        def tokens(dram, t):
            return dram[bass.ts(t, P), :]

        def weight(dram):
            return dram.rearrange("(k p) n -> p k n", p=P)

        def col(name, c):
            return cols[:, COL[name] + c:COL[name] + c + 1]

        def col_wide(name):
            return cols[:, COL[name]:COL[name] + C].unsqueeze(2).broadcast_to([P, C, NB])

        def loaded(n):
            return 16 * n

        @block.sync
        def _(sp):
            sp.dma_start(cols[:], cols_d).then_inc(consts_in, 16)
            sp.dma_start(cond[:], cond_t.rearrange("(k p) b -> p k b", p=P)).then_inc(consts_in, 16)
            for t in range(2):
                sp.dma_start(xa[:, t], tokens(xt, t)).then_inc(x_in[t], 16)
            sp.dma_start(wgb[:, 0], weight(wg_t)).then_inc(wgb_in, 16)
            sp.dma_start(wgb[:, 1], weight(wb_t)).then_inc(wgb_in, 16)
            for t in range(2, GB):
                sp.dma_start(xa[:, t], tokens(xt, t)).then_inc(x_in[t], 16)
            units = [wqkv[:, D:2 * D], wqkv[:, 0:D], wqkv[:, 2 * D:3 * D], wp0]
            for i in range(2):
                sp.dma_start(stage_a[:, i], weight(units[i])).then_inc(stage_in[i], 16)
            for row, src in ((bp0, bp0_d), (bv0, bv0_d), (cb1, pb1_d), (b2, b2_d)):
                sp.dma_start(row[:], src.partition_broadcast(P)).then_inc(rows_in, 16)
            for i in range(2, 4):
                sp.wait_ge(wa_lo_made, i - 1)
                sp.dma_start(stage_a[:, i % 2], weight(units[i])).then_inc(stage_in[i % 2], 16)
            sp.wait_ge(st_rows_made, 2)
            sp.dma_start(st_dram[:], st_rows[:]).then_inc(st_stored, 16)
            sp.wait_ge(st_stored, 16)

            def load_x(g, b):
                wait(sp, hi_ready, GB * (g - 1) + b + 1)
                sp.dma_start(xa[:, b], tokens(xt, GB * g + b)).then_inc(x_in[b], 16)

            def load_xr(g, b):
                wait(sp, h1_ready, GB * g + b - 1)
                sp.dma_start(xra[:, b % 2], tokens(xt, GB * g + b)).then_inc(xr_in[b % 2], 16)

            def load_rows(g, b):
                wait(sp, ln2_shifted, GB * g + max(b - 1, 0))
                sp.dma_start(rows[:, b % 2], st_dram[bass.ds(GB * g + b, 1), :].partition_broadcast(P))\
                    .then_inc(rows_ld[b % 2], 16)

            def store_x1(g, b):
                sp.wait_ge(x1_ready, GB * g + b + 1)
                sp.dma_start(tokens(x1_dram, GB * g + b), h1[:, b]).then_inc(x1_out[b], 16)

            def finish(g):
                for b in range(GB):
                    load_rows(g, b)
                for b in range(GB):
                    store_x1(g, b)

            def body(g, first, last):
                if not last:
                    for b in range(GB):
                        load_x(g + 1, b)
                load_xr(g, 0)
                load_xr(g, 1)
                if not first:
                    finish(g - 1)
                load_xr(g, 2)
                load_xr(g, 3)

            groups(sp, body)

            sp.wait_ge(g_free[1], bank_uses(NG - 1, 13) + 1)
            for i, w in enumerate((wv1_t, wp1, wq1, wk1)):
                sp.dma_start(raw_b[:, i], weight(w)).then_inc(raw_in[i], 16)
            sp.dma_start(film_b[:, 0], weight(film1)).then_inc(film_in[0], 16)
            sp.wait_ge(proj_done, NB)

            def load_bx(g, b, source=x1_dram, t=None):
                wait(sp, bxn, GB * g + b - 1)
                sp.dma_start(xb[:, b % 2], tokens(source, GB * g + b if t is None else t))\
                    .then_inc(bx_in[b % 2], 16)

            for b in range(GB):
                sp.wait_ge(x1_out[b], 16 * (NG - 1))
            load_bx(0, 0)
            load_bx(0, 1)
            load_rows(NG - 1, 0)
            load_rows(NG - 1, 1)
            sp.dma_start(film_b[:, 1], weight(film2)).then_inc(film_in[1], 16)
            load_bx(0, 2)
            load_bx(0, 3)
            load_rows(NG - 1, 2)
            load_rows(NG - 1, 3)
            for b in range(GB):
                store_x1(NG - 1, b)
            for b in range(GB):
                sp.wait_ge(x1_out[b], 16 * NG)

            def load_bxr(g, b):
                wait(sp, x2_out[b], 16 * g)
                sp.dma_start(xrb[:, b], tokens(x1_dram, GB * g + b)).then_inc(bxr_in[b], 16)

            def store_x2(g, b):
                sp.wait_ge(x2_ready, GB * g + b + 1)
                sp.dma_start(tokens(x2_dram, GB * g + b), xrb[:, b]).then_inc(x2_out[b], 16)

            def load_w2(i):
                wait(sp, w2_lo_made, i - 1)
                sp.dma_start(stage_w2[i % 2][:], weight(w2[2 * i * P:2 * (i + 1) * P, :]))\
                    .then_inc(w2_in[i % 2], 16)

            def load_next(g, b, last):
                if last:
                    sp.wait_ge(x2_out[b], 16)
                    load_bx(NG, b, x2_dram, b)
                else:
                    load_bx(g + 1, b)

            def body_b(g, first, last):
                load_next(g, 0, last)
                load_next(g, 1, last)
                for b in range(GB):
                    load_bxr(g, b)
                if first:
                    for k in range(2):
                        sp.dma_start(stage_w1[:, k], w1[k * P:(k + 1) * P, :]).then_inc(w1_in[k], 16)
                load_next(g, 2, last)
                load_next(g, 3, last)
                if last:
                    load_w2(0)
                store_x2(g, 0)
                if first:
                    sp.wait_ge(w1_lo_made, 1)
                    sp.dma_start(stage_w1[:, 0], w1[2 * P:3 * P, :]).then_inc(w1_in[0], 16)
                store_x2(g, 1)
                if first:
                    sp.wait_ge(w1_lo_made, 2)
                    sp.dma_start(stage_w1[:, 1], w1[3 * P:4 * P, :]).then_inc(w1_in[1], 16)
                store_x2(g, 2)
                store_x2(g, 3)

            groups(sp, body_b)

            for b in range(GB):
                sp.wait_ge(x2_out[b], 16 * NG)

            def load_cx(g, b):
                wait(sp, cxn, GB * g + b - 1)
                sp.dma_start(xc[:, b % 2], tokens(x2_dram, GB * g + GB + b)).then_inc(cx_in[b % 2], 16)

            def load_cxr(g, b):
                wait(sp, y_out[b], 16 * g)
                sp.dma_start(xrc[:, b], tokens(x2_dram, GB * g + b)).then_inc(cxr_in[b], 16)

            def store_y(g, b):
                sp.wait_ge(y_ready, GB * g + b + 1)
                sp.dma_start(tokens(out, GB * g + b), xrc[:, b]).then_inc(y_out[b], 16)

            sp.wait_ge(bxn, NB + GB)

            def body_c(g, first, last):
                if first:
                    load_w2(1)
                if not first:
                    for b in range(GB):
                        store_y(g - 1, b)
                for b in range(GB):
                    load_cxr(g, b)
                if not last:
                    for b in range(2):
                        load_cx(g, b)
                if first:
                    for i in range(2, FT // 2):
                        load_w2(i)
                if not last:
                    for b in range(2, GB):
                        load_cx(g, b)

            groups(sp, body_c)
            for b in range(GB):
                store_y(NG - 1, b)
            for b in range(GB):
                sp.wait_ge(y_out[b], 16 * NG)

        @block.tensor
        def _(pe):
            def split_product(dst, w_hi, w_lo, a_hi, a_lo, start, stop):
                nc.tensor.matmul(dst, w_hi, a_hi, start=start, stop=False)
                nc.tensor.matmul(dst, w_hi, a_lo, start=False, stop=False)
                return nc.tensor.matmul(dst, w_lo, a_hi, start=False, stop=stop)

            pe.wait_ge(consts_in, 32)
            pe.wait_ge(wgb_in, 32)
            for k in range(C):
                for i in range(2):
                    last = nc.tensor.matmul(ps_s[0][NB * i:NB * (i + 1), :], cond[:, k, :], wgb[:, i, k, :],
                                            start=(k == 0), stop=(k == C - 1))
            last.then_inc(film0_done, 1)
            pe.wait_ge(consts_made, 3)
            pe.wait_ge(film0_copied, 1)
            for c in range(C):
                last = nc.tensor.transpose(ps_s[1][:, 2 * NB * c:2 * NB * (c + 1)], fv0[:, c * P:(c + 1) * P],
                                           ident[0:2 * NB, 0:2 * NB])
            last.then_inc(film0_t, 1)
            pe.wait_ge(st0_made, 1)
            for i in range(2):
                for c in range(C):
                    last = nc.tensor.transpose(ps_t[i][0:NB, c * P:(c + 1) * P], st_flat[:, i * C + c, :], ident[:])
            last.then_inc(st0_t, 1)

            def norm_t(g, b, pos, banks_full, banks_free, xn, slot, ready):
                i, n = pos % 2, bank_uses(g, pos)
                pe.wait_ge(ready, GB * (g + 1) + b + 1)
                wait(pe, banks_free[i], n)
                for c in range(C):
                    last = nc.tensor.transpose(ps_g[i][:, c * P:(c + 1) * P], xn[:, slot, c * P:(c + 1) * P], ident[:])
                last.then_inc(banks_full[i], 1)

            def norm_a(g, b, pos):
                norm_t(g, b, pos, g_full, g_free, xa, b, xn_ready)

            for b in range(GB):
                norm_a(-1, b, 12 + b)

            def qk(g, m, pos, offset):
                i = pos % 2
                pe.wait_ge(g_free[i], bank_uses(g, pos))
                for k in range(C):
                    n = slice(offset + m * P, offset + (m + 1) * P)
                    last = split_product(ps_g[i][:], wa_hi[:, k, n], wa_lo[:, k, n], h_hi[:, k, :], h_lo[:, k, :],
                                         k == 0, k == C - 1)
                last.then_inc(g_full[i], 1)

            def values(g, b, pos, ks):
                i = pos % 2
                if ks[0] == 0:
                    pe.wait_ge(g_free[i], bank_uses(g, pos))
                t = slice(b * P, (b + 1) * P)
                for k in ks:
                    last = split_product(ps_g[i][:], h_hi[:, k, t], h_lo[:, k, t], wa_hi[:, k, 2 * D:3 * D],
                                         wa_lo[:, k, 2 * D:3 * D], k == 0, k == C - 1)
                if ks[-1] == C - 1:
                    last.then_inc(g_full[i], 1)

            def v_pos(b):
                return 8 if b == 0 else 7 + 2 * b

            def scores(g, u):
                b, m = u // C, u % C
                if b == 0:
                    pe.wait_ge(g_free[0], bank_uses(g, 2 * m) + 1)
                    pe.wait_ge(g_free[1], bank_uses(g, 2 * m + 1) + 1)
                wait(pe, exp_done, UNITS * g + u - 1)
                nc.tensor.matmul(ps_s[u % 2][:], qa[:, m, b * P:(b + 1) * P], k_diag[:, m, b, :, :],
                                 start=True, stop=True).then_inc(s_done, 1)

            def transpose_p(g, u):
                pe.wait_ge(exp_done, UNITS * g + u + 1)
                wait(pe, pt_copied, UNITS * g + u - 1)
                for j in range(HM):
                    last = nc.tensor.transpose(ps_t[u % 2][:, j * P:(j + 1) * P], pa[:, u % 2, j, :], ident[:])
                last.then_inc(tp_done, 1)

            def attend(g, u):
                b, m = u // C, u % C
                pe.wait_ge(pt_copied, UNITS * g + u + 1)
                if m == 0:
                    pe.wait_ge(g_free[v_pos(b) % 2], bank_uses(g, v_pos(b)) + 1)
                    wait(pe, o_scaled, GB * g + b)
                for j in range(HM):
                    f = (m * HM + j) * HD
                    last = nc.tensor.matmul(ps_o[j * HD:(j + 1) * HD, m * P:(m + 1) * P], va[:, b, f:f + HD],
                                            pta[:, u % 2, j, :], start=True, stop=True)
                last.then_inc(pv_done, 1)

            def recip_t(g, b):
                pe.wait_ge(rec_ready, GB * g + b + 1)
                wait(pe, h1_ready, GB * g + b)
                flat = recx[:].rearrange("p h d -> p (h d)")
                for m in range(C):
                    last = nc.tensor.transpose(ps_r[:, m * P:(m + 1) * P], flat[:, m * P:(m + 1) * P], ident[:])
                last.then_inc(r_done, 1)

            def project(g, b, ks):
                if ks[0] == 0:
                    pe.wait_ge(o_hi_ready, GB * g + b + 1)
                    pe.wait_ge(o_lo_ready, GB * g + b + 1)
                    pe.wait_ge(r_copied, GB * g + b + 1)
                for k in ks:
                    last = split_product(ps_r[:], o_hi[:, b % 2, k, :], o_lo[:, b % 2, k, :], wp_hi[:, k, :],
                                         wp_lo[:, k, :], k == 0, k == C - 1)
                if ks[-1] == C - 1:
                    last.then_inc(proj_done, 1)

            def body(g, first, last):
                pe.wait_ge(hi_ready, GB * g + GB)
                pe.wait_ge(lo_ready, GB * g + GB)
                for m in range(C):
                    if first and m == 0:
                        pe.wait_ge(wa_hi_made, 2)
                        pe.wait_ge(wa_lo_made, 2)
                    qk(g, m, 2 * m, D)
                    if m == 0 and not first:
                        recip_t(g - 1, GB - 1)
                    qk(g, m, 2 * m + 1, 0)
                    if m == 1 and not first:
                        project(g - 1, GB - 1, range(C))
                    if m >= 2:
                        scores(g, m - 2)
                if first:
                    pe.wait_ge(wa_hi_made, 3)
                    pe.wait_ge(wa_lo_made, 3)
                values(g, 0, v_pos(0), range(C))
                for u in range(UNITS):
                    b, m = u // C, u % C
                    transpose_p(g, u)
                    if u + 2 < UNITS:
                        scores(g, u + 2)
                    if u > 0:
                        attend(g, u - 1)
                    if m == 0 and b > 0:
                        recip_t(g, b - 1)
                    if b < GB - 1:
                        values(g, b + 1, v_pos(b + 1), [m])
                    if m == 1 and not last:
                        norm_a(g, b, [10, 12, 14, 15][b])
                    if b > 0 and m >= 2:
                        if first and b == 1 and m == 2:
                            pe.wait_ge(wa_hi_made, 4)
                            pe.wait_ge(wa_lo_made, 4)
                        project(g, b - 1, [0, 1] if m == 2 else [2, 3])
                attend(g, UNITS - 1)

            groups(pe, body)

            recip_t(NG - 1, GB - 1)
            pe.wait_ge(raw_in[0], 16)
            pe.wait_ge(raw_in[1], 16)
            for i in range(C):
                if i == 1:
                    project(NG - 1, GB - 1, range(C))
                for k in range(C):
                    last = nc.tensor.matmul(bank[2 + i][:], raw_b[:, 0, k, i * P:(i + 1) * P], raw_b[:, 1, k, :],
                                            start=(k == 0), stop=(k == C - 1))
                last.then_inc(wvp_done, 1)
            pe.wait_ge(g_free[1], bank_uses(NG - 1, 13) + 1)
            for k in range(C):
                last = nc.tensor.matmul(ps_g[1][:], col("bv1", k).broadcast_to([P, P]), raw_b[:, 1, k, :],
                                        start=(k == 0), stop=(k == C - 1))
            last.then_inc(bvp_done, 1)
            pe.wait_ge(film_in[0], 16)
            pe.wait_ge(film_in[1], 16)
            for k in range(C):
                for i in range(4):
                    last = nc.tensor.matmul(ps_g[0][NB * i:NB * (i + 1), :], cond[:, k, :],
                                            film_b[:, i // 2, k, (i % 2) * D:(i % 2 + 1) * D],
                                            start=(k == 0), stop=(k == C - 1))
            last.then_inc(film1_done, 1)
            pe.wait_ge(film1_copied, 1)
            pe.wait_ge(h1_ready, NB)
            for c in range(C):
                last = nc.tensor.transpose(ps_r[:, c * P:(c + 1) * P], fv1[:, c * P:(c + 1) * P], ident[:])
            last.then_inc(film1_t, 1)

            pe.wait_ge(cb_made, 1)

            def norm_b(g, b, pos):
                norm_t(g, b, pos, bg_full, bg_free, xnb, b, bxn)

            for b in range(GB):
                norm_b(-1, b, 12 + b)

            def qk_b(g, m, pos, which):
                i = pos % 2
                pe.wait_ge(bg_free[i], bank_uses(g, pos))
                for k in range(C):
                    n = slice(m * P, (m + 1) * P)
                    last = split_product(ps_g[i][:], wqk_hi[:, which, k, n], wqk_lo[:, which, k, n], hb_hi[:, k, :],
                                         hb_lo[:, k, :], k == 0, k == C - 1)
                last.then_inc(bg_full[i], 1)

            def values_b(g, b):
                tok = slice(b * P, (b + 1) * P)
                pe.wait_ge(bg_free[0], bank_uses(g, 8 + 2 * b))
                for k in range(C):
                    last = split_product(ps_g[0][:], hb_hi[:, k, tok], hb_lo[:, k, tok], wvp_hi[:, k, :],
                                         wvp_lo[:, k, :], k == 0, k == C - 1)
                last.then_inc(bg_full[0], 1)

            def attend_b(g, b):
                t = GB * g + b
                pe.wait_ge(bpt, t + 1)
                pe.wait_ge(bg_free[0], bank_uses(g, 8 + 2 * b) + 1)
                wait(pe, x2_ready, t - 1)
                nc.tensor.matmul(bank[6 + b % 2][:], ptb[:, b % 2, :], vb[:, b, :], start=True, stop=True)\
                    .then_inc(bpv, 1)

            def body_b(g, first, last):
                pe.wait_ge(bhi, GB * g + GB)
                pe.wait_ge(blo, GB * g + GB)
                if first:
                    pe.wait_ge(wqk_hi_made, 2)
                    pe.wait_ge(wqk_lo_made, 2)
                    pe.wait_ge(st1_made, 1)
                for m in range(C):
                    qk_b(g, m, 2 * m, 1)
                    qk_b(g, m, 2 * m + 1, 0)
                if first:
                    pe.wait_ge(wvp_hi_made, C)
                    pe.wait_ge(wvp_lo_made, C)
                values_b(g, 0)
                for b in range(GB):
                    t = GB * g + b
                    norm_b(g, b, 9 + 2 * b)
                    if b == 0:
                        pe.wait_ge(bg_free[0], bank_uses(g, 6) + 1)
                        pe.wait_ge(bg_free[1], bank_uses(g, 7) + 1)
                    wait(pe, bexp, t - 1)
                    tok = slice(b * P, (b + 1) * P)
                    for k in range(C):
                        s = nc.tensor.matmul(ps_s[b % 2][:, 0:P], qb[:, k, tok], kb[:, k, tok], start=(k == 0),
                                             stop=(k == C - 1))
                    s.then_inc(bs_done, 1)
                    if b < GB - 1:
                        values_b(g, b + 1)
                    if b > 0:
                        attend_b(g, b - 1)
                    pe.wait_ge(bexp, t + 1)
                    wait(pe, bpt, t - 1)
                    nc.tensor.transpose(ps_t[b % 2][:, 0:P], pb[:, b % 2, :], ident[:]).then_inc(btp, 1)
                attend_b(g, GB - 1)

            groups(pe, body_b)

            def norm_c(g, b):
                t = GB * g + b
                pe.wait_ge(cxn, t + 1)
                wait(pe, ct_free_act if b % 2 else ct_free_dve, 2 * g + b // 2)
                for c in range(C):
                    last = nc.tensor.transpose(bank[6 + b % 2][:, c * P:(c + 1) * P], xnc[:, b, c * P:(c + 1) * P],
                                               ident[:])
                last.then_inc(ct_full, 1)

            pe.wait_ge(bg_free[0], bank_uses(NG - 1, 14) + 1)
            pe.wait_ge(bg_free[1], bank_uses(NG - 1, 15) + 1)

            def up(g, f):
                n = FT * g + f
                wait(pe, gelu_done, n - 1)
                for k in range(C):
                    last = split_product(bank[f % 2][:], w1_hi[:, k, f * P:(f + 1) * P], w1_lo[:, k, f * P:(f + 1) * P],
                                         hc_hi[:, k, :], hc_lo[:, k, :], k == 0, k == C - 1)
                last.then_inc(up_done, 1)

            def down(g, f, first):
                n = FT * g + f
                if first and f % 2 == 0:
                    pe.wait_ge(w2_hi_made, f // 2 + 1)
                    pe.wait_ge(w2_lo_made, f // 2 + 1)
                pe.wait_ge(g_hi_ready, n + 1)
                pe.wait_ge(g_lo_ready, n + 1)
                if f == 0:
                    wait(pe, y_ready, GB * g)
                for b in range(GB):
                    tok = slice(b * P, (b + 1) * P)
                    last = split_product(bank[2 + b][:], g_hi[:, f % (LAG + 1), tok], g_lo[:, f % (LAG + 1), tok],
                                         w2_hi[:, f, :], w2_lo[:, f, :], f == 0, f == FT - 1)
                    if f == FT - 1:
                        last.then_inc(acc_done, 1)
                if f < FT - 1:
                    last.then_inc(down_done, 1)

            def body_c(g, first, last):
                if first:
                    pe.wait_ge(blo, NB + GB)
                wait(pe, clo, GB * g)
                if first:
                    pe.wait_ge(w1_hi_made, C)
                    pe.wait_ge(w1_lo_made, C)
                for f in range(FT):
                    up(g, f)
                    if f >= LAG:
                        down(g, f - LAG, first)
                if first:
                    pe.wait_ge(x2_ready, NB)
                for f in range(FT - LAG, FT):
                    if not last and f < FT - LAG + 2:
                        for b in range(2):
                            norm_c(g, 2 * (f - (FT - LAG)) + b)
                    down(g, f, first)

            groups(pe, body_c)

        @block.scalar
        def _(act):
            act.wait_ge(film0_done, 1)
            nc.scalar.activation(fv0[:], ps_s[0][0:2 * NB, :], ACT.Identity).then_inc(film0_copied, 1)
            wa_dst = [wa_hi[:, :, D:2 * D], wa_hi[:, :, 0:D], wa_hi[:, :, 2 * D:3 * D], wp_hi[:]]

            def split_wa(i):
                act.wait_ge(stage_in[i % 2], 16 * (i // 2 + 1))
                nc.scalar.activation(wa_dst[i], stage_a[:, i % 2], ACT.Identity).then_inc(wa_hi_made, 1)

            split_wa(0)

            def affine(src, dst, b, free, st=cur_st):
                for c in range(C):
                    last = nc.scalar.activation(dst[:, c, :], src[:, c * P:(c + 1) * P], ACT.Identity,
                                                bias=st[:, b, C + c:C + c + 1], scale=st[:, b, c:c + 1])
                last.then_inc(free, 1)

            def scale_norm(g, b, pos, full, free, cur, low, buf):
                i, n = pos % 2, bank_uses(g, pos)
                act.wait_ge(cur, g + 2)
                act.wait_ge(full[i], n + 1)
                wait(act, low, GB * (g + 1) + b - 1)
                affine(ps_g[i], buf[:, b % 2], b, free[i])

            def round_norm(g, b, pos, free, high, buf, dst):
                act.wait_ge(free[pos % 2], bank_uses(g, pos) + 1)
                nc.scalar.activation(dst[:, :, b * P:(b + 1) * P], buf[:, b % 2], ACT.Identity).then_inc(high, 1)

            def norm_split(g, b, pos, full, free, cur, low, high, buf, dst):
                scale_norm(g, b, pos, full, free, cur, low, buf)
                round_norm(g, b, pos, free, high, buf, dst)

            def norm_a(g, b, pos):
                norm_split(g, b, pos, g_full, g_free, cur_ready, lo_ready, hi_ready, hf, h_hi)

            for b in range(GB):
                norm_a(-1, b, 12 + b)
                if b == 1:
                    split_wa(1)
            split_wa(2)
            split_wa(3)

            def keys(g, m):
                if isinstance(g, int) and g == 0 and m == 0:
                    act.wait_ge(k_zeroed, 1)
                act.wait_ge(g_full[0], bank_uses(g, 2 * m) + 1)
                for j in range(HM):
                    q = slice(j * HD, (j + 1) * HD)
                    c = COL["bk0"] + m
                    last = nc.scalar.activation(k_diag[q, m, :, j, :], ps_g[0][q, :].rearrange("p (b t) -> p b t", b=GB),
                                                ACT.Identity, bias=cols[q, c:c + 1])
                last.then_inc(g_free[0], 1)

            def exps(g, u):
                b, m = u // C, u % C
                act.wait_ge(max_done, UNITS * g + u + 1)
                wait(act, tp_done, UNITS * g + u - 1)
                for j in range(HM):
                    h = m * HM + j
                    last = nc.scalar.activation(pa[:, u % 2, j, :], ps_s[u % 2][:, j * P:(j + 1) * P], ACT.Exp,
                                                bias=neg_max[:, u % 2, j:j + 1], accum_out=sums[:, b % 2, h:h + 1])
                last.then_inc(exp_done, 1)

            def copy_r(g, b):
                t = GB * g + b
                act.wait_ge(r_done, t + 1)
                wait(act, o_scaled, t)
                nc.scalar.activation(rs[:], ps_r[:], ACT.Copy, scale=INV_SQRT_D).then_inc(r_copied, 1)

            def round_o(g, b):
                t = GB * g + b
                act.wait_ge(o_scaled, t + 1)
                wait(act, proj_done, t - 1)
                nc.scalar.activation(o_hi[:, b % 2], of[:], ACT.Identity).then_inc(o_hi_ready, 1)

            def body(g, first, last):
                keys(g, 0)
                if not first:
                    copy_r(g - 1, GB - 1)
                    round_o(g - 1, GB - 1)
                for m in range(1, C):
                    keys(g, m)
                exps(g, 0)
                for u in range(UNITS):
                    b, m = u // C, u % C
                    if u + 1 < UNITS:
                        exps(g, u + 1)
                    if m == 0 and b > 0:
                        copy_r(g, b - 1)
                    if m == 1 and b > 0:
                        round_o(g, b - 1)
                    if m == 2 and not last:
                        norm_a(g, b, [10, 12, 14, 15][b])

            groups(act, body)
            copy_r(NG - 1, GB - 1)
            round_o(NG - 1, GB - 1)

            def squares(g, b, x, x_sem, sum_sem, var_sem):
                act.wait_ge(x_sem[b % 2], loaded(2 * g + b // 2 + 1))
                wait(act, var_sem, GB * g + b - 1)
                nc.scalar.activation(junk[:], x[:, b % 2], ACT.Square, accum_out=ssq[:, b % 2:b % 2 + 1])\
                    .then_inc(sum_sem, 1)

            def squares_b(g, b):
                wait(act, bssq, GB * g + b)
                squares(g, b, xb, bx_in, bssq, bvar)

            act.wait_ge(s_done, UNITS * NG)
            for i in range(2):
                act.wait_ge(raw_in[2 + i], 16)
                nc.scalar.activation(wqk_hi[:, i], raw_b[:, 2 + i], ACT.Identity).then_inc(wqk_hi_made, 1)
            for i in range(C):
                act.wait_ge(wvp_done, i + 1)
                nc.scalar.activation(wvp_hi[:, i], bank[2 + i][:], ACT.Identity).then_inc(wvp_hi_made, 1)
                squares_b(0, i)
            act.wait_ge(film1_done, 1)
            act.wait_ge(xr_ready, NB)
            nc.scalar.activation(fv1[:], ps_g[0][:], ACT.Identity).then_inc(film1_copied, 1)

            def norm_b(g, b, pos):
                norm_split(g, b, pos, bg_full, bg_free, bcur, blo, bhi, hfb, hb_hi)

            for b in range(GB):
                norm_b(-1, b, 12 + b)

            def copy_vb(g, b):
                act.wait_ge(bg_full[0], bank_uses(g, 8 + 2 * b) + 1)
                nc.scalar.activation(vb[:, b, :], ps_g[0][:], ACT.Identity).then_inc(bg_free[0], 1)

            def split_w1(i):
                act.wait_ge(w1_in[i % 2], 16 * (i // 2 + 1))
                nc.scalar.activation(w1_hi[:, i, :], stage_w1[:, i % 2], ACT.Identity).then_inc(w1_hi_made, 1)

            def body_b(g, first, last):
                for m in range(C):
                    act.wait_ge(bg_full[0], bank_uses(g, 2 * m) + 1)
                    nc.scalar.activation(kb[:, m, :], ps_g[0][:], ACT.Identity, bias=col("bk1", m))\
                        .then_inc(bg_free[0], 1)
                    squares_b(g + 1, m)
                copy_vb(g, 0)
                for b in range(GB):
                    t = GB * g + b
                    scale_norm(g, b, 9 + 2 * b, bg_full, bg_free, bcur, blo, hfb)
                    act.wait_ge(bmax, t + 1)
                    wait(act, btp, t - 1)
                    nc.scalar.activation(pb[:, b % 2, :], ps_s[b % 2][:, 0:P], ACT.Exp, scale=INV_SQRT_D,
                                         bias=neg_max[:, b % 2, 1:2], accum_out=sums[:, b % 2, 0:1]).then_inc(bexp, 1)
                    round_norm(g, b, 9 + 2 * b, bg_free, bhi, hfb, hb_hi)
                    if b < GB - 1:
                        copy_vb(g, b + 1)
                    if first and b >= 2:
                        act.wait_ge(wqk_lo_made, 2)
                        split_w1(b - 2)
                    if last and b < 2:
                        split_w1(b + 2)

            groups(act, body_b)

            def squares_c(g, b):
                wait(act, cssq, GB * g + b)
                squares(g, b, xc, cx_in, cssq, cvar)

            def norm_c(g, b):
                t = GB * g + b
                act.wait_ge(ccur, g + 1)
                act.wait_ge(ct_full, t + 1)
                wait(act, clo, t - 1)
                affine(bank[7], hfc_act, b, ct_free_act)
                act.wait_ge(ct_free_act, 2 * g + b // 2 + 1)
                nc.scalar.activation(hc_hi[:, :, b * P:(b + 1) * P], hfc_act[:], ACT.Identity).then_inc(chi_act, 1)

            def body_c(g, first, last):
                for f in range(FT):
                    n = FT * g + f
                    if first and f < FT // 2:
                        act.wait_ge(w2_in[f % 2], 16 * (f // 2 + 1))
                        nc.scalar.activation(w2_hi[:, 2 * f:2 * f + 2, :], stage_w2[f % 2][:], ACT.Identity)\
                            .then_inc(w2_hi_made, 1)
                    act.wait_ge(up_done, n + 1)
                    wait(act, g_lo_ready, n - 1)
                    nc.scalar.activation(gf[f % 2][:], bank[f % 2][:], ACT.Gelu, bias=cols[:, B1_COL + f:B1_COL + f + 1])\
                        .then_inc(gelu_done, 1)
                    if not last and f % 2 == 1 and 3 <= f < 3 + 2 * GB:
                        squares_c(g, (f - 3) // 2)
                if not last:
                    norm_c(g, 1)
                    norm_c(g, 3)

            groups(act, body_c)

        @block.vector
        def _(dve):
            step = [0]

            def then(instruction):
                step[0] += 1
                instruction.then_inc(dve_step, 1)
                dve.wait_ge(dve_step, step[0])

            def low_half(dst, whole, high):
                return nc.vector.tensor_tensor(dst, whole, high.bitcast(F32), ALU.subtract)

            def table(st, c0):
                return st[:, :, c0:c0 + C].rearrange("p b c -> p c b")

            def mean_var(g, b):
                dve.wait_ge(x_in[b], loaded(g + 1))
                wait(dve, xn_ready, GB * g + b - 1)
                wait(dve, var_ready, 2 * (GB * g + b))
                nc.vector.bn_stats(stats[:], xa[:, b]).then_inc(bn_done, 1)
                wait_apart(dve, bn_done, GB * g + b + 1, dve_passed)
                nc.vector.bn_aggr(mv1[:, b % 2], stats[:]).then_inc(var_ready, 1)
                dve.wait_ge(var_ready, 2 * (GB * g + b) + 1)
                nc.vector.tensor_scalar(ve1[:, b % 2:b % 2 + 1], mv1[:, b % 2, 1:2], EPS_LN, None, ALU.add)\
                    .then_inc(var_ready, 1)

            for b in range(3):
                mean_var(0, b)
            dve.wait_ge(film0_t, 1)
            dve.wait_ge(consts_in, 32)
            ft = ps_s[1][:, 0:2 * NB * C].rearrange("p (c v b) -> p c v b", c=C, v=2)
            then(nc.vector.tensor_tensor(tmp_a[:], ft[:, :, 0, :], col_wide("bg"), ALU.add))
            then(nc.vector.tensor_tensor(tmp_b[:], ft[:, :, 1, :], col_wide("bb"), ALU.add))
            nc.vector.tensor_tensor(st_flat[:, 0:C, :], tmp_a[:], col_wide("ln_g"), ALU.mult)
            then(nc.vector.tensor_tensor(st_flat[:, C:2 * C, :], tmp_a[:], col_wide("ln_b"), ALU.mult))
            then(nc.vector.tensor_tensor(st_flat[:, C:2 * C, :], st_flat[:, C:2 * C, :], tmp_b[:], ALU.add))
            nc.vector.tensor_copy(st_ln[:], st_flat[:].rearrange("p v b -> p b v")).then_inc(st0_made, 1)

            wa_dst = [wa_lo[:, :, D:2 * D], wa_lo[:, :, 0:D], wa_lo[:, :, 2 * D:3 * D], wp_lo[:]]
            wa_src = [wa_hi[:, :, D:2 * D], wa_hi[:, :, 0:D], wa_hi[:, :, 2 * D:3 * D], wp_hi[:]]

            def split_wa(i):
                dve.wait_ge(wa_hi_made, i + 1)
                low_half(wa_dst[i], stage_a[:, i % 2], wa_src[i]).then_inc(wa_lo_made, 1)

            split_wa(0)
            mean_var(0, 3)

            def norm_low(t, b, high, low, dst, buf, src):
                dve.wait_ge(high, t + 1)
                tok = slice(b * P, (b + 1) * P)
                low_half(dst[:, :, tok], buf[:, b % 2], src[:, :, tok]).then_inc(low, 1)

            for b in range(GB):
                norm_low(b, b, hi_ready, lo_ready, h_lo, hf, h_hi)
                if b == 1:
                    split_wa(1)
            dve.wait_ge(st0_t, 1)
            for i in range(2):
                nc.vector.tensor_copy(st_rows[:, i * D:(i + 1) * D], ps_t[i][0:NB, :]).then_inc(st_rows_made, 1)
            split_wa(2)
            split_wa(3)

            def row_max(g, u):
                dve.wait_ge(s_done, UNITS * g + u + 1)
                nc.vector.tensor_reduce(neg_max[:, u % 2, :], ps_s[u % 2][:].rearrange("p (h k) -> p h k", h=HM), AX.X,
                                        ALU.max, negate=True).then_inc(max_done, 1)

            def copy_v(g, b, pos):
                i = pos % 2
                dve.wait_ge(g_full[i], bank_uses(g, pos) + 1)
                nc.vector.tensor_tensor(va[:, b, :], ps_g[i][:], bv0[:], ALU.add).then_inc(g_free[i], 1)

            def copy_pt(g, u):
                dve.wait_ge(tp_done, UNITS * g + u + 1)
                wait(dve, pv_done, UNITS * g + u - 1)
                nc.vector.tensor_copy(pta[:, u % 2].rearrange("p h q -> p (h q)"), ps_t[u % 2][:]).then_inc(pt_copied, 1)

            def recip(g, b):
                t = GB * g + b
                wait(dve, r_copied, t)
                dve.wait_ge(exp_done, UNITS * g + C * b + C)
                nc.vector.reciprocal(rec[:], sums[:, b % 2, :]).then_inc(rec_made, 1)
                dve.wait_ge(rec_made, t + 1)
                nc.vector.tensor_copy(recx[:], rec[:].unsqueeze(2).broadcast_to([P, HEADS, HD]))\
                    .then_inc(rec_ready, 1)

            def scale_o(g, b):
                t = GB * g + b
                dve.wait_ge(r_copied, t + 1)
                wait(dve, o_lo_ready, t)
                dve.wait_ge(pv_done, UNITS * g + C * b + C)
                nc.vector.tensor_tensor(of[:].rearrange("p c t -> p (c t)"), ps_o[:], rs[:], ALU.mult)\
                    .then_inc(o_scaled, 1)

            def low_o(g, b):
                t = GB * g + b
                dve.wait_ge(o_hi_ready, t + 1)
                low_half(o_lo[:, b % 2], of[:], o_hi[:, b % 2]).then_inc(o_lo_ready, 1)

            def residual(g, b):
                t = GB * g + b
                dve.wait_ge(proj_done, t + 1)
                dve.wait_ge(xr_ready, t + 1)
                wait(dve, x1_out[b], 16 * g)
                nc.vector.tensor_tensor(h1[:, b], ps_r[:], xra[:, b % 2], ALU.add).then_inc(h1_ready, 1)

            def mean_var2(g):
                dve.wait_ge(h1_ready, GB * g + GB)
                wait(dve, ln2_shifted, GB * g)
                for b in range(GB):
                    nc.vector.bn_stats(stats2[:, b], h1[:, b]).then_inc(bn2_done, 1)
                for b in range(GB):
                    wait_apart(dve, bn2_done, 2 * GB * g + GB + b, dve_passed)
                    nc.vector.bn_aggr(mv2[:, b], stats2[:, b]).then_inc(bn2_done, 1)
                dve.wait_ge(bn2_done, 2 * GB * g + 2 * GB)
                nc.vector.tensor_scalar(ve2[:], mv2[:, :, 1], EPS_LN, None, ALU.add).then_inc(var2_ready, 1)

            def norm2(g, b):
                dve.wait_ge(rows_ld[b % 2], loaded(2 * g + b // 2 + 1))
                nc.vector.scalar_tensor_tensor(nb[:, b], h1[:, b], mv2[:, b, 0:1], rows[:, b % 2, 0:D], ALU.subtract,
                                               ALU.mult).then_inc(ln2_normed, 1)

            def add_x1(g, b):
                dve.wait_ge(rstd2_ready, g + 1)
                dve.wait_ge(ln2_shifted, GB * g + b + 1)
                nc.vector.scalar_tensor_tensor(h1[:, b], nb[:, b], rstd2[:, b:b + 1], h1[:, b], ALU.mult, ALU.add)\
                    .then_inc(x1_ready, 1)

            def body(g, first, last):
                for m in range(C):
                    if m == 0 and not first:
                        scale_o(g - 1, GB - 1)
                    dve.wait_ge(g_full[1], bank_uses(g, 2 * m + 1) + 1)
                    nc.vector.tensor_scalar(qa[:, m, :], ps_g[1][:], col("bq0", m), None, ALU.add).then_inc(g_free[1], 1)
                    if m >= 2:
                        row_max(g, m - 2)
                    if m == 0 and not first:
                        low_o(g - 1, GB - 1)
                    if not last:
                        mean_var(g + 1, m)
                    if not first:
                        if m == 1:
                            residual(g - 1, GB - 1)
                            mean_var2(g - 1)
                            norm2(g - 1, 0)
                            norm2(g - 1, 1)
                        if m == 2:
                            add_x1(g - 1, 0)
                            add_x1(g - 1, 1)
                            norm2(g - 1, 2)
                        if m == 3:
                            norm2(g - 1, 3)
                            add_x1(g - 1, 2)
                for u in range(UNITS):
                    b, m = u // C, u % C
                    if m == 0:
                        copy_v(g, b, 8 if b == 0 else 7 + 2 * b)
                    copy_pt(g, u)
                    if u + 2 < UNITS:
                        row_max(g, u + 2)
                    if m == 0 and b > 0:
                        scale_o(g, b - 1)
                    if m == 1 and b > 0:
                        low_o(g, b - 1)
                    if m == 3:
                        if not last:
                            norm_low(GB * (g + 1) + b, b, hi_ready, lo_ready, h_lo, hf, h_hi)
                        recip(g, b)
                        if b > 0:
                            residual(g, b - 1)
                    if u == 1 and not first:
                        add_x1(g - 1, 3)

            groups(dve, body)
            scale_o(NG - 1, GB - 1)
            low_o(NG - 1, GB - 1)
            residual(NG - 1, GB - 1)
            mean_var2(NG - 1)

            def mean_square(g, b, sum_sem, xn_sem, var_sem):
                dve.wait_ge(sum_sem, GB * g + b + 1)
                wait(dve, xn_sem, GB * g + b - 1)
                nc.vector.tensor_scalar(ve1[:, b % 2:b % 2 + 1], ssq[:, b % 2:b % 2 + 1], 1.0 / D, EPS_RMS, ALU.mult,
                                        ALU.add).then_inc(var_sem, 1)

            for i in range(2):
                dve.wait_ge(wqk_hi_made, i + 1)
                low_half(wqk_lo[:, i], raw_b[:, 2 + i], wqk_hi[:, i]).then_inc(wqk_lo_made, 1)
            for i in range(C):
                dve.wait_ge(wvp_hi_made, i + 1)
                low_half(wvp_lo[:, i], bank[2 + i][:], wvp_hi[:, i]).then_inc(wvp_lo_made, 1)
                mean_square(0, i, bssq, bxn, bvar)
                if i == 1:
                    norm2(NG - 1, 0)
                    norm2(NG - 1, 1)
            dve.wait_ge(rows_in, 64)
            dve.wait_ge(bvp_done, 1)
            nc.vector.tensor_tensor(cb1[:], ps_g[1][:], cb1[:], ALU.add).then_inc(cb_made, 1)
            dve.wait_ge(film1_t, 1)
            fl = ps_r[:].rearrange("p (c v b) -> p c v b", c=C, v=4)
            for i, (st, n) in enumerate(((st_f1, "1"), (st_f2, "2"))):
                then(nc.vector.tensor_tensor(tmp_a[:], fl[:, :, 2 * i, :], col_wide(f"f{n}scale"), ALU.add))
                then(nc.vector.tensor_scalar(tmp_a[:], tmp_a[:], 1.0, None, ALU.add))
                nc.vector.tensor_tensor(table(st, 0), tmp_a[:], col_wide(f"norm{n}"), ALU.mult)
                then(nc.vector.tensor_tensor(table(st, C), fl[:, :, 2 * i + 1, :], col_wide(f"f{n}shift"), ALU.add))
            nc.vector.memset(tmp_b[:, 0, 0:1], 0.0).then_inc(st1_made, 1)
            for b in range(2):
                add_x1(NG - 1, b)
            for b in range(2, GB):
                norm2(NG - 1, b)

            def norm_low_b(g, b):
                norm_low(GB * g + b, b, bhi, blo, hb_lo, hfb, hb_hi)

            for b in range(GB):
                norm_low_b(0, b)
            for b in range(2, GB):
                add_x1(NG - 1, b)

            def residual_b(g, b):
                t = GB * g + b
                dve.wait_ge(bpv, t + 1)
                dve.wait_ge(bxr, t + 1)
                nc.vector.scalar_tensor_tensor(xrb[:, b], bank[6 + b % 2][:], ssq_rec[:, b % 2:b % 2 + 1], xrb[:, b],
                                               ALU.mult, ALU.add).then_inc(x2_ready, 1)

            def split_w1(i):
                dve.wait_ge(w1_hi_made, i + 1)
                low_half(w1_lo[:, i, :], stage_w1[:, i % 2], w1_hi[:, i, :]).then_inc(w1_lo_made, 1)

            def body_b(g, first, last):
                for m in range(C):
                    dve.wait_ge(bg_full[1], bank_uses(g, 2 * m + 1) + 1)
                    nc.vector.tensor_scalar(qb[:, m, :], ps_g[1][:], col("bq1", m), None, ALU.add)\
                        .then_inc(bg_free[1], 1)
                    mean_square(g + 1, m, bssq, bxn, bvar)
                for b in range(GB):
                    t = GB * g + b
                    dve.wait_ge(bs_done, t + 1)
                    nc.vector.tensor_reduce(neg_max[:, b % 2, 0:1], ps_s[b % 2][:, 0:P], AX.X, ALU.max, negate=True)\
                        .then_inc(braw, 1)
                    dve.wait_ge(braw, t + 1)
                    nc.vector.tensor_scalar(neg_max[:, b % 2, 1:2], neg_max[:, b % 2, 0:1], INV_SQRT_D, None, ALU.mult)\
                        .then_inc(bmax, 1)
                    if b < GB - 1:
                        norm_low_b(g + 1, b)
                    dve.wait_ge(btp, t + 1)
                    wait(dve, bpv, t - 1)
                    nc.vector.tensor_copy(ptb[:, b % 2, :], ps_t[b % 2][:, 0:P]).then_inc(bpt, 1)
                    if b == GB - 1:
                        norm_low_b(g + 1, b)
                    wait(dve, x2_ready, t - 1)
                    nc.vector.reciprocal(ssq_rec[:, b % 2:b % 2 + 1], sums[:, b % 2, 0:1]).then_inc(brec, 1)
                    if b > 0:
                        dve.wait_ge(brec, t)
                        residual_b(g, b - 1)
                    if first and b >= 2:
                        split_w1(b - 2)
                    if last and b < 2:
                        split_w1(b + 2)
                dve.wait_ge(brec, GB * g + GB)
                residual_b(g, GB - 1)

            groups(dve, body_b)

            def norm_c(g, b):
                t = GB * g + b
                tok = slice(b * P, (b + 1) * P)
                if b % 2 == 0:
                    dve.wait_ge(ccur, g + 1)
                    dve.wait_ge(ct_full, t + 1)
                    wait(dve, clo, t - 1)
                    for c in range(C):
                        last = nc.vector.tensor_scalar(hfc_dve[:, c, :], bank[6][:, c * P:(c + 1) * P],
                                                       cur_st[:, b, c:c + 1], cur_st[:, b, C + c:C + c + 1], ALU.mult,
                                                       ALU.add)
                    last.then_inc(ct_free_dve, 1)
                    dve.wait_ge(ct_free_dve, 2 * g + b // 2 + 1)
                    nc.vector.tensor_copy(hc_hi[:, :, tok], hfc_dve[:]).then_inc(chi_dve, 1)
                    dve.wait_ge(chi_dve, 2 * g + b // 2 + 1)
                    low_half(hc_lo[:, :, tok], hfc_dve[:], hc_hi[:, :, tok]).then_inc(clo, 1)
                else:
                    dve.wait_ge(chi_act, 2 * g + b // 2 + 1)
                    low_half(hc_lo[:, :, tok], hfc_act[:], hc_hi[:, :, tok]).then_inc(clo, 1)

            def body_c(g, first, last):
                for f in range(FT):
                    n = FT * g + f
                    if first and f < FT // 2:
                        dve.wait_ge(w2_hi_made, f + 1)
                        low_half(w2_lo[:, 2 * f:2 * f + 2, :], stage_w2[f % 2][:], w2_hi[:, 2 * f:2 * f + 2, :])\
                            .then_inc(w2_lo_made, 1)
                    r = f % (LAG + 1)
                    dve.wait_ge(gelu_done, n + 1)
                    if f >= LAG + 1:
                        dve.wait_ge(down_done, (FT - 1) * g + f - LAG)
                    elif f < LAG:
                        wait(dve, down_done, (FT - 1) * (g - 1) + FT - LAG + f)
                    else:
                        wait(dve, acc_done, GB * g)
                    nc.vector.tensor_copy(g_hi[:, r, :], gf[f % 2][:]).then_inc(g_hi_ready, 1)
                    dve.wait_ge(g_hi_ready, n + 1)
                    low_half(g_lo[:, r, :], gf[f % 2][:], g_hi[:, r, :]).then_inc(g_lo_ready, 1)
                    if not last and f % 2 == 0 and 4 <= f < 4 + 2 * GB:
                        mean_square(g, (f - 4) // 2, cssq, cxn, cvar)
                if not last:
                    for b in range(GB):
                        norm_c(g, b)
                for b in range(GB):
                    t = GB * g + b
                    dve.wait_ge(acc_done, t + 1)
                    dve.wait_ge(cxr, t + 1)
                    nc.vector.tensor_tensor(xrc[:, b], bank[2 + b][:], xrc[:, b], ALU.add).then_inc(y_ready, 1)

            groups(dve, body_c)

        @block.gpsimd
        def _(pool):
            nc.gpsimd.memset(ident[:], 0.0).then_inc(consts_made, 1)
            nc.gpsimd.memset(neg_half[:], -0.5).then_inc(consts_made, 1)
            pool.wait_ge(consts_made, 2)
            nc.gpsimd.affine_select(out=ident[:], in_=ident[:], compare_op=ALU.not_equal, fill=1.0, base=0,
                                    pattern=[[-1, P]], channel_multiplier=1).then_inc(consts_made, 1)

            def scales(g, table, cur, used, row=None):
                wait(pool, used, GB * g)
                nc.gpsimd.tensor_copy(cur_st[:], table[:, bass.ds(GB * g if row is None else row, GB), :])\
                    .then_inc(cur, 1)

            def norm_a(g, b):
                t = GB * g + b
                i = b % 2
                pool.wait_ge(var_ready, 2 * t + 2)
                nc.gpsimd.tensor_tensor(rstd1[:, i:i + 1], ve1[:, i:i + 1], neg_half[:, 0:1], ALU.pow)\
                    .then_inc(rstd_ready, 1)
                wait_apart(pool, rstd_ready, t + 1, pool_passed)
                nc.gpsimd.tensor_scalar(xa[:, b], xa[:, b], mv1[:, i, 0:1], rstd1[:, i:i + 1], ALU.subtract,
                                        ALU.mult).then_inc(xn_ready, 1)

            norm_a(0, 0)
            norm_a(0, 1)
            norm_a(0, 2)
            pool.wait_ge(st0_made, 1)
            scales(0, st_ln, cur_ready, hi_ready)
            norm_a(0, 3)
            nc.gpsimd.memset(k_diag[:], 0.0).then_inc(k_zeroed, 1)
            pool.wait_ge(rows_in, 64)

            def add_bias(t, i, x, row, x_sem, count, ready):
                pool.wait_ge(x_sem, count)
                nc.gpsimd.tensor_tensor(x[:, i], x[:, i], row[:], ALU.add).then_inc(ready, 1)

            def finish(g, all_four=True):
                wait(pool, x1_ready, GB * g)
                pool.wait_ge(var2_ready, g + 1)
                nc.gpsimd.tensor_tensor(rstd2[:], ve2[:], neg_half[:], ALU.pow).then_inc(rstd2_ready, 1)
                shift(g, range(GB) if all_four else range(2))

            def shift(g, bs):
                for b in bs:
                    pool.wait_ge(ln2_normed, GB * g + b + 1)
                    nc.gpsimd.tensor_tensor(h1[:, b], h1[:, b], rows[:, b % 2, D:2 * D], ALU.add)\
                        .then_inc(ln2_shifted, 1)

            def body(g, first, last):
                if not last:
                    scales(g + 1, st_ln, cur_ready, hi_ready)
                    norm_a(g + 1, 0)
                    norm_a(g + 1, 1)
                if not first:
                    finish(g - 1)
                for b in range(GB):
                    if b >= 2 and not last:
                        norm_a(g + 1, b)
                    add_bias(GB * g + b, b % 2, xra, bp0, xr_in[b % 2], loaded(2 * g + b // 2 + 1), xr_ready)

            groups(pool, body)

            def norm_rms(g, b, x, xn, slot, var, ready, freed, freed_at, rr):
                t = GB * g + b
                i = b % 2
                pool.wait_ge(var, t + 1)
                nc.gpsimd.tensor_tensor(rstd1[:, i:i + 1], ve1[:, i:i + 1], neg_half[:, 0:1], ALU.pow).then_inc(rr, 1)
                wait(pool, freed, freed_at)
                wait_apart(pool, rr, t + 1, pool_passed)
                nc.gpsimd.tensor_scalar(xn[:, slot], x[:, i], rstd1[:, i:i + 1], None, ALU.mult).then_inc(ready, 1)

            def norm_b(g, b):
                norm_rms(g, b, xb, xnb, b, bvar, bxn, bhi, GB * (g - 1) + b + 1, brstd)

            for b in range(GB):
                norm_b(0, b)
            finish(NG - 1, all_four=False)
            pool.wait_ge(st1_made, 1)
            pool.wait_ge(cb_made, 1)
            scales(0, st_f1, bcur, bhi)
            shift(NG - 1, range(2, GB))

            def body_b(g, first, last):
                if last:
                    scales(NG, st_f2, bcur, bhi, 0)
                else:
                    scales(g + 1, st_f1, bcur, bhi)
                norm_b(g + 1, 0)
                norm_b(g + 1, 1)
                add_bias(GB * g, 0, xrb, cb1, bxr_in[0], loaded(g + 1), bxr)
                norm_b(g + 1, 2)
                add_bias(GB * g + 1, 1, xrb, cb1, bxr_in[1], loaded(g + 1), bxr)
                norm_b(g + 1, 3)
                for b in range(2, GB):
                    add_bias(GB * g + b, b, xrb, cb1, bxr_in[b], loaded(g + 1), bxr)

            groups(pool, body_b)

            def norm_c(g, b):
                norm_rms(g, b, xc, xnc, b, cvar, cxn, clo, GB * g, crstd)

            pool.wait_ge(blo, NB + GB)

            def body_c(g, first, last):
                for b in range(GB):
                    add_bias(GB * g + b, b, xrc, b2, cxr_in[b], loaded(g + 1), cxr)
                if not last:
                    scales(g, st_f2, ccur, clo, GB * g + GB)
                    for b in range(GB):
                        norm_c(g, b)

            groups(pool, body_c)


def kernel(**inputs):
    import numpy as np
    import concourse.bacc as bacc
    from concourse.bass_utils import run_bass_kernel_spmd as run

    a = {k: np.asarray(v) for k, v in inputs.items()}
    l0, l1 = "L0_cond_", "L1_cond_"

    def chunks(v):
        return v.reshape(-1, P).T

    qkv_b = a[l0 + "bqkv"].reshape(D, 3)
    f1b, f2b = a[l1 + "film1_b"], a[l1 + "film2_b"]
    vectors = {
        "ln_g": a[l0 + "ln_g"], "ln_b": a[l0 + "ln_b"], "bg": a[l0 + "bg"], "bb": a[l0 + "bb"],
        "bq0": qkv_b[:, 0], "bk0": qkv_b[:, 1], "norm1": a[l1 + "norm1_w"], "f1scale": f1b[:D], "f1shift": f1b[D:],
        "bq1": a[l1 + "q_b"], "bk1": a[l1 + "k_b"], "bv1": a[l1 + "v_b"], "norm2": a[l1 + "norm2_w"],
        "f2scale": f2b[:D], "f2shift": f2b[D:],
    }
    arrays = {
        "xt": a["x"].reshape(NB * P, D),
        "cond_t": a["cond_1024"].T,
        "cols_d": np.concatenate([chunks(vectors[n]) for n in COLS] + [chunks(a[l1 + "mlp_b1"])], axis=1),
        "bp0_d": a[l0 + "bp"],
        "bv0_d": qkv_b[:, 2],
        "pb1_d": a[l1 + "proj_b"],
        "b2_d": a[l1 + "mlp_b2"],
        "wg_t": a[l0 + "Wg"].T,
        "wb_t": a[l0 + "Wb"].T,
        "wqkv": a[l0 + "Wqkv"].reshape(D, 3, D).transpose(2, 1, 0).reshape(D, 3 * D),
        "wp0": a[l0 + "Wp"].T,
        "film1": a[l1 + "film1_w"],
        "film2": a[l1 + "film2_w"],
        "wq1": a[l1 + "q_w"],
        "wk1": a[l1 + "k_w"],
        "wv1_t": a[l1 + "v_w"].T,
        "wp1": a[l1 + "proj_w"],
        "w1": a[l1 + "mlp_w1"],
        "w2": a[l1 + "mlp_w2"],
    }
    nc = bacc.Bacc("TRN2", target_bir_lowering=False, num_devices=1)
    sent, args = {}, {}
    for name, v in arrays.items():
        sent[name + "_in"] = v = np.ascontiguousarray(v)
        args[name] = nc.dram_tensor(name + "_in", v.shape, mybir.dt.from_np(v.dtype), kind="ExternalInput").ap()
    out = nc.dram_tensor("out", (NB * P, D), F32, kind="ExternalOutput").ap()
    block_pair_kernel(nc, **args, out=out)
    r = run(nc, [sent], core_ids=[0])
    return r.results[0]["out"].reshape(NB, P, D)
```

```python
import concourse.bass as bass
from concourse import mybir
from contextlib import ExitStack

F32 = mybir.dt.float32
F32R = mybir.dt.float32r
BF16 = mybir.dt.bfloat16
ALU = mybir.AluOpType
ACT = mybir.ActivationFunctionType
AX = mybir.AxisListType

P = 128
D = 512
C = D // P
NB = 32
GB = 4
GT = GB * P
NG = NB // GB
HEADS = 16
HD = D // HEADS
HM = P // HD
UNITS = GB * C
FF = 4 * D
FT = FF // P
LAG = 3
EPS_LN, EPS_RMS = 1e-5, 1e-6
INV_SQRT_D = float(D) ** -0.5

COLS = ["ln_g", "ln_b", "bg", "bb", "bq0", "bk0", "norm1", "f1scale", "f1shift", "bq1", "bk1", "bv1",
        "norm2", "f2scale", "f2shift"]
COL = {n: i * C for i, n in enumerate(COLS)}
B1_COL = len(COLS) * C
N_COLS = B1_COL + FT


def wait(engine, sem, value):
    if isinstance(value, int) and value <= 0:
        return
    engine.wait_ge(sem, value)


def wait_apart(engine, sem, value, passed):
    wait(engine, sem, value)
    if not isinstance(value, int):
        engine.sem_inc(passed, 1)


def bank_uses(g, pos):
    return 8 * g + 2 + pos // 2


def bank_uses_b(g, pos):
    return 6 * g + 2 + pos // 2


def w2_pair(f):
    if f == 0:
        return 0
    return f - 2 if 3 <= f < FT // 2 + 2 else None


def w1_piece(i):
    half = i // 2 % 2
    return i // 4 * 2 + i % 2, slice(half * FF // 2, (half + 1) * FF // 2)


def groups(engine, body):
    body(0, True, False)
    with engine.Fori(1, NG - 1) as g:
        body(g, False, False)
    body(NG - 1, False, True)


def block_pair_kernel(nc, xt, cond_t, cols_d, bp0_d, bv0_d, pb1_d, b2_d, wg_t, wb_t, wqkv, wp0,
                      film1, film2, wq1_t, wk1_t, wv1_t, wp1, w1, w2, out):
    with ExitStack() as ctx:
        base = 16512
        kib = 1024

        def at(name, shape, dt, offset):
            return nc.alloc_sbuf_tensor_at(name, shape, dt, offset=base + offset)

        class Run:

            def __init__(self, offset):
                self.offset = offset

            def __call__(self, name, shape, dt=F32):
                n = 1
                for s in shape[1:]:
                    n *= s
                t = at(name, shape, dt, self.offset)
                self.offset += -(-n * (2 if dt == BF16 else 4) // 32) * 32
                return t

        keep = Run(0)
        ident = keep("ident", [P, P])
        cols = keep("cols", [P, N_COLS])
        cond = keep("cond", [P, C, NB])
        st_at = keep.offset
        st_ln = keep("st_ln", [P, NB, 2 * C])
        st_f1 = keep("st_f1", [P, NB, 2 * C])
        st_f2 = keep("st_f2", [P, NB, 2 * C])
        st_flat_at = keep.offset
        st_flat = keep("st_flat", [P, 2 * C, NB])
        junk = at("junk", [P, D], BF16, st_flat_at)
        tmp_at = keep.offset
        tmp_a = keep("tmp_a", [P, C, NB])
        tmp_b = keep("tmp_b", [P, C, NB])
        cur_st = keep("cur_st", [P, GB, 2 * C])
        neg_half = keep("neg_half", [P, GB])
        stats = keep("stats", [P, 6])
        mv1 = keep("mv1", [P, 2, 2])
        ve1 = keep("ve1", [P, 2])
        rstd1 = keep("rstd1", [P, 2])
        stats2 = keep("stats2", [P, GB, 6])
        mv2 = keep("mv2", [P, GB, 2])
        ve2 = keep("ve2", [P, GB])
        rstd2 = keep("rstd2", [P, GB])
        neg_max = keep("neg_max", [P, 2, HM])
        sums = keep("sums", [P, 2, HEADS])
        rec = keep("rec", [P, HEADS])
        ssq = keep("ssq", [P, 2])
        uc = keep("uc", [P, 2, C])
        uc_part = keep("uc_part", [P, 2, C])
        bqk = keep("bqk", [P, C])
        bqk_sum = keep("bqk_sum", [P, 2])
        inv_hd = keep("inv_hd", [P, 1])
        ssq_rec = keep("ssq_rec", [P, 2])
        rows_at = keep.offset
        bp0 = keep("bp0", [P, D])
        bv0 = keep("bv0", [P, D])
        cb1 = keep("cb1", [P, D])
        b2 = keep("b2", [P, D])
        R0 = -(-keep.offset // 64) * 64

        run = Run(R0)
        wa_hi = run("wa_hi", [P, C, 3 * D], F32R)
        wa_lo = run("wa_lo", [P, C, 3 * D], F32R)
        wp_hi = run("wp_hi", [P, C, D], F32R)
        wp_lo = run("wp_lo", [P, C, D], F32R)
        k_diag = run("k_diag", [P, C, GB, HM, P])
        h_hi = run("h_hi", [P, C, GT], F32R)
        h_lo = run("h_lo", [P, C, GT], F32R)
        work_at = run.offset
        xa = run("xa", [P, GB, D])
        hf = run("hf", [P, 2, C, P])
        qa = run("qa", [P, C, GT])
        va = run("va", [P, GB, D])
        pa_at = run.offset
        pa = run("pa", [P, 2, HM, P])
        pta = run("pta", [P, 2, HM, P])
        recx = run("recx", [P, HEADS, HD])
        rs = run("rs", [P, D])
        of = run("of", [P, C, P])
        o_hi = run("o_hi", [P, 2, C, P], F32R)
        o_lo = run("o_lo", [P, 2, C, P], F32R)
        xra = run("xra", [P, 2, D])
        stage_at = run.offset
        h1 = run("h1", [P, GB, D])
        rows = run("rows", [P, 2, 2 * D])
        nb = run("nb", [P, GB, D])
        assert base + run.offset <= 229344
        stage_a = at("stage_a", [P, 2, C, D], F32, stage_at)
        wgb = at("wgb", [P, 2, C, D], F32, R0 + 96 * kib)
        fv0 = at("fv0", [P, D], F32, pa_at)
        st_rows = at("st_rows", [NB, 2 * D], F32, pa_at + 4 * kib)

        raw_b = at("raw_b", [P, 4, C, D], F32, R0)
        film_b = at("film_b", [P, 2, C, 2 * D], F32, R0 + 32 * kib)
        run = Run(R0 + 64 * kib)
        g_hi_b = run("g_hi_b", [P, C, D], F32R)
        g_lo_b = run("g_lo_b", [P, C, D], F32R)
        wvp_hi = run("wvp_hi", [P, C, D], F32R)
        wvp_lo = run("wvp_lo", [P, C, D], F32R)
        hb_new = run("hb_new", [P, C, GT])
        hb = run("hb", [P, C, GT])
        assert run.offset == work_at
        tb = run("tb", [P, C, GT])
        rb = run("rb", [P, GT])
        vb_lo = run("vb_lo", [P, GB - 1, D], F32R)
        hb_at = work_at + 16 * kib
        assert run.offset <= hb_at
        run = Run(hb_at)
        hb_hi = run("hb_hi", [P, C, GT], F32R)
        hb_lo = run("hb_lo", [P, C, GT], F32R)
        xb = run("xb", [P, 2, D])
        xnb = run("xnb", [P, GB, D])
        vb_at = run.offset
        vb_hi = run("vb_hi", [P, GB, D], F32R)
        xrb_at = run.offset
        assert xrb_at <= stage_at
        xrb = run("xrb", [P, GB, D])
        stage_w1_at = run.offset
        stage_w1 = run("stage_w1", [P, 2, FF])
        assert base + run.offset <= 229344
        pb = at("pb", [P, 2, P], F32, tmp_at)
        ptb_hi = at("ptb_hi", [P, 2, P], F32R, rows_at)
        ptb_lo = at("ptb_lo", [P, 2, P], F32R, rows_at + kib)
        fv1 = at("fv1", [P, D], F32, vb_at)
        uc_rows = at("uc_rows", [P, D], F32, vb_at + 2 * kib)

        run = Run(R0)
        w1_hi = run("w1_hi", [P, C, FF], F32R)
        w1_lo = run("w1_lo", [P, C, FF], F32R)
        w2_hi = run("w2_hi", [P, FT, D], F32R)
        w2_lo = run("w2_lo", [P, FT, D], F32R)
        assert run.offset == hb_at
        hc_hi, hc_lo, xc, xnc = hb_hi, hb_lo, xb, xnb
        run = Run(vb_at)
        hfc_act = run("hfc_act", [P, C, P])
        stage_w2 = [None, run("stage_w2_1", [P, 2, D])]
        assert run.offset <= xrb_at
        xrc = at("xrc", [P, GB, D], F32, xrb_at)
        run = Run(stage_w1_at)
        g_hi = run("g_hi", [P, LAG + 1, GT], F32R)
        g_lo = run("g_lo", [P, LAG + 1, GT], F32R)
        stage_w2[0] = run("stage_w2_0", [P, 2, D])
        assert base + run.offset <= 229344
        run = Run(rows_at)
        hfc_dve = run("hfc_dve", [P, C, P])
        gf1 = run("gf1", [P, GT])
        gf0 = at("gf0", [P, GT], F32, st_at)
        gf = [gf0, gf1]

        bank = [ctx.enter_context(nc.psum_tensor(f"bank{i}", [P, D], F32)) for i in range(8)]
        ps_g = bank[0:2]
        ps_s = bank[2:4]
        ps_t = bank[4:6]
        ps_o = bank[6]
        ps_r = bank[7]

        st_dram = nc.dram_tensor("st_dram", (NB, 2 * D), F32).ap()
        x1_dram = nc.dram_tensor("x1_dram", (NB * P, D), F32).ap()
        x2_dram = nc.dram_tensor("x2_dram", (NB * P, D), F32).ap()

        def sem(name):
            return ctx.enter_context(nc.semaphore(name))

        consts_in, rows_in = sem("consts_in"), sem("rows_in")
        wgb_in = [sem("wgb_in0"), sem("wgb_in1")]
        consts_made = sem("consts_made")
        bn_done, bn2_done, rstd_ready, rstd2_ready = sem("bn_done"), sem("bn2_done"), sem("rstd_ready"), sem("rstd2_ready")
        ln2_normed, braw, brstd, crstd = sem("ln2_normed"), sem("braw"), sem("brstd"), sem("crstd")
        film0_done, film0_copied, film0_t = sem("film0_done"), sem("film0_copied"), sem("film0_t")
        st0_made, st0_t, st_rows_made = sem("st0_made"), sem("st0_t"), sem("st_rows_made")
        st_stored = sem("st_stored")
        stage_in = [sem("stage_in0"), sem("stage_in1")]
        wa_hi_made, wa_lo_made = sem("wa_hi_made"), sem("wa_lo_made")
        dve_step, passed = sem("dve_step"), sem("passed")
        x_in = [sem(f"x_in{b}") for b in range(GB)]
        xr_in = [sem("xr_in0"), sem("xr_in1")]
        rows_ld = [sem("rows_ld0"), sem("rows_ld1")]
        x1_out = [sem(f"x1_out{b}") for b in range(GB)]
        var_ready, xn_ready, cur_ready = sem("var_ready"), sem("xn_ready"), sem("cur_ready")
        hi_ready, lo_ready = sem("hi_ready"), sem("lo_ready")
        g_full = [sem("g_full0"), sem("g_full1")]
        g_free = [sem("g_free0"), sem("g_free1")]
        s_done, max_done, exp_done = sem("s_done"), sem("max_done"), sem("exp_done")
        tp_done, pt_copied, pv_done = sem("tp_done"), sem("pt_copied"), sem("pv_done")
        rec_made, rec_ready, r_done, r_copied = sem("rec_made"), sem("rec_ready"), sem("r_done"), sem("r_copied")
        o_scaled, o_hi_ready, o_lo_ready = sem("o_scaled"), sem("o_hi_ready"), sem("o_lo_ready")
        proj_done, xr_ready, h1_ready = sem("proj_done"), sem("xr_ready"), sem("h1_ready")
        var2_ready, ln2_shifted, x1_ready = sem("var2_ready"), sem("ln2_shifted"), sem("x1_ready")
        raw_in = [sem(f"raw_in{i}") for i in range(4)]
        film_in = [sem("film_in0"), sem("film_in1")]
        g_done, g_hi_made, g_lo_made = sem("g_done"), sem("g_hi_made"), sem("g_lo_made")
        uc_done, uc_copied, uc_t, uc_made = sem("uc_done"), sem("uc_copied"), sem("uc_t"), sem("uc_made")
        wvp_done, wvp_hi_made, wvp_lo_made = sem("wvp_done"), sem("wvp_hi_made"), sem("wvp_lo_made")
        bvp_done, film1_done, film1_copied = sem("bvp_done"), sem("film1_done"), sem("film1_copied")
        film1_t, st1_made, cb_made = sem("film1_t"), sem("st1_made"), sem("cb_made")
        bx_in = [sem("bx_in0"), sem("bx_in1")]
        bxr_in = [sem(f"bxr_in{b}") for b in range(GB)]
        x2_out = [sem(f"x2_out{b}") for b in range(GB)]
        bssq, bvar, bxn, bcur = sem("bssq"), sem("bvar"), sem("bxn"), sem("bcur")
        bhi, blo = sem("bhi"), sem("blo")
        bg_full = [sem("bg_full0"), sem("bg_full1")]
        bg_free = [sem("bg_free0"), sem("bg_free1")]
        bs_done, bmax, bexp, btp, bpt = sem("bs_done"), sem("bmax"), sem("bexp"), sem("btp"), sem("bpt")
        hb_copied, br_done, br_copied = sem("hb_copied"), sem("br_done"), sem("br_copied")
        bv_hi = sem("bv_hi")
        bpv, brec, bxr, x2_ready = sem("bpv"), sem("brec"), sem("bxr"), sem("x2_ready")
        w1_in = [sem("w1_in0"), sem("w1_in1")]
        w1_hi_made, w1_lo_made = sem("w1_hi_made"), sem("w1_lo_made")
        w2_in = [sem("w2_in0"), sem("w2_in1")]
        w2_hi_made, w2_lo_made = sem("w2_hi_made"), sem("w2_lo_made")
        cx_in = [sem("cx_in0"), sem("cx_in1")]
        cxr_in = [sem(f"cxr_in{b}") for b in range(GB)]
        y_out = [sem(f"y_out{b}") for b in range(GB)]
        cssq, cvar, cxn, ccur = sem("cssq"), sem("cvar"), sem("cxn"), sem("ccur")
        ct_full, ct_free_act, ct_free_dve = sem("ct_full"), sem("ct_free_act"), sem("ct_free_dve")
        chi_act, chi_dve, clo = sem("chi_act"), sem("chi_dve"), sem("clo")
        up_done, gelu_done = sem("up_done"), sem("gelu_done")
        g_hi_ready, g_lo_ready, down_done = sem("g_hi_ready"), sem("g_lo_ready"), sem("down_done")
        acc_done, cxr, y_ready = sem("acc_done"), sem("cxr"), sem("y_ready")

        block = ctx.enter_context(nc.Block())

        def tokens(dram, t):
            return dram[bass.ts(t, P), :]

        def weight(dram):
            return dram.rearrange("(k p) n -> p k n", p=P)

        def col(name, c):
            return cols[:, COL[name] + c:COL[name] + c + 1]

        def col_wide(name):
            return cols[:, COL[name]:COL[name] + C].unsqueeze(2).broadcast_to([P, C, NB])

        def loaded(n):
            return 16 * n

        @block.sync
        def _(sp):
            sp.dma_start(cols[:], cols_d).then_inc(consts_in, 16)
            sp.dma_start(cond[:], cond_t.rearrange("(k p) b -> p k b", p=P)).then_inc(consts_in, 16)
            for t in range(2):
                sp.dma_start(xa[:, t], tokens(xt, t)).then_inc(x_in[t], 16)
            for k in range(2):
                for i, w in enumerate((wg_t, wb_t)):
                    sp.dma_start(wgb[:, i, 2 * k:2 * k + 2], weight(w[2 * k * P:2 * (k + 1) * P, :])).then_inc(wgb_in[k], 16)
            for t in range(2, GB):
                sp.dma_start(xa[:, t], tokens(xt, t)).then_inc(x_in[t], 16)
            units = [wqkv[:, D:2 * D], wqkv[:, 0:D], wqkv[:, 2 * D:3 * D], wp0]
            for i in range(2):
                sp.dma_start(stage_a[:, i], weight(units[i])).then_inc(stage_in[i], 16)
            for row, src in ((bp0, bp0_d), (bv0, bv0_d), (cb1, pb1_d), (b2, b2_d)):
                sp.dma_start(row[:], src.partition_broadcast(P)).then_inc(rows_in, 16)
            for i in range(2, 4):
                sp.wait_ge(wa_lo_made, i - 1)
                sp.dma_start(stage_a[:, i % 2], weight(units[i])).then_inc(stage_in[i % 2], 16)
            sp.wait_ge(st_rows_made, 2)
            sp.dma_start(st_dram[:], st_rows[:]).then_inc(st_stored, 16)
            sp.wait_ge(st_stored, 16)

            def load_x(g, b):
                wait(sp, hi_ready, GB * (g - 1) + b + 1)
                sp.dma_start(xa[:, b], tokens(xt, GB * g + b)).then_inc(x_in[b], 16)

            def load_xr(g, b):
                wait(sp, h1_ready, GB * g + b - 1)
                sp.dma_start(xra[:, b % 2], tokens(xt, GB * g + b)).then_inc(xr_in[b % 2], 16)

            def load_rows(g, b):
                wait(sp, ln2_shifted, GB * g + max(b - 1, 0))
                sp.dma_start(rows[:, b % 2], st_dram[bass.ds(GB * g + b, 1), :].partition_broadcast(P))\
                    .then_inc(rows_ld[b % 2], 16)

            def store_x1(g, b):
                sp.wait_ge(x1_ready, GB * g + b + 1)
                sp.dma_start(tokens(x1_dram, GB * g + b), h1[:, b]).then_inc(x1_out[b], 16)

            def finish(g):
                for b in range(GB):
                    load_rows(g, b)
                for b in range(GB):
                    store_x1(g, b)

            def body(g, first, last):
                if not last:
                    for b in range(GB):
                        load_x(g + 1, b)
                load_xr(g, 0)
                load_xr(g, 1)
                if not first:
                    finish(g - 1)
                load_xr(g, 2)
                load_xr(g, 3)

            groups(sp, body)

            sp.wait_ge(g_free[1], bank_uses(NG - 1, 13) + 1)
            for i, w in enumerate((wv1_t, wp1, wq1_t, wk1_t)):
                sp.dma_start(raw_b[:, i], weight(w)).then_inc(raw_in[i], 16)
            sp.dma_start(film_b[:, 0], weight(film1)).then_inc(film_in[0], 16)
            sp.wait_ge(proj_done, NB)

            def load_bx(g, b, source=x1_dram, t=None):
                wait(sp, bxn, GB * g + b - 1)
                sp.dma_start(xb[:, b % 2], tokens(source, GB * g + b if t is None else t))\
                    .then_inc(bx_in[b % 2], 16)

            for b in range(GB):
                sp.wait_ge(x1_out[b], 16 * (NG - 1))
            load_bx(0, 0)
            load_bx(0, 1)
            load_rows(NG - 1, 0)
            load_rows(NG - 1, 1)
            sp.dma_start(film_b[:, 1], weight(film2)).then_inc(film_in[1], 16)
            load_bx(0, 2)
            load_bx(0, 3)
            load_rows(NG - 1, 2)
            load_rows(NG - 1, 3)
            load_bx(1, 0)
            load_bx(1, 1)
            for b in range(GB):
                store_x1(NG - 1, b)
            for b in range(GB):
                sp.wait_ge(x1_out[b], 16 * NG)

            def load_bxr(g, b):
                wait(sp, x2_out[b], 16 * g)
                sp.dma_start(xrb[:, b], tokens(x1_dram, GB * g + b)).then_inc(bxr_in[b], 16)

            def store_x2(g, b):
                sp.wait_ge(x2_ready, GB * g + b + 1)
                sp.dma_start(tokens(x2_dram, GB * g + b), xrb[:, b]).then_inc(x2_out[b], 16)

            def load_w2(i):
                wait(sp, w2_lo_made, i - 1)
                sp.dma_start(stage_w2[i % 2][:], weight(w2[2 * i * P:2 * (i + 1) * P, :]))\
                    .then_inc(w2_in[i % 2], 16)

            def load_next(g, b, last):
                if last:
                    sp.wait_ge(x2_out[b], 16)
                    load_bx(NG, b, x2_dram, b)
                else:
                    load_bx(g + 1, b)

            def body_b(g, first, last):
                if not first:
                    load_next(g, 0, last)
                    load_next(g, 1, last)
                    store_x2(g - 1, GB - 1)
                for b in range(GB):
                    load_bxr(g, b)
                load_next(g, 2, last)
                load_next(g, 3, last)
                if first:
                    for k in range(2):
                        sp.dma_start(stage_w1[:, k], w1[k * P:(k + 1) * P, :]).then_inc(w1_in[k], 16)
                if last:
                    for k in range(2):
                        sp.wait_ge(w1_lo_made, k + 3)
                        sp.dma_start(stage_w1[:, k], w1[(2 + k) * P:(3 + k) * P, :]).then_inc(w1_in[k], 16)
                    load_w2(0)
                for b in range(GB - 1):
                    store_x2(g, b)

            groups(sp, body_b)
            store_x2(NG - 1, GB - 1)

            for b in range(GB):
                sp.wait_ge(x2_out[b], 16 * NG)

            def load_cx(g, b):
                wait(sp, cxn, GB * g + b - 1)
                sp.dma_start(xc[:, b % 2], tokens(x2_dram, GB * g + GB + b)).then_inc(cx_in[b % 2], 16)

            def load_cxr(g, b):
                wait(sp, y_out[b], 16 * g)
                sp.dma_start(xrc[:, b], tokens(x2_dram, GB * g + b)).then_inc(cxr_in[b], 16)

            def store_y(g, b):
                sp.wait_ge(y_ready, GB * g + b + 1)
                sp.dma_start(tokens(out, GB * g + b), xrc[:, b]).then_inc(y_out[b], 16)

            sp.wait_ge(bxn, NB + GB)

            def body_c(g, first, last):
                if first:
                    load_w2(1)
                if not first:
                    for b in range(GB):
                        store_y(g - 1, b)
                for b in range(GB):
                    load_cxr(g, b)
                if not last:
                    for b in range(2):
                        load_cx(g, b)
                if first:
                    for i in range(2, FT // 2):
                        load_w2(i)
                if not last:
                    for b in range(2, GB):
                        load_cx(g, b)

            groups(sp, body_c)
            for b in range(GB):
                store_y(NG - 1, b)
            for b in range(GB):
                sp.wait_ge(y_out[b], 16 * NG)

        @block.tensor
        def _(pe):
            def split_product(dst, w_hi, w_lo, a_hi, a_lo, start, stop):
                nc.tensor.matmul(dst, w_hi, a_hi, start=start, stop=False)
                nc.tensor.matmul(dst, w_hi, a_lo, start=False, stop=False)
                return nc.tensor.matmul(dst, w_lo, a_hi, start=False, stop=stop)

            pe.wait_ge(consts_in, 32)
            for k in range(C):
                if k % 2 == 0:
                    pe.wait_ge(wgb_in[k // 2], 32)
                for i in range(2):
                    tile = 2 * (k % 2) + i
                    last = nc.tensor.matmul(ps_s[0][NB * tile:NB * (tile + 1), :], cond[:, k, :], wgb[:, i, k, :],
                                            start=(k < 2), stop=(k >= 2))
            last.then_inc(film0_done, 1)
            pe.wait_ge(consts_made, 3)
            pe.wait_ge(film0_copied, 1)
            for c in range(C):
                last = nc.tensor.transpose(ps_s[1][:, c * P:(c + 1) * P], fv0[:, c * P:(c + 1) * P], ident[:])
            last.then_inc(film0_t, 1)

            def norm_t(g, b, pos, banks_full, banks_free, xn, slot, ready, uses=bank_uses):
                i, n = pos % 2, uses(g, pos)
                pe.wait_ge(ready, GB * (g + 1) + b + 1)
                wait(pe, banks_free[i], n)
                for c in range(C):
                    last = nc.tensor.transpose(ps_g[i][:, c * P:(c + 1) * P], xn[:, slot, c * P:(c + 1) * P], ident[:])
                last.then_inc(banks_full[i], 1)

            def norm_a(g, b, pos):
                norm_t(g, b, pos, g_full, g_free, xa, b, xn_ready)

            for b in range(GB):
                norm_a(-1, b, 12 + b)
            pe.wait_ge(st0_made, 1)
            for i in range(2):
                for c in range(C):
                    last = nc.tensor.transpose(ps_t[i][0:NB, c * P:(c + 1) * P], st_flat[:, i * C + c, :], ident[:])
            last.then_inc(st0_t, 1)

            def qk(g, m, pos, offset):
                i = pos % 2
                pe.wait_ge(g_free[i], bank_uses(g, pos))
                for k in range(C):
                    n = slice(offset + m * P, offset + (m + 1) * P)
                    last = split_product(ps_g[i][:], wa_hi[:, k, n], wa_lo[:, k, n], h_hi[:, k, :], h_lo[:, k, :],
                                         k == 0, k == C - 1)
                last.then_inc(g_full[i], 1)

            def values(g, b, pos, ks):
                i = pos % 2
                if ks[0] == 0:
                    pe.wait_ge(g_free[i], bank_uses(g, pos))
                t = slice(b * P, (b + 1) * P)
                for k in ks:
                    last = split_product(ps_g[i][:], h_hi[:, k, t], h_lo[:, k, t], wa_hi[:, k, 2 * D:3 * D],
                                         wa_lo[:, k, 2 * D:3 * D], k == 0, k == C - 1)
                if ks[-1] == C - 1:
                    last.then_inc(g_full[i], 1)

            def v_pos(b):
                return 8 if b == 0 else 7 + 2 * b

            def scores(g, u):
                b, m = u // C, u % C
                if b == 0:
                    pe.wait_ge(g_free[0], bank_uses(g, 2 * m) + 1)
                    pe.wait_ge(g_free[1], bank_uses(g, 2 * m + 1) + 1)
                wait(pe, exp_done, UNITS * g + u - 1)
                nc.tensor.matmul(ps_s[u % 2][:], qa[:, m, b * P:(b + 1) * P], k_diag[:, m, b, :, :],
                                 start=True, stop=True).then_inc(s_done, 1)

            def transpose_p(g, u):
                pe.wait_ge(exp_done, UNITS * g + u + 1)
                wait(pe, pt_copied, UNITS * g + u - 1)
                for j in range(HM):
                    last = nc.tensor.transpose(ps_t[u % 2][:, j * P:(j + 1) * P], pa[:, u % 2, j, :], ident[:])
                last.then_inc(tp_done, 1)

            def attend(g, u):
                b, m = u // C, u % C
                pe.wait_ge(pt_copied, UNITS * g + u + 1)
                if m == 0:
                    pe.wait_ge(g_free[v_pos(b) % 2], bank_uses(g, v_pos(b)) + 1)
                    wait(pe, o_scaled, GB * g + b)
                for j in range(HM):
                    f = (m * HM + j) * HD
                    last = nc.tensor.matmul(ps_o[j * HD:(j + 1) * HD, m * P:(m + 1) * P], va[:, b, f:f + HD],
                                            pta[:, u % 2, j, :], start=True, stop=True)
                last.then_inc(pv_done, 1)

            def recip_t(g, b):
                pe.wait_ge(rec_ready, GB * g + b + 1)
                wait(pe, h1_ready, GB * g + b)
                flat = recx[:].rearrange("p h d -> p (h d)")
                for m in range(C):
                    last = nc.tensor.transpose(ps_r[:, m * P:(m + 1) * P], flat[:, m * P:(m + 1) * P], ident[:])
                last.then_inc(r_done, 1)

            def project(g, b, ks):
                if ks[0] == 0:
                    pe.wait_ge(o_hi_ready, GB * g + b + 1)
                    pe.wait_ge(o_lo_ready, GB * g + b + 1)
                    pe.wait_ge(r_copied, GB * g + b + 1)
                for k in ks:
                    last = split_product(ps_r[:], o_hi[:, b % 2, k, :], o_lo[:, b % 2, k, :], wp_hi[:, k, :],
                                         wp_lo[:, k, :], k == 0, k == C - 1)
                if ks[-1] == C - 1:
                    last.then_inc(proj_done, 1)

            def body(g, first, last):
                pe.wait_ge(hi_ready, GB * g + GB)
                pe.wait_ge(lo_ready, GB * g + GB)
                for m in range(C):
                    if first and m == 0:
                        pe.wait_ge(wa_hi_made, 1)
                        pe.wait_ge(wa_lo_made, 1)
                    qk(g, m, 2 * m, D)
                    if m == 0 and not first:
                        recip_t(g - 1, GB - 1)
                    if first and m == 0:
                        pe.wait_ge(wa_hi_made, 2)
                        pe.wait_ge(wa_lo_made, 2)
                    qk(g, m, 2 * m + 1, 0)
                    if m == 1 and not first:
                        project(g - 1, GB - 1, range(C))
                    if m >= 2:
                        scores(g, m - 2)
                if first:
                    pe.wait_ge(wa_hi_made, 3)
                    pe.wait_ge(wa_lo_made, 3)
                values(g, 0, v_pos(0), range(C))
                for u in range(UNITS):
                    b, m = u // C, u % C
                    transpose_p(g, u)
                    if u + 2 < UNITS:
                        scores(g, u + 2)
                    if u > 0:
                        attend(g, u - 1)
                    if m == 0 and b > 0:
                        recip_t(g, b - 1)
                    if b < GB - 1:
                        values(g, b + 1, v_pos(b + 1), [m])
                    if m == 1 and not last:
                        norm_a(g, b, [10, 12, 14, 15][b])
                    if b > 0 and m >= 2:
                        if first and b == 1 and m == 2:
                            pe.wait_ge(wa_hi_made, 4)
                            pe.wait_ge(wa_lo_made, 4)
                        project(g, b - 1, [0, 1] if m == 2 else [2, 3])
                attend(g, UNITS - 1)

            groups(pe, body)

            recip_t(NG - 1, GB - 1)
            pe.wait_ge(raw_in[0], 16)
            pe.wait_ge(raw_in[1], 16)
            for i in range(C):
                if i == 1:
                    project(NG - 1, GB - 1, range(C))
                for k in range(C):
                    last = nc.tensor.matmul(bank[2 + i][:], raw_b[:, 0, k, i * P:(i + 1) * P], raw_b[:, 1, k, :],
                                            start=(k == 0), stop=(k == C - 1))
                last.then_inc(wvp_done, 1)

            def wq_wk(i):
                if i == 0:
                    pe.wait_ge(raw_in[2], 16)
                    pe.wait_ge(raw_in[3], 16)
                pe.wait_ge(wvp_lo_made, i + 1)
                for k in range(C):
                    last = nc.tensor.matmul(bank[2 + i][:], raw_b[:, 2, k, i * P:(i + 1) * P], raw_b[:, 3, k, :],
                                            start=(k == 0), stop=(k == C - 1))
                last.then_inc(g_done, 1)

            wq_wk(0)
            wq_wk(1)
            pe.wait_ge(film_in[0], 16)
            pe.wait_ge(film_in[1], 16)
            for k in range(C):
                for i in range(4):
                    last = nc.tensor.matmul(ps_g[0][NB * i:NB * (i + 1), :], cond[:, k, :],
                                            film_b[:, i // 2, k, (i % 2) * D:(i % 2 + 1) * D],
                                            start=(k == 0), stop=(k == C - 1))
            last.then_inc(film1_done, 1)
            for k in range(2):
                for i in range(4):
                    n = 2 * (i % 2) + k
                    last = nc.tensor.matmul(ps_o[HD * i:HD * (i + 1), :],
                                            col("bk1" if i < 2 else "bq1", n).broadcast_to([P, HD]),
                                            raw_b[:, 2 + i // 2, n, :], start=(k == 0), stop=(k == 1))
            last.then_inc(uc_done, 1)
            pe.wait_ge(film1_copied, 1)
            pe.wait_ge(h1_ready, NB)
            for c in range(C):
                last = nc.tensor.transpose(ps_r[:, c * P:(c + 1) * P], fv1[:, c * P:(c + 1) * P], ident[:])
            last.then_inc(film1_t, 1)
            pe.wait_ge(uc_copied, 1)
            for c in range(C):
                last = nc.tensor.transpose(ps_o[:, c * P:(c + 1) * P], uc_rows[:, c * P:(c + 1) * P], ident[:])
            last.then_inc(uc_t, 1)

            pe.wait_ge(g_free[1], bank_uses(NG - 1, 13) + 1)

            def norm_b(g, b, pos):
                norm_t(g, b, pos, bg_full, bg_free, xnb, b, bxn, bank_uses_b)

            for b in range(GB):
                if b % 2 == 0:
                    wq_wk(2 + b // 2)
                norm_b(-1, b, 8 + b)
            pe.wait_ge(uc_made, 1)
            for k in range(C):
                last = nc.tensor.matmul(ps_o[:], col("bv1", k).broadcast_to([P, P]), raw_b[:, 1, k, :],
                                        start=(k == 0), stop=(k == C - 1))
            last.then_inc(bvp_done, 1)

            def h_g(g, m, first):
                i = m % 2
                wait(pe, bg_free[i], bank_uses_b(g, m))
                for k in range(C):
                    if first and m == 0:
                        pe.wait_ge(g_hi_made, k + 1)
                        pe.wait_ge(g_lo_made, k + 1)
                    n = slice(m * P, (m + 1) * P)
                    last = split_product(ps_g[i][:], g_hi_b[:, k, n], g_lo_b[:, k, n], hb_hi[:, k, :],
                                         hb_lo[:, k, :], k == 0, k == C - 1)
                last.then_inc(bg_full[i], 1)

            def h_u(g):
                pe.wait_ge(hb_copied, g + 1)
                wait(pe, x2_ready, GB * g)
                for k in range(C):
                    last = nc.tensor.matmul(bank[7][HD * k:HD * (k + 1), :], uc[:, 0, k:k + 1].broadcast_to([P, HD]),
                                            hb[:, k, :], start=True, stop=True)
                last.then_inc(br_done, 1)

            def values_b(g, b):
                tok = slice(b * P, (b + 1) * P)
                pe.wait_ge(bg_free[0], bank_uses_b(g, 4 + 2 * b))
                for k in range(C):
                    last = split_product(ps_g[0][:], hb_hi[:, k, tok], hb_lo[:, k, tok], wvp_hi[:, k, :],
                                         wvp_lo[:, k, :], k == 0, k == C - 1)
                last.then_inc(bg_full[0], 1)

            def transpose_pb(g, b):
                t = GB * g + b
                pe.wait_ge(bexp, t + 1)
                wait(pe, bpt, 2 * (t - 1))
                nc.tensor.transpose(ps_t[b % 2][:, 0:P], pb[:, b % 2, :], ident[:]).then_inc(btp, 1)

            def attend_b(g, b):
                t = GB * g + b
                pe.wait_ge(bpt, 2 * t + 2)
                pe.wait_ge(bg_free[0], bank_uses_b(g, 4 + 2 * b) + 1)
                wait(pe, x2_ready, t - 1)
                split_product(bank[6 + b % 2][:], ptb_hi[:, b % 2, :], ptb_lo[:, b % 2, :], vb_hi[:, b, :],
                              vb_lo[:, b % (GB - 1), :], True, True).then_inc(bpv, 1)

            def body_b(g, first, last):
                pe.wait_ge(bhi, GB * g + GB)
                pe.wait_ge(blo, GB * g + GB)
                if first:
                    pe.wait_ge(st1_made, 1)
                    pe.wait_ge(cb_made, 1)
                for m in range(C):
                    h_g(g, m, first)
                    if m == 0 and not first:
                        transpose_pb(g - 1, GB - 1)
                    if m == 1 and not first:
                        attend_b(g - 1, GB - 1)
                    if m == 2:
                        h_u(g)
                if first:
                    pe.wait_ge(wvp_hi_made, C)
                    pe.wait_ge(wvp_lo_made, C)
                values_b(g, 0)
                for b in range(GB):
                    t = GB * g + b
                    if b < GB - 1:
                        norm_b(g, b, 5 + 2 * b)
                    if b == 0:
                        pe.wait_ge(bg_free[0], bank_uses_b(g, 2) + 1)
                        pe.wait_ge(bg_free[1], bank_uses_b(g, 3) + 1)
                        pe.wait_ge(br_copied, g + 1)
                    wait(pe, bexp, t - 1)
                    tok = slice(b * P, (b + 1) * P)
                    for k in range(C):
                        nc.tensor.matmul(ps_s[b % 2][:, 0:P], tb[:, k, tok], hb[:, k, tok], start=(k == 0),
                                         stop=False)
                    nc.tensor.matmul(ps_s[b % 2][:, 0:P], rb[:, tok], inv_hd[:].broadcast_to([P, P]), start=False,
                                     stop=True).then_inc(bs_done, 1)
                    if b < GB - 1:
                        values_b(g, b + 1)
                    if b == GB - 2:
                        norm_b(g, b + 1, 7 + 2 * b)
                    if b > 0:
                        attend_b(g, b - 1)
                    if b < GB - 1:
                        transpose_pb(g, b)

            groups(pe, body_b)

            def norm_c(g, b):
                t = GB * g + b
                pe.wait_ge(cxn, t + 1)
                wait(pe, ct_free_act if b % 2 else ct_free_dve, 2 * g + b // 2)
                for c in range(C):
                    last = nc.tensor.transpose(bank[6 + b % 2][:, c * P:(c + 1) * P], xnc[:, b, c * P:(c + 1) * P],
                                               ident[:])
                last.then_inc(ct_full, 1)

            pe.wait_ge(bg_free[0], bank_uses_b(NG - 1, 10) + 1)
            pe.wait_ge(bg_free[1], bank_uses_b(NG - 1, 11) + 1)

            def up(g, f):
                n = FT * g + f
                wait(pe, gelu_done, n - 1)
                for k in range(C):
                    last = split_product(bank[f % 2][:], w1_hi[:, k, f * P:(f + 1) * P], w1_lo[:, k, f * P:(f + 1) * P],
                                         hc_hi[:, k, :], hc_lo[:, k, :], k == 0, k == C - 1)
                last.then_inc(up_done, 1)

            def down(g, f, first):
                n = FT * g + f
                if first and f % 2 == 0:
                    pe.wait_ge(w2_hi_made, f // 2 + 1)
                    pe.wait_ge(w2_lo_made, f // 2 + 1)
                pe.wait_ge(g_hi_ready, n + 1)
                pe.wait_ge(g_lo_ready, n + 1)
                if f == 0:
                    wait(pe, y_ready, GB * g)
                for b in range(GB):
                    tok = slice(b * P, (b + 1) * P)
                    last = split_product(bank[2 + b][:], g_hi[:, f % (LAG + 1), tok], g_lo[:, f % (LAG + 1), tok],
                                         w2_hi[:, f, :], w2_lo[:, f, :], f == 0, f == FT - 1)
                    if f == FT - 1:
                        last.then_inc(acc_done, 1)
                if f < FT - 1:
                    last.then_inc(down_done, 1)

            def body_c(g, first, last):
                if first:
                    pe.wait_ge(blo, NB + GB)
                wait(pe, clo, GB * g)
                if first:
                    pe.wait_ge(w1_hi_made, 2 * C - 2)
                    pe.wait_ge(w1_lo_made, 2 * C - 2)
                for f in range(FT):
                    if first and f == FT // 2:
                        pe.wait_ge(w1_hi_made, 2 * C)
                        pe.wait_ge(w1_lo_made, 2 * C)
                    up(g, f)
                    if first and f == 0:
                        transpose_pb(NG - 1, GB - 1)
                    if first and f == 1:
                        attend_b(NG - 1, GB - 1)
                    if f >= LAG:
                        down(g, f - LAG, first)
                if first:
                    pe.wait_ge(x2_ready, NB)
                for f in range(FT - LAG, FT):
                    if not last and f < FT - LAG + 2:
                        for b in range(2):
                            norm_c(g, 2 * (f - (FT - LAG)) + b)
                    down(g, f, first)

            groups(pe, body_c)

        @block.scalar
        def _(act):
            act.wait_ge(film0_done, 1)
            nc.scalar.activation(fv0[:], ps_s[0][:], ACT.Identity).then_inc(film0_copied, 1)
            wa_dst = [wa_hi[:, :, D:2 * D], wa_hi[:, :, 0:D], wa_hi[:, :, 2 * D:3 * D], wp_hi[:]]

            def split_wa(i):
                act.wait_ge(stage_in[i % 2], 16 * (i // 2 + 1))
                nc.scalar.activation(wa_dst[i], stage_a[:, i % 2], ACT.Identity).then_inc(wa_hi_made, 1)

            split_wa(0)

            def affine(src, dst, b, free, st=cur_st):
                for c in range(C):
                    last = nc.scalar.activation(dst[:, c, :], src[:, c * P:(c + 1) * P], ACT.Identity,
                                                bias=st[:, b, C + c:C + c + 1], scale=st[:, b, c:c + 1])
                last.then_inc(free, 1)

            def scale_norm(g, b, pos, full, free, cur, buf, uses=bank_uses):
                i, n = pos % 2, uses(g, pos)
                act.wait_ge(cur, g + 2)
                act.wait_ge(full[i], n + 1)
                affine(ps_g[i], buf, b, free[i])

            def round_norm(g, b, pos, free, high, buf, dst, uses=bank_uses):
                act.wait_ge(free[pos % 2], uses(g, pos) + 1)
                nc.scalar.activation(dst[:, :, b * P:(b + 1) * P], buf, ACT.Identity).then_inc(high, 1)

            def norm_a(g, b, pos):
                wait(act, lo_ready, GB * (g + 1) + b - 1)
                scale_norm(g, b, pos, g_full, g_free, cur_ready, hf[:, b % 2])
                round_norm(g, b, pos, g_free, hi_ready, hf[:, b % 2], h_hi)

            for b in range(0, GB, 2):
                wait(act, lo_ready, b - 1)
                scale_norm(-1, b, 12 + b, g_full, g_free, cur_ready, hf[:, 0])
                for i in range(2):
                    round_norm(-1, b + i, 12 + b + i, g_free, hi_ready, hf[:, i], h_hi)
            split_wa(1)

            def keys(g, m):
                if isinstance(g, int) and g == 0 and m == 0:
                    act.wait_ge(consts_made, 4)
                act.wait_ge(g_full[0], bank_uses(g, 2 * m) + 1)
                for j in range(HM):
                    q = slice(j * HD, (j + 1) * HD)
                    c = COL["bk0"] + m
                    last = nc.scalar.activation(k_diag[q, m, :, j, :], ps_g[0][q, :].rearrange("p (b t) -> p b t", b=GB),
                                                ACT.Identity, bias=cols[q, c:c + 1])
                last.then_inc(g_free[0], 1)

            def exps(g, u):
                b, m = u // C, u % C
                act.wait_ge(max_done, UNITS * g + u + 1)
                wait(act, tp_done, UNITS * g + u - 1)
                for j in range(HM):
                    h = m * HM + j
                    last = nc.scalar.activation(pa[:, u % 2, j, :], ps_s[u % 2][:, j * P:(j + 1) * P], ACT.Exp,
                                                bias=neg_max[:, u % 2, j:j + 1], accum_out=sums[:, b % 2, h:h + 1])
                last.then_inc(exp_done, 1)

            def copy_r(g, b):
                t = GB * g + b
                act.wait_ge(r_done, t + 1)
                wait(act, o_scaled, t)
                nc.scalar.activation(rs[:], ps_r[:], ACT.Copy, scale=INV_SQRT_D).then_inc(r_copied, 1)

            def round_o(g, b):
                t = GB * g + b
                act.wait_ge(o_scaled, t + 1)
                wait(act, proj_done, t - 1)
                nc.scalar.activation(o_hi[:, b % 2], of[:], ACT.Identity).then_inc(o_hi_ready, 1)

            def body(g, first, last):
                keys(g, 0)
                if not first:
                    copy_r(g - 1, GB - 1)
                    round_o(g - 1, GB - 1)
                for m in range(1, C):
                    keys(g, m)
                    if first and m < 3:
                        split_wa(m + 1)
                exps(g, 0)
                for u in range(UNITS):
                    b, m = u // C, u % C
                    if u + 1 < UNITS:
                        exps(g, u + 1)
                    if m == 0 and b > 0:
                        copy_r(g, b - 1)
                    if m == 1 and b > 0:
                        round_o(g, b - 1)
                    if m == 2 and not last:
                        norm_a(g, b, [10, 12, 14, 15][b])

            groups(act, body)
            copy_r(NG - 1, GB - 1)
            round_o(NG - 1, GB - 1)

            def squares(g, b, x, x_sem, sum_sem, var_sem):
                act.wait_ge(x_sem[b % 2], loaded(2 * g + b // 2 + 1))
                wait(act, var_sem, GB * g + b - 1)
                nc.scalar.activation(junk[:], x[:, b % 2], ACT.Square, accum_out=ssq[:, b % 2:b % 2 + 1])\
                    .then_inc(sum_sem, 1)

            def squares_b(g, b):
                wait(act, bssq, GB * g + b)
                squares(g, b, xb, bx_in, bssq, bvar)

            act.wait_ge(s_done, UNITS * NG)
            for i in range(C):
                act.wait_ge(wvp_done, i + 1)
                nc.scalar.activation(wvp_hi[:, i], bank[2 + i][:], ACT.Identity).then_inc(wvp_hi_made, 1)
                squares_b(0, i)

            def round_g(i):
                act.wait_ge(g_done, i + 1)
                nc.scalar.activation(g_hi_b[:, i], bank[2 + i][:], ACT.Identity).then_inc(g_hi_made, 1)

            round_g(0)
            act.wait_ge(film1_done, 1)
            nc.scalar.activation(fv1[:], ps_g[0][:], ACT.Identity).then_inc(film1_copied, 1)
            act.wait_ge(uc_done, 1)
            nc.scalar.activation(uc_rows[:], ps_o[:], ACT.Identity).then_inc(uc_copied, 1)
            round_g(1)

            def scale_b(g, b, pos):
                own = hb_new[:, :, b * P:(b + 1) * P]
                scale_norm(g, b, pos, bg_full, bg_free, bcur, own, bank_uses_b)

            def round_b(g, b, pos):
                own = hb_new[:, :, b * P:(b + 1) * P]
                round_norm(g, b, pos, bg_free, bhi, own, hb_hi, bank_uses_b)

            for b in range(0, GB, 2):
                round_g(2 + b // 2)
                scale_b(-1, b, 8 + b)
                round_b(-1, b, 8 + b)
                round_b(-1, b + 1, 9 + b)

            def copy_vb(g, b):
                act.wait_ge(bg_full[0], bank_uses_b(g, 4 + 2 * b) + 1)
                nc.scalar.activation(vb_hi[:, b, :], ps_g[0][:], ACT.Identity).then_inc(bv_hi, 1)

            def split_w1(i):
                k, n = w1_piece(i)
                act.wait_ge(w1_in[k % 2], 16 * (k // 2 + 1))
                nc.scalar.activation(w1_hi[:, k, n], stage_w1[:, k % 2, n], ACT.Identity).then_inc(w1_hi_made, 1)

            def body_b(g, first, last):
                act.wait_ge(blo, GB * g + GB)
                nc.scalar.activation(hb[:], hb_new[:], ACT.Identity).then_inc(hb_copied, 1)
                squares_b(g + 1, 0)
                squares_b(g + 1, 1)
                if first:
                    act.wait_ge(uc_made, 1)
                act.wait_ge(br_done, g + 1)
                nc.scalar.activation(rb[:], bank[7][:], ACT.Identity, bias=bqk_sum[:, 1:2]).then_inc(br_copied, 1)
                squares_b(g + 1, 2)
                squares_b(g + 1, 3)
                act.wait_ge(hb_copied, g + 1)
                copy_vb(g, 0)
                for b in range(GB):
                    t = GB * g + b
                    if b < GB - 1:
                        scale_b(g, b, 5 + 2 * b)
                    act.wait_ge(bmax, t + 1)
                    wait(act, btp, t - 1)
                    nc.scalar.activation(pb[:, b % 2, :], ps_s[b % 2][:, 0:P], ACT.Exp, scale=INV_SQRT_D,
                                         bias=neg_max[:, b % 2, 1:2], accum_out=sums[:, b % 2, 0:1]).then_inc(bexp, 1)
                    if b < GB - 1:
                        round_b(g, b, 5 + 2 * b)
                        copy_vb(g, b + 1)
                    if b == GB - 2:
                        scale_b(g, b + 1, 7 + 2 * b)
                        round_b(g, b + 1, 7 + 2 * b)
                    if first or last:
                        split_w1(b if first else GB + b)

            groups(act, body_b)

            def squares_c(g, b):
                wait(act, cssq, GB * g + b)
                squares(g, b, xc, cx_in, cssq, cvar)

            def norm_c(g, b):
                t = GB * g + b
                act.wait_ge(ccur, g + 1)
                act.wait_ge(ct_full, t + 1)
                wait(act, clo, t - 1)
                affine(bank[7], hfc_act, b, ct_free_act)
                act.wait_ge(ct_free_act, 2 * g + b // 2 + 1)
                nc.scalar.activation(hc_hi[:, :, b * P:(b + 1) * P], hfc_act[:], ACT.Identity).then_inc(chi_act, 1)

            def body_c(g, first, last):
                for f in range(FT):
                    n = FT * g + f
                    if first and w2_pair(f) is not None:
                        i = w2_pair(f)
                        act.wait_ge(w2_in[i % 2], 16 * (i // 2 + 1))
                        nc.scalar.activation(w2_hi[:, 2 * i:2 * i + 2, :], stage_w2[i % 2][:], ACT.Identity)\
                            .then_inc(w2_hi_made, 1)
                    act.wait_ge(up_done, n + 1)
                    wait(act, g_lo_ready, n - 1)
                    nc.scalar.activation(gf[f % 2][:], bank[f % 2][:], ACT.Gelu, bias=cols[:, B1_COL + f:B1_COL + f + 1])\
                        .then_inc(gelu_done, 1)
                    if not last and f % 2 == 1 and 3 <= f < 3 + 2 * GB:
                        squares_c(g, (f - 3) // 2)
                if not last:
                    norm_c(g, 1)
                    norm_c(g, 3)

            groups(act, body_c)

        @block.vector
        def _(dve):
            step = [0]

            def then(instruction):
                step[0] += 1
                instruction.then_inc(dve_step, 1)
                dve.wait_ge(dve_step, step[0])

            def low_half(dst, whole, high):
                return nc.vector.tensor_tensor(dst, whole, high.bitcast(F32), ALU.subtract)

            def table(st, c0):
                return st[:, :, c0:c0 + C].rearrange("p b c -> p c b")

            def mean_var(g, b):
                dve.wait_ge(x_in[b], loaded(g + 1))
                wait(dve, xn_ready, GB * g + b - 1)
                wait(dve, var_ready, 2 * (GB * g + b))
                nc.vector.bn_stats(stats[:], xa[:, b]).then_inc(bn_done, 1)
                wait_apart(dve, bn_done, GB * g + b + 1, passed)
                nc.vector.bn_aggr(mv1[:, b % 2], stats[:]).then_inc(var_ready, 1)
                dve.wait_ge(var_ready, 2 * (GB * g + b) + 1)
                nc.vector.tensor_scalar(ve1[:, b % 2:b % 2 + 1], mv1[:, b % 2, 1:2], EPS_LN, None, ALU.add)\
                    .then_inc(var_ready, 1)

            for b in range(GB):
                mean_var(0, b)
            dve.wait_ge(film0_t, 1)
            dve.wait_ge(consts_in, 32)
            ft = ps_s[1][:].rearrange("p (c s v b) -> p c s v b", c=C, s=2, v=2)
            then(nc.vector.tensor_tensor(tmp_a[:], ft[:, :, 0, 0, :], col_wide("bg"), ALU.add))
            then(nc.vector.tensor_tensor(tmp_b[:], ft[:, :, 0, 1, :], col_wide("bb"), ALU.add))
            then(nc.vector.tensor_tensor(tmp_a[:], tmp_a[:], ft[:, :, 1, 0, :], ALU.add))
            then(nc.vector.tensor_tensor(tmp_b[:], tmp_b[:], ft[:, :, 1, 1, :], ALU.add))
            nc.vector.tensor_tensor(st_flat[:, 0:C, :], tmp_a[:], col_wide("ln_g"), ALU.mult)
            then(nc.vector.tensor_tensor(st_flat[:, C:2 * C, :], tmp_a[:], col_wide("ln_b"), ALU.mult))
            then(nc.vector.tensor_tensor(st_flat[:, C:2 * C, :], st_flat[:, C:2 * C, :], tmp_b[:], ALU.add))
            nc.vector.tensor_copy(st_ln[:], st_flat[:].rearrange("p v b -> p b v")).then_inc(st0_made, 1)

            wa_dst = [wa_lo[:, :, D:2 * D], wa_lo[:, :, 0:D], wa_lo[:, :, 2 * D:3 * D], wp_lo[:]]
            wa_src = [wa_hi[:, :, D:2 * D], wa_hi[:, :, 0:D], wa_hi[:, :, 2 * D:3 * D], wp_hi[:]]

            def split_wa(i):
                dve.wait_ge(wa_hi_made, i + 1)
                low_half(wa_dst[i], stage_a[:, i % 2], wa_src[i]).then_inc(wa_lo_made, 1)

            def scale_odd(b, n, full, free, cur, dst):
                dve.wait_ge(cur, 1)
                dve.wait_ge(full[1], n + 1)
                for c in range(C):
                    last = nc.vector.tensor_scalar(dst[:, c, :], ps_g[1][:, c * P:(c + 1) * P], cur_st[:, b, c:c + 1],
                                                   cur_st[:, b, C + c:C + c + 1], ALU.mult, ALU.add)
                last.then_inc(free[1], 1)

            def norm_low(t, b, high, low, dst, buf, src):
                dve.wait_ge(high, t + 1)
                tok = slice(b * P, (b + 1) * P)
                low_half(dst[:, :, tok], buf[:, b % 2], src[:, :, tok]).then_inc(low, 1)

            for b in range(0, GB, 2):
                wait(dve, lo_ready, b)
                scale_odd(b + 1, b // 2, g_full, g_free, cur_ready, hf[:, 1])
                for i in range(2):
                    norm_low(b + i, b + i, hi_ready, lo_ready, h_lo, hf, h_hi)
                split_wa(b // 2)
            dve.wait_ge(st0_t, 1)
            for i in range(2):
                nc.vector.tensor_copy(st_rows[:, i * D:(i + 1) * D], ps_t[i][0:NB, :]).then_inc(st_rows_made, 1)

            def row_max(g, u):
                dve.wait_ge(s_done, UNITS * g + u + 1)
                nc.vector.tensor_reduce(neg_max[:, u % 2, :], ps_s[u % 2][:].rearrange("p (h k) -> p h k", h=HM), AX.X,
                                        ALU.max, negate=True).then_inc(max_done, 1)

            def copy_v(g, b, pos):
                i = pos % 2
                dve.wait_ge(g_full[i], bank_uses(g, pos) + 1)
                nc.vector.tensor_tensor(va[:, b, :], ps_g[i][:], bv0[:], ALU.add).then_inc(g_free[i], 1)

            def copy_pt(g, u):
                dve.wait_ge(tp_done, UNITS * g + u + 1)
                wait(dve, pv_done, UNITS * g + u - 1)
                nc.vector.tensor_copy(pta[:, u % 2].rearrange("p h q -> p (h q)"), ps_t[u % 2][:]).then_inc(pt_copied, 1)

            def recip(g, b):
                t = GB * g + b
                wait(dve, r_copied, t)
                dve.wait_ge(exp_done, UNITS * g + C * b + C)
                nc.vector.reciprocal(rec[:], sums[:, b % 2, :]).then_inc(rec_made, 1)
                dve.wait_ge(rec_made, t + 1)
                nc.vector.tensor_copy(recx[:], rec[:].unsqueeze(2).broadcast_to([P, HEADS, HD]))\
                    .then_inc(rec_ready, 1)

            def scale_o(g, b):
                t = GB * g + b
                dve.wait_ge(r_copied, t + 1)
                wait(dve, o_lo_ready, t)
                dve.wait_ge(pv_done, UNITS * g + C * b + C)
                nc.vector.tensor_tensor(of[:].rearrange("p c t -> p (c t)"), ps_o[:], rs[:], ALU.mult)\
                    .then_inc(o_scaled, 1)

            def low_o(g, b):
                t = GB * g + b
                dve.wait_ge(o_hi_ready, t + 1)
                low_half(o_lo[:, b % 2], of[:], o_hi[:, b % 2]).then_inc(o_lo_ready, 1)

            def residual(g, b):
                t = GB * g + b
                dve.wait_ge(proj_done, t + 1)
                dve.wait_ge(xr_ready, t + 1)
                wait(dve, x1_out[b], 16 * g)
                nc.vector.tensor_tensor(h1[:, b], ps_r[:], xra[:, b % 2], ALU.add).then_inc(h1_ready, 1)

            def mean_var2(g):
                dve.wait_ge(h1_ready, GB * g + GB)
                wait(dve, ln2_shifted, GB * g)
                for b in range(GB):
                    nc.vector.bn_stats(stats2[:, b], h1[:, b]).then_inc(bn2_done, 1)
                for b in range(GB):
                    wait_apart(dve, bn2_done, 2 * GB * g + GB + b, passed)
                    nc.vector.bn_aggr(mv2[:, b], stats2[:, b]).then_inc(bn2_done, 1)
                dve.wait_ge(bn2_done, 2 * GB * g + 2 * GB)
                nc.vector.tensor_scalar(ve2[:], mv2[:, :, 1], EPS_LN, None, ALU.add).then_inc(var2_ready, 1)

            def norm2(g, b):
                dve.wait_ge(rows_ld[b % 2], loaded(2 * g + b // 2 + 1))
                nc.vector.scalar_tensor_tensor(nb[:, b], h1[:, b], mv2[:, b, 0:1], rows[:, b % 2, 0:D], ALU.subtract,
                                               ALU.mult).then_inc(ln2_normed, 1)

            def add_x1(g, b):
                dve.wait_ge(rstd2_ready, g + 1)
                dve.wait_ge(ln2_shifted, GB * g + b + 1)
                nc.vector.scalar_tensor_tensor(h1[:, b], nb[:, b], rstd2[:, b:b + 1], h1[:, b], ALU.mult, ALU.add)\
                    .then_inc(x1_ready, 1)

            def body(g, first, last):
                for m in range(C):
                    if m == 0 and not first:
                        scale_o(g - 1, GB - 1)
                    dve.wait_ge(g_full[1], bank_uses(g, 2 * m + 1) + 1)
                    nc.vector.tensor_scalar(qa[:, m, :], ps_g[1][:], col("bq0", m), None, ALU.add).then_inc(g_free[1], 1)
                    if m >= 2:
                        row_max(g, m - 2)
                    if first and 0 < m < 3:
                        split_wa(m + 1)
                    if m == 0 and not first:
                        low_o(g - 1, GB - 1)
                    if not last:
                        mean_var(g + 1, m)
                    if not first:
                        if m == 1:
                            residual(g - 1, GB - 1)
                            mean_var2(g - 1)
                            norm2(g - 1, 0)
                            norm2(g - 1, 1)
                        if m == 2:
                            add_x1(g - 1, 0)
                            add_x1(g - 1, 1)
                            norm2(g - 1, 2)
                        if m == 3:
                            norm2(g - 1, 3)
                            add_x1(g - 1, 2)
                for u in range(UNITS):
                    b, m = u // C, u % C
                    if m == 0:
                        copy_v(g, b, 8 if b == 0 else 7 + 2 * b)
                    copy_pt(g, u)
                    if u + 2 < UNITS:
                        row_max(g, u + 2)
                    if m == 0 and b > 0:
                        scale_o(g, b - 1)
                    if m == 1 and b > 0:
                        low_o(g, b - 1)
                    if m == 3:
                        if not last:
                            norm_low(GB * (g + 1) + b, b, hi_ready, lo_ready, h_lo, hf, h_hi)
                        recip(g, b)
                        if b > 0:
                            residual(g, b - 1)
                    if u == 1 and not first:
                        add_x1(g - 1, 3)

            groups(dve, body)
            scale_o(NG - 1, GB - 1)
            low_o(NG - 1, GB - 1)
            residual(NG - 1, GB - 1)
            mean_var2(NG - 1)

            def mean_square(g, b, sum_sem, xn_sem, var_sem):
                dve.wait_ge(sum_sem, GB * g + b + 1)
                wait(dve, xn_sem, GB * g + b - 1)
                nc.vector.tensor_scalar(ve1[:, b % 2:b % 2 + 1], ssq[:, b % 2:b % 2 + 1], 1.0 / D, EPS_RMS, ALU.mult,
                                        ALU.add).then_inc(var_sem, 1)

            for i in range(C):
                dve.wait_ge(wvp_hi_made, i + 1)
                low_half(wvp_lo[:, i], bank[2 + i][:], wvp_hi[:, i]).then_inc(wvp_lo_made, 1)
                mean_square(0, i, bssq, bxn, bvar)
                if i == 1:
                    norm2(NG - 1, 0)
                    norm2(NG - 1, 1)

            def low_g(i):
                dve.wait_ge(g_hi_made, i + 1)
                low_half(g_lo_b[:, i], bank[2 + i][:], g_hi_b[:, i]).then_inc(g_lo_made, 1)

            low_g(0)
            then(nc.vector.tensor_tensor(bqk[:], cols[:, COL["bq1"]:COL["bq1"] + C], cols[:, COL["bk1"]:COL["bk1"] + C],
                                         ALU.mult))
            then(nc.vector.tensor_reduce(bqk_sum[:, 0:1], bqk[:], AX.X, ALU.add))
            nc.vector.tensor_scalar(bqk_sum[:, 1:2], bqk_sum[:, 0:1], float(HD), None, ALU.mult)
            dve.wait_ge(film1_t, 1)
            fl = ps_r[:].rearrange("p (c v b) -> p c v b", c=C, v=4)
            for i, (st, n) in enumerate(((st_f1, "1"), (st_f2, "2"))):
                then(nc.vector.tensor_tensor(tmp_a[:], fl[:, :, 2 * i, :], col_wide(f"f{n}scale"), ALU.add))
                then(nc.vector.tensor_scalar(tmp_a[:], tmp_a[:], 1.0, None, ALU.add))
                nc.vector.tensor_tensor(table(st, 0), tmp_a[:], col_wide(f"norm{n}"), ALU.mult)
                then(nc.vector.tensor_tensor(table(st, C), fl[:, :, 2 * i + 1, :], col_wide(f"f{n}shift"), ALU.add))
            nc.vector.memset(tmp_b[:, 0, 0:1], 0.0).then_inc(st1_made, 1)
            dve.wait_ge(uc_t, 1)
            shares = ps_o[:].rearrange("p (c v h q) -> p c v h q", c=C, v=2, h=2)
            then(nc.vector.tensor_copy(uc_part[:].rearrange("p v c -> p c v"), shares[:, :, :, 0, 0]))
            nc.vector.tensor_tensor(uc[:].rearrange("p v c -> p c v"), shares[:, :, :, 1, 0],
                                    uc_part[:].rearrange("p v c -> p c v"), ALU.add).then_inc(uc_made, 1)
            dve.wait_ge(uc_made, 1)
            for b in range(2):
                add_x1(NG - 1, b)
            for b in range(2, GB):
                norm2(NG - 1, b)

            low_g(1)

            def norm_low_b(g, b):
                tok = slice(b * P, (b + 1) * P)
                dve.wait_ge(bhi, GB * g + b + 1)
                low_half(hb_lo[:, :, tok], hb_new[:, :, tok], hb_hi[:, :, tok]).then_inc(blo, 1)

            for b in range(0, GB, 2):
                low_g(2 + b // 2)
                scale_odd(b + 1, b // 2, bg_full, bg_free, bcur, hb_new[:, :, (b + 1) * P:(b + 2) * P])
                norm_low_b(0, b)
                norm_low_b(0, b + 1)
            dve.wait_ge(rows_in, 64)
            dve.wait_ge(bvp_done, 1)
            nc.vector.tensor_tensor(cb1[:], ps_o[:], cb1[:], ALU.add).then_inc(cb_made, 1)
            for b in range(2, GB):
                add_x1(NG - 1, b)

            def residual_b(g, b):
                t = GB * g + b
                dve.wait_ge(bpv, t + 1)
                dve.wait_ge(bxr, t + 1)
                nc.vector.scalar_tensor_tensor(xrb[:, b], bank[6 + b % 2][:], ssq_rec[:, b % 2:b % 2 + 1], xrb[:, b],
                                               ALU.mult, ALU.add).then_inc(x2_ready, 1)

            def low_v(g, b):
                dve.wait_ge(bv_hi, GB * g + b + 1)
                low_half(vb_lo[:, b % (GB - 1), :], ps_g[0][:], vb_hi[:, b, :]).then_inc(bg_free[0], 1)

            def copy_ptb(g, b):
                t = GB * g + b
                dve.wait_ge(btp, t + 1)
                wait(dve, bpv, t - 1)
                nc.vector.tensor_copy(ptb_hi[:, b % 2, :], ps_t[b % 2][:, 0:P]).then_inc(bpt, 1)
                dve.wait_ge(bpt, 2 * t + 1)
                low_half(ptb_lo[:, b % 2, :], ps_t[b % 2][:, 0:P], ptb_hi[:, b % 2, :]).then_inc(bpt, 1)
                wait(dve, x2_ready, t - 1)
                nc.vector.reciprocal(ssq_rec[:, b % 2:b % 2 + 1], sums[:, b % 2, 0:1]).then_inc(brec, 1)

            def split_w1(i):
                k, n = w1_piece(i)
                dve.wait_ge(w1_hi_made, i + 1)
                low_half(w1_lo[:, k, n], stage_w1[:, k % 2, n], w1_hi[:, k, n]).then_inc(w1_lo_made, 1)

            def body_b(g, first, last):
                for m in range(C):
                    dve.wait_ge(bg_full[m % 2], bank_uses_b(g, m) + 1)
                    nc.vector.tensor_scalar(tb[:, m, :], ps_g[m % 2][:], uc[:, 1, m:m + 1], None, ALU.add)\
                        .then_inc(bg_free[m % 2], 1)
                    if m == 0 and not first:
                        copy_ptb(g - 1, GB - 1)
                    if m == 1 and not first:
                        dve.wait_ge(brec, GB * g)
                        residual_b(g - 1, GB - 1)
                    mean_square(g + 1, m, bssq, bxn, bvar)
                low_v(g, 0)
                for b in range(GB):
                    t = GB * g + b
                    if b == GB - 1:
                        norm_low_b(g + 1, b)
                    dve.wait_ge(bs_done, t + 1)
                    nc.vector.tensor_reduce(neg_max[:, b % 2, 0:1], ps_s[b % 2][:, 0:P], AX.X, ALU.max, negate=True)\
                        .then_inc(braw, 1)
                    dve.wait_ge(braw, t + 1)
                    nc.vector.tensor_scalar(neg_max[:, b % 2, 1:2], neg_max[:, b % 2, 0:1], INV_SQRT_D, None, ALU.mult)\
                        .then_inc(bmax, 1)
                    if b < GB - 1:
                        norm_low_b(g + 1, b)
                        low_v(g, b + 1)
                        copy_ptb(g, b)
                    if b > 0:
                        dve.wait_ge(brec, t)
                        residual_b(g, b - 1)
                    if first or last:
                        for i in ([0], [1], [], [2, 3])[b]:
                            split_w1(i if first else GB + i)

            groups(dve, body_b)

            def norm_c(g, b):
                t = GB * g + b
                tok = slice(b * P, (b + 1) * P)
                if b % 2 == 0:
                    dve.wait_ge(ccur, g + 1)
                    dve.wait_ge(ct_full, t + 1)
                    wait(dve, clo, t - 1)
                    for c in range(C):
                        last = nc.vector.tensor_scalar(hfc_dve[:, c, :], bank[6][:, c * P:(c + 1) * P],
                                                       cur_st[:, b, c:c + 1], cur_st[:, b, C + c:C + c + 1], ALU.mult,
                                                       ALU.add)
                    last.then_inc(ct_free_dve, 1)
                    dve.wait_ge(ct_free_dve, 2 * g + b // 2 + 1)
                    nc.vector.tensor_copy(hc_hi[:, :, tok], hfc_dve[:]).then_inc(chi_dve, 1)
                    dve.wait_ge(chi_dve, 2 * g + b // 2 + 1)
                    low_half(hc_lo[:, :, tok], hfc_dve[:], hc_hi[:, :, tok]).then_inc(clo, 1)
                else:
                    dve.wait_ge(chi_act, 2 * g + b // 2 + 1)
                    low_half(hc_lo[:, :, tok], hfc_act[:], hc_hi[:, :, tok]).then_inc(clo, 1)

            def body_c(g, first, last):
                for f in range(FT):
                    n = FT * g + f
                    if first and f == 0:
                        copy_ptb(NG - 1, GB - 1)
                    if first and f == 1:
                        dve.wait_ge(brec, NB)
                        residual_b(NG - 1, GB - 1)
                    if first and w2_pair(f) is not None:
                        i = w2_pair(f)
                        dve.wait_ge(w2_hi_made, i + 1)
                        low_half(w2_lo[:, 2 * i:2 * i + 2, :], stage_w2[i % 2][:], w2_hi[:, 2 * i:2 * i + 2, :])\
                            .then_inc(w2_lo_made, 1)
                    r = f % (LAG + 1)
                    dve.wait_ge(gelu_done, n + 1)
                    if f >= LAG + 1:
                        dve.wait_ge(down_done, (FT - 1) * g + f - LAG)
                    elif f < LAG:
                        wait(dve, down_done, (FT - 1) * (g - 1) + FT - LAG + f)
                    else:
                        wait(dve, acc_done, GB * g)
                    nc.vector.tensor_copy(g_hi[:, r, :], gf[f % 2][:]).then_inc(g_hi_ready, 1)
                    dve.wait_ge(g_hi_ready, n + 1)
                    low_half(g_lo[:, r, :], gf[f % 2][:], g_hi[:, r, :]).then_inc(g_lo_ready, 1)
                    if not last and f % 2 == 0 and 4 <= f < 4 + 2 * GB:
                        mean_square(g, (f - 4) // 2, cssq, cxn, cvar)
                if not last:
                    for b in range(GB):
                        norm_c(g, b)
                for b in range(GB):
                    t = GB * g + b
                    dve.wait_ge(acc_done, t + 1)
                    dve.wait_ge(cxr, t + 1)
                    nc.vector.tensor_tensor(xrc[:, b], bank[2 + b][:], xrc[:, b], ALU.add).then_inc(y_ready, 1)

            groups(dve, body_c)

        @block.gpsimd
        def _(pool):
            nc.gpsimd.memset(ident[:], 0.0).then_inc(consts_made, 1)
            nc.gpsimd.memset(neg_half[:], -0.5).then_inc(consts_made, 1)
            nc.gpsimd.memset(inv_hd[:], 1.0 / HD)
            pool.wait_ge(consts_made, 2)
            nc.gpsimd.affine_select(out=ident[:], in_=ident[:], compare_op=ALU.not_equal, fill=1.0, base=0,
                                    pattern=[[-1, P]], channel_multiplier=1).then_inc(consts_made, 1)

            def scales(g, table, cur, used, row=None):
                wait(pool, used, GB * g)
                nc.gpsimd.tensor_copy(cur_st[:], table[:, bass.ds(GB * g if row is None else row, GB), :])\
                    .then_inc(cur, 1)

            def norm_a(g, b):
                t = GB * g + b
                i = b % 2
                pool.wait_ge(var_ready, 2 * t + 2)
                nc.gpsimd.tensor_tensor(rstd1[:, i:i + 1], ve1[:, i:i + 1], neg_half[:, 0:1], ALU.pow)\
                    .then_inc(rstd_ready, 1)
                wait_apart(pool, rstd_ready, t + 1, passed)
                nc.gpsimd.tensor_scalar(xa[:, b], xa[:, b], mv1[:, i, 0:1], rstd1[:, i:i + 1], ALU.subtract,
                                        ALU.mult).then_inc(xn_ready, 1)

            norm_a(0, 0)
            norm_a(0, 1)
            norm_a(0, 2)
            pool.wait_ge(st0_made, 1)
            scales(0, st_ln, cur_ready, hi_ready)
            norm_a(0, 3)
            nc.gpsimd.memset(k_diag[:], 0.0).then_inc(consts_made, 1)
            pool.wait_ge(rows_in, 64)

            def add_bias(t, i, x, row, x_sem, count, ready):
                pool.wait_ge(x_sem, count)
                nc.gpsimd.tensor_tensor(x[:, i], x[:, i], row[:], ALU.add).then_inc(ready, 1)

            def finish(g, all_four=True):
                wait(pool, x1_ready, GB * g)
                pool.wait_ge(var2_ready, g + 1)
                nc.gpsimd.tensor_tensor(rstd2[:], ve2[:], neg_half[:], ALU.pow).then_inc(rstd2_ready, 1)
                shift(g, range(GB) if all_four else range(2))

            def shift(g, bs):
                for b in bs:
                    pool.wait_ge(ln2_normed, GB * g + b + 1)
                    nc.gpsimd.tensor_tensor(h1[:, b], h1[:, b], rows[:, b % 2, D:2 * D], ALU.add)\
                        .then_inc(ln2_shifted, 1)

            def body(g, first, last):
                if not last:
                    scales(g + 1, st_ln, cur_ready, hi_ready)
                    norm_a(g + 1, 0)
                    norm_a(g + 1, 1)
                if not first:
                    finish(g - 1)
                for b in range(GB):
                    if b >= 2 and not last:
                        norm_a(g + 1, b)
                    add_bias(GB * g + b, b % 2, xra, bp0, xr_in[b % 2], loaded(2 * g + b // 2 + 1), xr_ready)

            groups(pool, body)

            def norm_rms(g, b, x, xn, slot, var, ready, freed, freed_at, rr):
                t = GB * g + b
                i = b % 2
                pool.wait_ge(var, t + 1)
                nc.gpsimd.tensor_tensor(rstd1[:, i:i + 1], ve1[:, i:i + 1], neg_half[:, 0:1], ALU.pow).then_inc(rr, 1)
                wait(pool, freed, freed_at)
                wait_apart(pool, rr, t + 1, passed)
                nc.gpsimd.tensor_scalar(xn[:, slot], x[:, i], rstd1[:, i:i + 1], None, ALU.mult).then_inc(ready, 1)

            def norm_b(g, b):
                norm_rms(g, b, xb, xnb, b, bvar, bxn, bhi, GB * (g - 1) + b + 1, brstd)

            for b in range(GB):
                norm_b(0, b)
            finish(NG - 1, all_four=False)
            pool.wait_ge(st1_made, 1)
            scales(0, st_f1, bcur, bhi)
            shift(NG - 1, range(2, GB))
            pool.wait_ge(cb_made, 1)

            def body_b(g, first, last):
                if last:
                    scales(NG, st_f2, bcur, bhi, 0)
                else:
                    scales(g + 1, st_f1, bcur, bhi)
                norm_b(g + 1, 0)
                norm_b(g + 1, 1)
                add_bias(GB * g, 0, xrb, cb1, bxr_in[0], loaded(g + 1), bxr)
                norm_b(g + 1, 2)
                add_bias(GB * g + 1, 1, xrb, cb1, bxr_in[1], loaded(g + 1), bxr)
                norm_b(g + 1, 3)
                for b in range(2, GB):
                    add_bias(GB * g + b, b, xrb, cb1, bxr_in[b], loaded(g + 1), bxr)

            groups(pool, body_b)

            def norm_c(g, b):
                norm_rms(g, b, xc, xnc, b, cvar, cxn, clo, GB * g, crstd)

            pool.wait_ge(blo, NB + GB)

            def body_c(g, first, last):
                for b in range(GB):
                    add_bias(GB * g + b, b, xrc, b2, cxr_in[b], loaded(g + 1), cxr)
                if not last:
                    scales(g, st_f2, ccur, clo, GB * g + GB)
                    for b in range(GB):
                        norm_c(g, b)

            groups(pool, body_c)


def kernel(**inputs):
    import numpy as np
    import concourse.bacc as bacc
    from concourse.bass_utils import run_bass_kernel_spmd as run

    a = {k: np.asarray(v) for k, v in inputs.items()}
    l0, l1 = "L0_cond_", "L1_cond_"

    def chunks(v):
        return v.reshape(-1, P).T

    qkv_b = a[l0 + "bqkv"].reshape(D, 3)
    f1b, f2b = a[l1 + "film1_b"], a[l1 + "film2_b"]
    vectors = {
        "ln_g": a[l0 + "ln_g"], "ln_b": a[l0 + "ln_b"], "bg": a[l0 + "bg"], "bb": a[l0 + "bb"],
        "bq0": qkv_b[:, 0], "bk0": qkv_b[:, 1], "norm1": a[l1 + "norm1_w"], "f1scale": f1b[:D], "f1shift": f1b[D:],
        "bq1": a[l1 + "q_b"], "bk1": a[l1 + "k_b"], "bv1": a[l1 + "v_b"], "norm2": a[l1 + "norm2_w"],
        "f2scale": f2b[:D], "f2shift": f2b[D:],
    }
    arrays = {
        "xt": a["x"].reshape(NB * P, D),
        "cond_t": a["cond_1024"].T,
        "cols_d": np.concatenate([chunks(vectors[n]) for n in COLS] + [chunks(a[l1 + "mlp_b1"])], axis=1),
        "bp0_d": a[l0 + "bp"],
        "bv0_d": qkv_b[:, 2],
        "pb1_d": a[l1 + "proj_b"],
        "b2_d": a[l1 + "mlp_b2"],
        "wg_t": a[l0 + "Wg"].T,
        "wb_t": a[l0 + "Wb"].T,
        "wqkv": a[l0 + "Wqkv"].reshape(D, 3, D).transpose(2, 1, 0).reshape(D, 3 * D),
        "wp0": a[l0 + "Wp"].T,
        "film1": a[l1 + "film1_w"],
        "film2": a[l1 + "film2_w"],
        "wq1_t": a[l1 + "q_w"].T,
        "wk1_t": a[l1 + "k_w"].T,
        "wv1_t": a[l1 + "v_w"].T,
        "wp1": a[l1 + "proj_w"],
        "w1": a[l1 + "mlp_w1"],
        "w2": a[l1 + "mlp_w2"],
    }
    nc = bacc.Bacc("TRN2", target_bir_lowering=False, num_devices=1)
    sent, args = {}, {}
    for name, v in arrays.items():
        sent[name + "_in"] = v = np.ascontiguousarray(v)
        args[name] = nc.dram_tensor(name + "_in", v.shape, mybir.dt.from_np(v.dtype), kind="ExternalInput").ap()
    out = nc.dram_tensor("out", (NB * P, D), F32, kind="ExternalOutput").ap()
    block_pair_kernel(nc, **args, out=out)
    r = run(nc, [sent], core_ids=[0])
    return r.results[0]["out"].reshape(NB, P, D)
```
